# Optimizing a Trainium2 kernel written in Bass

```python
import numpy as np
import jax
import jax.numpy as jnp

def _softmax(x, axis=-1):
    return jax.nn.softmax(x, axis=axis)

def _gelu(x):
    return jax.nn.gelu(x, approximate=True)

def _silu(x):
    return jax.nn.silu(x)

def _sigmoid(x):
    return jax.nn.sigmoid(x)

def _layernorm(x, axis=-1, eps=1e-05):
    m = jnp.mean(x, axis=axis, keepdims=True)
    v = jnp.var(x, axis=axis, keepdims=True)
    return (x - m) / jnp.sqrt(v + eps)

def _scatter_add(tgt, idx, src, axis=0):
    return tgt.at[idx].add(src)

def _segment_sum(src, seg, n):
    return jax.ops.segment_sum(src, seg, n)
kernel_name = 'mk_vit_tower_d4_tok_img768_r4_83d4d1'

def setup_inputs(seed: int=0):
    np.random.seed(seed)
    _w = jnp.asarray

    def _rec_inputs():
        import jax
        import jax.numpy as jnp
        _rk = jax.random.key(seed)
        x = -4.65018e-05 + 0.999886 * jax.random.normal(jax.random.fold_in(_rk, 1), (64, 3, 96, 96), jnp.float32)
        return x
    x = _rec_inputs()

    def _L0_tok_setup():
        import jax, jax.numpy as jnp
        import numpy as np
        P1 = P2 = 16
        C = 3
        E = 192
        key = jax.random.key(seed)
        ks = jax.random.split(key, 7)
        x = jax.random.normal(ks[0], (64, C, 128, 128), dtype=jnp.float32)
        W1 = jax.random.normal(ks[1], (1, P1), dtype=jnp.float32) / np.sqrt(P1)
        b1 = jax.random.normal(ks[2], (1,), dtype=jnp.float32) * 0.01
        W2 = jax.random.normal(ks[3], (1, P2), dtype=jnp.float32) / np.sqrt(P2)
        b2 = jax.random.normal(ks[4], (1,), dtype=jnp.float32) * 0.01
        W3 = jax.random.normal(ks[5], (E, C), dtype=jnp.float32) / np.sqrt(C)
        b3 = jax.random.normal(ks[6], (E,), dtype=jnp.float32) * 0.01
        return {'x': x, 'W1': W1, 'b1': b1, 'W2': W2, 'b2': b2, 'W3': W3, 'b3': b3}
    _L0_tok_all = _L0_tok_setup()
    _L0_tok_in = {k: v for k, v in _L0_tok_all.items() if k in ('W1', 'b1', 'W2', 'b2', 'W3', 'b3')}
    del _L0_tok_all

    def _L0_attn_setup():
        import jax, jax.numpy as jnp
        import numpy as np
        B, T, C = (16, 512, 192)

        def _wkv(k, v, w, u):
            Bb, Tt, Cc = k.shape

            def step(carry, kv):
                num, den, mx = carry
                kt, vt = kv
                m_out = jnp.maximum(mx, kt + u)
                e1 = jnp.exp(mx - m_out)
                e2 = jnp.exp(kt + u - m_out)
                out = (e1 * num + e2 * vt) / (e1 * den + e2)
                m_new = jnp.maximum(mx + w, kt)
                e1s = jnp.exp(mx + w - m_new)
                e2s = jnp.exp(kt - m_new)
                return ((e1s * num + e2s * vt, e1s * den + e2s, m_new), out)
            init = (jnp.zeros((Bb, Cc), k.dtype), jnp.zeros((Bb, Cc), k.dtype), jnp.full((Bb, Cc), -1e+38, k.dtype))
            _, outs = jax.lax.scan(step, init, (jnp.swapaxes(k, 0, 1), jnp.swapaxes(v, 0, 1)))
            return jnp.swapaxes(outs, 0, 1)
        key = jax.random.key(seed)
        ks = jax.random.split(key, 10)
        s = 0.02
        return {'x': jax.random.normal(ks[0], (B, T, C), dtype=jnp.float32), 'time_decay': jax.random.normal(ks[1], (C,), dtype=jnp.float32) * 0.5, 'time_first': jax.random.normal(ks[2], (C,), dtype=jnp.float32) * 0.5, 'mix_k': jax.random.uniform(ks[3], (C,), dtype=jnp.float32), 'mix_v': jax.random.uniform(ks[4], (C,), dtype=jnp.float32), 'mix_r': jax.random.uniform(ks[5], (C,), dtype=jnp.float32), 'Wk': jax.random.normal(ks[6], (C, C), dtype=jnp.float32) * s, 'Wv': jax.random.normal(ks[7], (C, C), dtype=jnp.float32) * s, 'Wr': jax.random.normal(ks[8], (C, C), dtype=jnp.float32) * s, 'Wo': jax.random.normal(ks[9], (C, C), dtype=jnp.float32) * s}
    _L0_attn_all = _L0_attn_setup()
    _L0_attn_in = {k: v for k, v in _L0_attn_all.items() if k in ('time_decay', 'time_first', 'mix_k', 'mix_v', 'mix_r', 'Wk', 'Wv', 'Wr', 'Wo')}
    del _L0_attn_all

    def _L0_ffn_setup():
        import jax, jax.numpy as jnp
        import numpy as np
        E = 192
        H = 12
        D = E // H
        HID = 768
        NEXP = 4
        TOPK = 2
        EPS = 1e-05

        def _ln(x, g, b):
            m = jnp.mean(x, axis=-1, keepdims=True)
            v = jnp.mean(jnp.square(x - m), axis=-1, keepdims=True)
            return (x - m) * jax.lax.rsqrt(v + EPS) * g + b
        key = jax.random.key(seed)
        ks = jax.random.split(key, 10)
        s = 0.02
        return {'x': jax.random.normal(ks[0], (8, 256, E), jnp.float32), 'ln1_g': jnp.ones((E,), jnp.float32), 'ln1_b': jnp.zeros((E,), jnp.float32), 'in_w': jax.random.normal(ks[1], (3 * E, E), jnp.float32) * s, 'in_b': jnp.zeros((3 * E,), jnp.float32), 'out_w': jax.random.normal(ks[2], (E, E), jnp.float32) * s, 'out_b': jnp.zeros((E,), jnp.float32), 'mlp_w1': jax.random.normal(ks[3], (E, HID), jnp.float32) * s, 'mlp_b1': jnp.zeros((HID,), jnp.float32), 'mlp_w2': jax.random.normal(ks[4], (HID, E), jnp.float32) * s, 'mlp_b2': jnp.zeros((E,), jnp.float32), 'ln2_g': jnp.ones((E,), jnp.float32), 'ln2_b': jnp.zeros((E,), jnp.float32), 'gate_w': jax.random.normal(ks[5], (NEXP, E), jnp.float32) * s, 'gate_b': jnp.zeros((NEXP,), jnp.float32), 'exp_w1': jax.random.normal(ks[6], (NEXP, E, HID), jnp.float32) * s, 'exp_b1': jnp.zeros((NEXP, HID), jnp.float32), 'exp_w2': jax.random.normal(ks[7], (NEXP, HID, E), jnp.float32) * s, 'exp_b2': jnp.zeros((NEXP, E), jnp.float32)}
    _L0_ffn_all = _L0_ffn_setup()
    _L0_ffn_in = {k: v for k, v in _L0_ffn_all.items() if k in ('ln1_g', 'ln1_b', 'in_w', 'in_b', 'out_w', 'out_b', 'mlp_w1', 'mlp_b1', 'mlp_w2', 'mlp_b2', 'ln2_g', 'ln2_b', 'gate_w', 'gate_b', 'exp_w1', 'exp_b1', 'exp_w2', 'exp_b2')}
    del _L0_ffn_all

    def _L1_attn_setup():
        import jax, jax.numpy as jnp
        import numpy as np
        N_EMBED = 192
        N_HEAD = 12
        key = jax.random.key(seed)
        k1, k2, k3, k4, k5 = jax.random.split(key, 5)
        B, S, D = (4, 512, N_EMBED)
        scale = 0.02
        return {'x': jax.random.normal(k1, (B, S, D), dtype=jnp.float32), 'W_attn': jax.random.normal(k2, (D, 3 * D), dtype=jnp.float32) * scale, 'b_attn': jnp.zeros((3 * D,), dtype=jnp.float32), 'W_proj': jax.random.normal(k3, (D, D), dtype=jnp.float32) * scale, 'b_proj': jnp.zeros((D,), dtype=jnp.float32)}
    _L1_attn_all = _L1_attn_setup()
    _L1_attn_in = {k: v for k, v in _L1_attn_all.items() if k in ('W_attn', 'b_attn', 'W_proj', 'b_proj')}
    del _L1_attn_all

    def _L1_ffn_setup():
        import jax, jax.numpy as jnp
        import numpy as np
        B, S, D, F, E = (2, 256, 192, 768, 8)
        key = jax.random.key(seed)
        k0, k1, k2, k3, k4, k5 = jax.random.split(key, 6)
        scale = 0.02
        return {'hidden_states': jax.random.normal(k0, (B, S, D), dtype=jnp.float32), 'Wg': jax.random.normal(k1, (D, E), dtype=jnp.float32) * scale, 'W1': jax.random.normal(k2, (E, D, F), dtype=jnp.float32) * scale, 'b1': jnp.zeros((E, F), dtype=jnp.float32), 'W2': jax.random.normal(k3, (E, F, D), dtype=jnp.float32) * scale, 'b2': jnp.zeros((E, D), dtype=jnp.float32)}
    _L1_ffn_all = _L1_ffn_setup()
    _L1_ffn_in = {k: v for k, v in _L1_ffn_all.items() if k in ('Wg', 'W1', 'b1', 'W2', 'b2')}
    del _L1_ffn_all

    def _L2_attn_setup():
        import math
        import jax, jax.numpy as jnp
        import numpy as np
        D_MODEL = 192
        N_HEAD = 12
        HEAD_DIM = D_MODEL // N_HEAD
        ROPE_BASE = 10000.0
        EPS = 1e-06

        def rotary_cache(seq_len, head_dim, base=ROPE_BASE):
            half = head_dim // 2
            freq = 1.0 / base ** (jnp.arange(half, dtype=jnp.float32) / half)
            freqs = jnp.arange(seq_len, dtype=jnp.float32)[:, None] * freq[None, :]
            return (jnp.cos(freqs), jnp.sin(freqs))

        def apply_rope(x, cos, sin):
            cos = cos.astype(x.dtype)
            sin = sin.astype(x.dtype)
            x1 = x[..., ::2]
            x2 = x[..., 1::2]
            out = jnp.stack((x1 * cos - x2 * sin, x1 * sin + x2 * cos), axis=-1)
            return out.reshape(x.shape)
        key = jax.random.key(seed)
        kx, kq, kk, kv, kp = jax.random.split(key, 5)
        B, S, D = (2, 512, D_MODEL)
        x = jax.random.normal(kx, (B, S, D), dtype=jnp.float32)
        scale = 0.02
        Wq = jax.random.normal(kq, (D, D), dtype=jnp.float32) * scale
        Wk = jax.random.normal(kk, (D, D), dtype=jnp.float32) * scale
        Wv = jax.random.normal(kv, (D, D), dtype=jnp.float32) * scale
        Wproj = jax.random.normal(kp, (D, D), dtype=jnp.float32) * scale
        return {'x': x, 'Wq': Wq, 'Wk': Wk, 'Wv': Wv, 'Wproj': Wproj}
    _L2_attn_all = _L2_attn_setup()
    _L2_attn_in = {k: v for k, v in _L2_attn_all.items() if k in ('Wq', 'Wk', 'Wv', 'Wproj')}
    del _L2_attn_all

    def _L2_ffn_setup():
        import jax, jax.numpy as jnp
        import numpy as np
        E = 8
        TOP_K = 2
        CAP_RATIO = 1.2
        key = jax.random.key(seed)
        k1, k2, k3, k4 = jax.random.split(key, 4)
        B, L, D, H = (2, 512, 192, 512)
        x = jax.random.normal(k1, (B, L, D), dtype=jnp.float32)
        Wg = jax.random.normal(k2, (D, E), dtype=jnp.float32) * 0.02
        W1 = jax.random.normal(k3, (E, D, 2 * H), dtype=jnp.float32) * 0.02
        W2 = jax.random.normal(k4, (E, H, D), dtype=jnp.float32) * 0.02
        return {'x': x, 'Wg': Wg, 'W1': W1, 'W2': W2}
    _L2_ffn_all = _L2_ffn_setup()
    _L2_ffn_in = {k: v for k, v in _L2_ffn_all.items() if k in ('Wg', 'W1', 'W2')}
    del _L2_ffn_all

    def _L3_attn_setup():
        import jax, jax.numpy as jnp
        import numpy as np
        NUM_HEADS = 12
        NEG = -1000000000.0
        key = jax.random.key(seed)
        ks = jax.random.split(key, 5)
        B, S, D = (4, 512, 192)
        scale = 0.02
        return {'x': jax.random.normal(ks[0], (B, S, D), dtype=jnp.float32), 'wq': jax.random.normal(ks[1], (D, D), dtype=jnp.float32) * scale, 'wk': jax.random.normal(ks[2], (D, D), dtype=jnp.float32) * scale, 'wv': jax.random.normal(ks[3], (D, D), dtype=jnp.float32) * scale, 'wo': jax.random.normal(ks[4], (D, D), dtype=jnp.float32) * scale}
    _L3_attn_all = _L3_attn_setup()
    _L3_attn_in = {k: v for k, v in _L3_attn_all.items() if k in ('wq', 'wk', 'wv', 'wo')}
    del _L3_attn_all

    def _L3_ffn_setup():
        import jax, jax.numpy as jnp
        import numpy as np
        H = 192
        I = 96
        E = 16
        G = 4
        TOPK_GROUP = 2
        TOP_K = 4
        SCALE = 2.5
        N_SHARED = 2
        IS = I * N_SHARED
        B, S = (1, 512)

        def _route(x, router_w, router_b, corr_bias):
            logits = x.astype(jnp.float32) @ router_w.T + router_b
            scores = jax.nn.sigmoid(logits)
            sfc = scores + corr_bias[None, :]
            grp = sfc.reshape(-1, G, E // G)
            group_scores = jax.lax.top_k(grp, 2)[0].sum(-1)
            _, gidx = jax.lax.top_k(group_scores, TOPK_GROUP)
            gmask = jax.nn.one_hot(gidx, G, dtype=sfc.dtype).sum(axis=1)
            score_mask = jnp.repeat(gmask, E // G, axis=-1)
            sfc = jnp.where(score_mask > 0, sfc, 0.0)
            _, idx = jax.lax.top_k(sfc, TOP_K)
            w = jnp.take_along_axis(scores, idx, axis=1)
            w = w / (w.sum(-1, keepdims=True) + 1e-20)
            return (idx, w * SCALE)

        def _forward(x3, router_w, router_b, corr_bias, gWg, gbg, gWu, gbu, gWd, gbd, sWg, sbg, sWu, sbu, sWd, sbd):
            orig_shape = x3.shape
            x = x3.reshape(-1, H)
            idx, w = _route(x, router_w, router_b, corr_bias)
            c = (jax.nn.one_hot(idx, E, dtype=w.dtype) * w[..., None]).sum(1)
            h = jax.nn.silu(jnp.einsum('th,ehi->tei', x, gWg) + gbg) * (jnp.einsum('th,ehi->tei', x, gWu) + gbu)
            out_e = jnp.einsum('tei,eih->teh', h, gWd) + gbd
            moe_out = jnp.einsum('te,teh->th', c, out_e)
            hs = jax.nn.silu(x @ sWg + sbg) * (x @ sWu + sbu)
            shared = hs @ sWd + sbd
            return (moe_out + shared).reshape(orig_shape)
        key = jax.random.key(seed)
        ks = jax.random.split(key, 16)
        s = lambda k, shape, fan: jax.random.normal(k, shape, jnp.float32) * fan ** (-0.5)
        return {'hidden_states': jax.random.normal(ks[0], (B, S, H), jnp.float32), 'router_w': s(ks[1], (E, H), H), 'router_b': jnp.zeros((E,), jnp.float32), 'corr_bias': jnp.zeros((E,), jnp.float32), 'gWg': s(ks[2], (E, H, I), H), 'gbg': jnp.zeros((E, I), jnp.float32), 'gWu': s(ks[3], (E, H, I), H), 'gbu': jnp.zeros((E, I), jnp.float32), 'gWd': s(ks[4], (E, I, H), I), 'gbd': jnp.zeros((E, H), jnp.float32), 'sWg': s(ks[5], (H, IS), H), 'sbg': jnp.zeros((IS,), jnp.float32), 'sWu': s(ks[6], (H, IS), H), 'sbu': jnp.zeros((IS,), jnp.float32), 'sWd': s(ks[7], (IS, H), IS), 'sbd': jnp.zeros((H,), jnp.float32)}
    _L3_ffn_all = _L3_ffn_setup()
    _L3_ffn_in = {k: v for k, v in _L3_ffn_all.items() if k in ('router_w', 'router_b', 'corr_bias', 'gWg', 'gbg', 'gWu', 'gbu', 'gWd', 'gbd', 'sWg', 'sbg', 'sWu', 'sbu', 'sWd', 'sbd')}
    del _L3_ffn_all
    return {'x': x, 'L0_tok_W1': _L0_tok_in['W1'], 'L0_tok_b1': _L0_tok_in['b1'], 'L0_tok_W2': _L0_tok_in['W2'], 'L0_tok_b2': _L0_tok_in['b2'], 'L0_tok_W3': _L0_tok_in['W3'], 'L0_tok_b3': _L0_tok_in['b3'], 'L0_attn_time_decay': _L0_attn_in['time_decay'], 'L0_attn_time_first': _L0_attn_in['time_first'], 'L0_attn_mix_k': _L0_attn_in['mix_k'], 'L0_attn_mix_v': _L0_attn_in['mix_v'], 'L0_attn_mix_r': _L0_attn_in['mix_r'], 'L0_attn_Wk': _L0_attn_in['Wk'], 'L0_attn_Wv': _L0_attn_in['Wv'], 'L0_attn_Wr': _L0_attn_in['Wr'], 'L0_attn_Wo': _L0_attn_in['Wo'], 'L0_ffn_ln1_g': _L0_ffn_in['ln1_g'], 'L0_ffn_ln1_b': _L0_ffn_in['ln1_b'], 'L0_ffn_in_w': _L0_ffn_in['in_w'], 'L0_ffn_in_b': _L0_ffn_in['in_b'], 'L0_ffn_out_w': _L0_ffn_in['out_w'], 'L0_ffn_out_b': _L0_ffn_in['out_b'], 'L0_ffn_mlp_w1': _L0_ffn_in['mlp_w1'], 'L0_ffn_mlp_b1': _L0_ffn_in['mlp_b1'], 'L0_ffn_mlp_w2': _L0_ffn_in['mlp_w2'], 'L0_ffn_mlp_b2': _L0_ffn_in['mlp_b2'], 'L0_ffn_ln2_g': _L0_ffn_in['ln2_g'], 'L0_ffn_ln2_b': _L0_ffn_in['ln2_b'], 'L0_ffn_gate_w': _L0_ffn_in['gate_w'], 'L0_ffn_gate_b': _L0_ffn_in['gate_b'], 'L0_ffn_exp_w1': _L0_ffn_in['exp_w1'], 'L0_ffn_exp_b1': _L0_ffn_in['exp_b1'], 'L0_ffn_exp_w2': _L0_ffn_in['exp_w2'], 'L0_ffn_exp_b2': _L0_ffn_in['exp_b2'], 'L1_attn_W_attn': _L1_attn_in['W_attn'], 'L1_attn_b_attn': _L1_attn_in['b_attn'], 'L1_attn_W_proj': _L1_attn_in['W_proj'], 'L1_attn_b_proj': _L1_attn_in['b_proj'], 'L1_ffn_Wg': _L1_ffn_in['Wg'], 'L1_ffn_W1': _L1_ffn_in['W1'], 'L1_ffn_b1': _L1_ffn_in['b1'], 'L1_ffn_W2': _L1_ffn_in['W2'], 'L1_ffn_b2': _L1_ffn_in['b2'], 'L2_attn_Wq': _L2_attn_in['Wq'], 'L2_attn_Wk': _L2_attn_in['Wk'], 'L2_attn_Wv': _L2_attn_in['Wv'], 'L2_attn_Wproj': _L2_attn_in['Wproj'], 'L2_ffn_Wg': _L2_ffn_in['Wg'], 'L2_ffn_W1': _L2_ffn_in['W1'], 'L2_ffn_W2': _L2_ffn_in['W2'], 'L3_attn_wq': _L3_attn_in['wq'], 'L3_attn_wk': _L3_attn_in['wk'], 'L3_attn_wv': _L3_attn_in['wv'], 'L3_attn_wo': _L3_attn_in['wo'], 'L3_ffn_router_w': _L3_ffn_in['router_w'], 'L3_ffn_router_b': _L3_ffn_in['router_b'], 'L3_ffn_corr_bias': _L3_ffn_in['corr_bias'], 'L3_ffn_gWg': _L3_ffn_in['gWg'], 'L3_ffn_gbg': _L3_ffn_in['gbg'], 'L3_ffn_gWu': _L3_ffn_in['gWu'], 'L3_ffn_gbu': _L3_ffn_in['gbu'], 'L3_ffn_gWd': _L3_ffn_in['gWd'], 'L3_ffn_gbd': _L3_ffn_in['gbd'], 'L3_ffn_sWg': _L3_ffn_in['sWg'], 'L3_ffn_sbg': _L3_ffn_in['sbg'], 'L3_ffn_sWu': _L3_ffn_in['sWu'], 'L3_ffn_sbu': _L3_ffn_in['sbu'], 'L3_ffn_sWd': _L3_ffn_in['sWd'], 'L3_ffn_sbd': _L3_ffn_in['sbd']}

def reference(x, L0_tok_W1, L0_tok_b1, L0_tok_W2, L0_tok_b2, L0_tok_W3, L0_tok_b3, L0_attn_time_decay, L0_attn_time_first, L0_attn_mix_k, L0_attn_mix_v, L0_attn_mix_r, L0_attn_Wk, L0_attn_Wv, L0_attn_Wr, L0_attn_Wo, L0_ffn_ln1_g, L0_ffn_ln1_b, L0_ffn_in_w, L0_ffn_in_b, L0_ffn_out_w, L0_ffn_out_b, L0_ffn_mlp_w1, L0_ffn_mlp_b1, L0_ffn_mlp_w2, L0_ffn_mlp_b2, L0_ffn_ln2_g, L0_ffn_ln2_b, L0_ffn_gate_w, L0_ffn_gate_b, L0_ffn_exp_w1, L0_ffn_exp_b1, L0_ffn_exp_w2, L0_ffn_exp_b2, L1_attn_W_attn, L1_attn_b_attn, L1_attn_W_proj, L1_attn_b_proj, L1_ffn_Wg, L1_ffn_W1, L1_ffn_b1, L1_ffn_W2, L1_ffn_b2, L2_attn_Wq, L2_attn_Wk, L2_attn_Wv, L2_attn_Wproj, L2_ffn_Wg, L2_ffn_W1, L2_ffn_W2, L3_attn_wq, L3_attn_wk, L3_attn_wv, L3_attn_wo, L3_ffn_router_w, L3_ffn_router_b, L3_ffn_corr_bias, L3_ffn_gWg, L3_ffn_gbg, L3_ffn_gWu, L3_ffn_gbu, L3_ffn_gWd, L3_ffn_gbd, L3_ffn_sWg, L3_ffn_sbg, L3_ffn_sWu, L3_ffn_sbu, L3_ffn_sWd, L3_ffn_sbd):
    import jax
    import jax.numpy as jnp

    def _L0_tok_ref(x, W1, b1, W2, b2, W3, b3):
        import jax, jax.numpy as jnp
        import numpy as np
        P1 = P2 = 16
        C = 3
        E = 192
        B, Cc, H, W = x.shape
        Gh, Gw = (H // P1, W // P2)
        p = x.reshape(B, Cc, Gh, P1, Gw, P2).transpose(0, 2, 4, 3, 5, 1)
        p = p.reshape(B * Gh * Gw, P1, P2, Cc)
        y = jnp.einsum('npqc,ip->niqc', p, W1) + b1[None, :, None, None]
        y = jnp.einsum('niqc,jq->nijc', y, W2) + b2[None, None, :, None]
        y = jnp.einsum('nijc,ec->nije', y, W3) + b3
        return y.reshape(B, Gh * Gw, E)

    def _L0_attn_ref(x, time_decay, time_first, mix_k, mix_v, mix_r, Wk, Wv, Wr, Wo):
        import jax, jax.numpy as jnp
        import numpy as np
        B, T, C = (16, 512, 192)

        def _wkv(k, v, w, u):
            Bb, Tt, Cc = k.shape

            def step(carry, kv):
                num, den, mx = carry
                kt, vt = kv
                m_out = jnp.maximum(mx, kt + u)
                e1 = jnp.exp(mx - m_out)
                e2 = jnp.exp(kt + u - m_out)
                out = (e1 * num + e2 * vt) / (e1 * den + e2)
                m_new = jnp.maximum(mx + w, kt)
                e1s = jnp.exp(mx + w - m_new)
                e2s = jnp.exp(kt - m_new)
                return ((e1s * num + e2s * vt, e1s * den + e2s, m_new), out)
            init = (jnp.zeros((Bb, Cc), k.dtype), jnp.zeros((Bb, Cc), k.dtype), jnp.full((Bb, Cc), -1e+38, k.dtype))
            _, outs = jax.lax.scan(step, init, (jnp.swapaxes(k, 0, 1), jnp.swapaxes(v, 0, 1)))
            return jnp.swapaxes(outs, 0, 1)
        x_prev = jnp.pad(x, ((0, 0), (1, 0), (0, 0)))[:, :-1]
        k = jnp.einsum('btc,dc->btd', x * mix_k + x_prev * (1.0 - mix_k), Wk)
        v = jnp.einsum('btc,dc->btd', x * mix_v + x_prev * (1.0 - mix_v), Wv)
        r = jax.nn.sigmoid(jnp.einsum('btc,dc->btd', x * mix_r + x_prev * (1.0 - mix_r), Wr))
        w = -jnp.exp(time_decay)
        wkv = _wkv(k, v, w, time_first)
        return jnp.einsum('btc,dc->btd', r * wkv, Wo)

    def _L0_ffn_ref(x, ln1_g, ln1_b, in_w, in_b, out_w, out_b, mlp_w1, mlp_b1, mlp_w2, mlp_b2, ln2_g, ln2_b, gate_w, gate_b, exp_w1, exp_b1, exp_w2, exp_b2):
        import jax, jax.numpy as jnp
        import numpy as np
        E = 192
        H = 12
        D = E // H
        HID = 768
        NEXP = 4
        TOPK = 2
        EPS = 1e-05

        def _ln(x, g, b):
            m = jnp.mean(x, axis=-1, keepdims=True)
            v = jnp.mean(jnp.square(x - m), axis=-1, keepdims=True)
            return (x - m) * jax.lax.rsqrt(v + EPS) * g + b
        B, N, _ = x.shape
        h = _ln(x, ln1_g, ln1_b)
        qkv = h @ in_w.T + in_b
        q, k, v = jnp.split(qkv, 3, axis=-1)
        q = q.reshape(B, N, H, D)
        k = k.reshape(B, N, H, D)
        v = v.reshape(B, N, H, D)
        scores = jnp.einsum('bqhd,bkhd->bhqk', q, k) / jnp.sqrt(jnp.float32(D))
        attn = jax.nn.softmax(scores, axis=-1)
        ctx = jnp.einsum('bhqk,bkhd->bqhd', attn, v).reshape(B, N, E)
        x = x + ctx @ out_w.T + out_b
        x = x + jax.nn.gelu(x @ mlp_w1 + mlp_b1, approximate=False) @ mlp_w2 + mlp_b2
        xm = _ln(x, ln2_g, ln2_b)
        logits = xm @ gate_w.T + gate_b
        topv, topi = jax.lax.top_k(logits, TOPK)
        gates = jax.nn.softmax(topv, axis=-1)
        onehot = jax.nn.one_hot(topi, NEXP, dtype=x.dtype)
        comb = jnp.einsum('bnk,bnke->bne', gates, onehot)
        moe_out = jnp.zeros_like(x)
        for e in range(NEXP):
            he = jax.nn.gelu(xm @ exp_w1[e] + exp_b1[e], approximate=False)
            oe = he @ exp_w2[e] + exp_b2[e]
            moe_out = moe_out + comb[..., e:e + 1] * oe
        return x + moe_out

    def _L1_attn_ref(x, W_attn, b_attn, W_proj, b_proj):
        import jax, jax.numpy as jnp
        import numpy as np
        N_EMBED = 192
        N_HEAD = 12
        B, S, D = x.shape
        H = N_HEAD
        hd = D // H
        qkv = x @ W_attn + b_attn
        q, k, v = jnp.split(qkv, 3, axis=2)
        q = q.reshape(B, S, H, hd).transpose(0, 2, 1, 3)
        k = k.reshape(B, S, H, hd).transpose(0, 2, 1, 3)
        v = v.reshape(B, S, H, hd).transpose(0, 2, 1, 3)
        attn = jnp.einsum('bhqd,bhkd->bhqk', q, k) / jnp.sqrt(jnp.float32(hd))
        causal = jnp.tril(jnp.ones((S, S), dtype=bool))
        attn = jnp.where(causal[None, None], attn, jnp.float32(-jnp.inf))
        attn = jax.nn.softmax(attn, axis=-1)
        y = jnp.einsum('bhqk,bhkd->bhqd', attn, v)
        y = y.transpose(0, 2, 1, 3).reshape(B, S, D)
        return y @ W_proj + b_proj

    def _L1_ffn_ref(hidden_states, Wg, W1, b1, W2, b2):
        import jax, jax.numpy as jnp
        import numpy as np
        B, S, D, F, E = (2, 256, 192, 768, 8)
        b, s, d = hidden_states.shape
        e = W1.shape[0]
        x = hidden_states.reshape(-1, d)
        logits = x @ Wg
        probs = jax.nn.softmax(logits, axis=-1)
        gate = jnp.max(probs, axis=-1)
        expert_idx = jnp.argmax(probs, axis=-1)
        h = jax.nn.silu(jnp.einsum('td,edf->etf', x, W1) + b1[:, None, :])
        y = jnp.einsum('etf,efd->etd', h, W2) + b2[:, None, :]
        combine = jax.nn.one_hot(expert_idx, e, dtype=x.dtype) * gate[:, None]
        out = jnp.einsum('te,etd->td', combine, y)
        return out.reshape(b, s, d)

    def _L2_attn_ref(x, Wq, Wk, Wv, Wproj):
        import math
        import jax, jax.numpy as jnp
        import numpy as np
        D_MODEL = 192
        N_HEAD = 12
        HEAD_DIM = D_MODEL // N_HEAD
        ROPE_BASE = 10000.0
        EPS = 1e-06

        def rotary_cache(seq_len, head_dim, base=ROPE_BASE):
            half = head_dim // 2
            freq = 1.0 / base ** (jnp.arange(half, dtype=jnp.float32) / half)
            freqs = jnp.arange(seq_len, dtype=jnp.float32)[:, None] * freq[None, :]
            return (jnp.cos(freqs), jnp.sin(freqs))

        def apply_rope(x, cos, sin):
            cos = cos.astype(x.dtype)
            sin = sin.astype(x.dtype)
            x1 = x[..., ::2]
            x2 = x[..., 1::2]
            out = jnp.stack((x1 * cos - x2 * sin, x1 * sin + x2 * cos), axis=-1)
            return out.reshape(x.shape)
        B, S, D = x.shape
        H, hd = (N_HEAD, HEAD_DIM)

        def heads(W):
            return (x @ W.T).reshape(B, S, H, hd).transpose(0, 2, 1, 3)
        q, k, v = (heads(Wq), heads(Wk), heads(Wv))
        cos, sin = rotary_cache(S, hd)
        cos = cos[None, None]
        sin = sin[None, None]
        q = apply_rope(q, cos, sin)
        k = apply_rope(k, cos, sin)
        scores = jnp.einsum('bhsd,bhtd->bhst', q.astype(jnp.float32), k.astype(jnp.float32))
        scores = scores / math.sqrt(hd)
        weights = jax.lax.erf(scores) + 1.0
        mask = jnp.tril(jnp.ones((S, S), dtype=bool))[None, None]
        weights = jnp.where(mask, weights, 0.0)
        denom = jnp.maximum(weights.sum(axis=-1, keepdims=True), EPS)
        y = jnp.einsum('bhst,bhtd->bhsd', weights, v.astype(jnp.float32)) / denom
        y = y.astype(v.dtype)
        y = y.transpose(0, 2, 1, 3).reshape(B, S, D)
        return y @ Wproj.T

    def _L2_ffn_ref(x, Wg, W1, W2):
        import jax, jax.numpy as jnp
        import numpy as np
        E = 8
        TOP_K = 2
        CAP_RATIO = 1.2
        B, L, D = x.shape
        H = W2.shape[1]
        xf = x.reshape(-1, D)
        N = xf.shape[0]
        capacity = int(CAP_RATIO * N / E)
        logits = xf @ Wg
        scores, idx = jax.lax.top_k(logits, TOP_K)
        weights = jax.nn.softmax(scores, axis=-1)
        xpad = jnp.concatenate([xf, jnp.zeros((1, D), xf.dtype)], axis=0)
        wpad_zero = jnp.zeros((1,), weights.dtype)
        out = jnp.zeros((N, D), x.dtype)
        for k in range(TOP_K):
            ik = idx[:, k]
            onehot = ik[:, None] == jnp.arange(E)[None, :]
            pos = jnp.cumsum(onehot, axis=0) - 1
            posk = jnp.take_along_axis(pos, ik[:, None], axis=1)[:, 0]
            keep = posk < capacity
            buf = jnp.full((E, capacity), N, dtype=jnp.int32)
            buf = buf.at[ik, posk].set(jnp.arange(N, dtype=jnp.int32), mode='drop')
            xg = xpad[buf]
            h = jnp.einsum('ecd,edh->ech', xg, W1)
            act = h[..., :H] * jax.nn.silu(h[..., H:])
            ye = jnp.einsum('ech,ehd->ecd', act, W2)
            wk = jnp.where(keep, weights[:, k], 0.0)
            w_buf = jnp.concatenate([wk, wpad_zero])[buf]
            out = out.at[buf.reshape(-1)].add((w_buf[..., None] * ye).reshape(E * capacity, D), mode='drop')
        return out.reshape(B, L, D)

    def _L3_attn_ref(x, wq, wk, wv, wo):
        import jax, jax.numpy as jnp
        import numpy as np
        NUM_HEADS = 12
        NEG = -1000000000.0
        B, S, D = x.shape
        H = NUM_HEADS
        dh = D // H

        def proj(w):
            return (x @ w.T).reshape(B, S, H, dh).transpose(0, 2, 1, 3)
        q, k, v = (proj(wq), proj(wk), proj(wv))
        score = jnp.einsum('bhqd,bhkd->bhqk', q, k) / jnp.float32(np.sqrt(dh))
        causal = jnp.triu(jnp.ones((S, S), dtype=bool), k=1)
        score = score + jnp.where(causal, jnp.float32(NEG), jnp.float32(0.0))
        attn = jax.nn.softmax(score, axis=-1)
        out = jnp.einsum('bhqk,bhkd->bhqd', attn, v)
        out = out.transpose(0, 2, 1, 3).reshape(B, S, D)
        return out @ wo.T

    def _L3_ffn_ref(hidden_states, router_w, router_b, corr_bias, gWg, gbg, gWu, gbu, gWd, gbd, sWg, sbg, sWu, sbu, sWd, sbd):
        import jax, jax.numpy as jnp
        import numpy as np
        H = 192
        I = 96
        E = 16
        G = 4
        TOPK_GROUP = 2
        TOP_K = 4
        SCALE = 2.5
        N_SHARED = 2
        IS = I * N_SHARED
        B, S = (1, 512)

        def _route(x, router_w, router_b, corr_bias):
            logits = x.astype(jnp.float32) @ router_w.T + router_b
            scores = jax.nn.sigmoid(logits)
            sfc = scores + corr_bias[None, :]
            grp = sfc.reshape(-1, G, E // G)
            group_scores = jax.lax.top_k(grp, 2)[0].sum(-1)
            _, gidx = jax.lax.top_k(group_scores, TOPK_GROUP)
            gmask = jax.nn.one_hot(gidx, G, dtype=sfc.dtype).sum(axis=1)
            score_mask = jnp.repeat(gmask, E // G, axis=-1)
            sfc = jnp.where(score_mask > 0, sfc, 0.0)
            _, idx = jax.lax.top_k(sfc, TOP_K)
            w = jnp.take_along_axis(scores, idx, axis=1)
            w = w / (w.sum(-1, keepdims=True) + 1e-20)
            return (idx, w * SCALE)

        def _forward(x3, router_w, router_b, corr_bias, gWg, gbg, gWu, gbu, gWd, gbd, sWg, sbg, sWu, sbu, sWd, sbd):
            orig_shape = x3.shape
            x = x3.reshape(-1, H)
            idx, w = _route(x, router_w, router_b, corr_bias)
            c = (jax.nn.one_hot(idx, E, dtype=w.dtype) * w[..., None]).sum(1)
            h = jax.nn.silu(jnp.einsum('th,ehi->tei', x, gWg) + gbg) * (jnp.einsum('th,ehi->tei', x, gWu) + gbu)
            out_e = jnp.einsum('tei,eih->teh', h, gWd) + gbd
            moe_out = jnp.einsum('te,teh->th', c, out_e)
            hs = jax.nn.silu(x @ sWg + sbg) * (x @ sWu + sbu)
            shared = hs @ sWd + sbd
            return (moe_out + shared).reshape(orig_shape)
        return _forward(hidden_states, router_w, router_b, corr_bias, gWg, gbg, gWu, gbu, gWd, gbd, sWg, sbg, sWu, sbu, sWd, sbd)
    h = _L0_tok_ref(x, L0_tok_W1, L0_tok_b1, L0_tok_W2, L0_tok_b2, L0_tok_W3, L0_tok_b3)
    h = h + _L0_attn_ref(_layernorm(h, axis=-1), L0_attn_time_decay, L0_attn_time_first, L0_attn_mix_k, L0_attn_mix_v, L0_attn_mix_r, L0_attn_Wk, L0_attn_Wv, L0_attn_Wr, L0_attn_Wo)
    h = h + _L0_ffn_ref(_layernorm(h, axis=-1), L0_ffn_ln1_g, L0_ffn_ln1_b, L0_ffn_in_w, L0_ffn_in_b, L0_ffn_out_w, L0_ffn_out_b, L0_ffn_mlp_w1, L0_ffn_mlp_b1, L0_ffn_mlp_w2, L0_ffn_mlp_b2, L0_ffn_ln2_g, L0_ffn_ln2_b, L0_ffn_gate_w, L0_ffn_gate_b, L0_ffn_exp_w1, L0_ffn_exp_b1, L0_ffn_exp_w2, L0_ffn_exp_b2)
    h = h + _L1_attn_ref(_layernorm(h, axis=-1), L1_attn_W_attn, L1_attn_b_attn, L1_attn_W_proj, L1_attn_b_proj)
    h = h + _L1_ffn_ref(_layernorm(h, axis=-1), L1_ffn_Wg, L1_ffn_W1, L1_ffn_b1, L1_ffn_W2, L1_ffn_b2)
    h = h + _L2_attn_ref(_layernorm(h, axis=-1), L2_attn_Wq, L2_attn_Wk, L2_attn_Wv, L2_attn_Wproj)
    h = h + _L2_ffn_ref(_layernorm(h, axis=-1), L2_ffn_Wg, L2_ffn_W1, L2_ffn_W2)
    h = h + _L3_attn_ref(_layernorm(h, axis=-1), L3_attn_wq, L3_attn_wk, L3_attn_wv, L3_attn_wo)
    h = h + _L3_ffn_ref(_layernorm(h, axis=-1), L3_ffn_router_w, L3_ffn_router_b, L3_ffn_corr_bias, L3_ffn_gWg, L3_ffn_gbg, L3_ffn_gWu, L3_ffn_gbu, L3_ffn_gWd, L3_ffn_gbd, L3_ffn_sWg, L3_ffn_sbg, L3_ffn_sWu, L3_ffn_sbu, L3_ffn_sWd, L3_ffn_sbd)
    return h

_drawn_inputs = setup_inputs


def setup_inputs(seed=0):
    import zlib

    import numpy as np

    out = dict(_drawn_inputs(seed))
    spreads = {'L0_ffn_ln1_g': (1.0, 0.6),
     'L0_ffn_ln1_b': (0.0, 0.376),
     'L0_ffn_in_b': (0.0, 0.1),
     'L0_ffn_out_b': (0.0, 0.1),
     'L0_ffn_mlp_b1': (0.0, 0.1),
     'L0_ffn_mlp_b2': (0.0, 0.1),
     'L0_ffn_ln2_g': (1.0, 0.541),
     'L0_ffn_ln2_b': (0.0, 0.409),
     'L0_ffn_gate_b': (0.0, 0.1),
     'L0_ffn_exp_b1': (0.0, 0.1),
     'L0_ffn_exp_b2': (0.0, 0.1),
     'L1_attn_b_attn': (0.0, 0.1),
     'L1_attn_b_proj': (0.0, 0.1),
     'L1_ffn_b1': (0.0, 0.494),
     'L1_ffn_b2': (0.0, 0.1),
     'L3_ffn_router_b': (0.0, 0.1),
     'L3_ffn_corr_bias': (0.0, 0.1),
     'L3_ffn_gbg': (0.0, 0.274),
     'L3_ffn_gbu': (0.0, 0.274),
     'L3_ffn_gbd': (0.0, 0.1),
     'L3_ffn_sbg': (0.0, 0.383),
     'L3_ffn_sbu': (0.0, 0.406),
     'L3_ffn_sbd': (0.0, 0.1)}
    factors = {'L0_attn_time_decay': 3.83,
     'L0_attn_time_first': 2.985,
     'L0_attn_mix_k': 8.0,
     'L0_attn_mix_v': 3.105,
     'L0_attn_mix_r': 6.046,
     'L0_attn_Wk': 3.973,
     'L0_attn_Wr': 4.126,
     'L0_ffn_in_w': 2.826,
     'L1_ffn_Wg': 2.699,
     'L1_ffn_W2': 2.697,
     'L2_attn_Wq': 6.432,
     'L2_attn_Wk': 8.0,
     'L2_ffn_Wg': 3.068,
     'L2_ffn_W1': 3.05,
     'L2_ffn_W2': 2.681,
     'L3_attn_wq': 8.0,
     'L3_attn_wk': 8.0}
    for name, (base, spread) in spreads.items():
        noise = np.random.default_rng([zlib.crc32(name.encode()), seed]).standard_normal(out[name].shape)
        drawn = base * np.exp(spread * noise) if base else spread * noise
        out[name] = jnp.asarray(drawn.astype(out[name].dtype))
    for name, factor in factors.items():
        out[name] = (out[name] * factor).astype(out[name].dtype)
    return out
```

```python
from contextlib import ExitStack

import concourse.bass as bass
import concourse.mybir as mybir
import numpy as np

F32 = mybir.dt.float32
ALU = mybir.AluOpType
ACT = mybir.ActivationFunctionType
AX = mybir.AxisListType.X
ds = bass.ds

IMAGES, CHANNELS, SIDE, PATCH = 64, 3, 96, 16
GRID = SIDE // PATCH
SEQ = GRID * GRID
TOKENS = IMAGES * SEQ
D = 192
FP = 96
FC = D // FP
P = 128
TILES = TOKENS // P
HEADS, HEAD = 12, 16
PAIRS = IMAGES // 2
PAIR = 2 * SEQ
HPC = FP // HEAD
GROUP = 3
GROUPS = HEADS // GROUP
SECOND = 64
CHUNK = 384
CHUNKS = TOKENS // CHUNK
NEG = -1e30
EPS = 1e-5


LEAD = 4


class Signal:

    def __init__(self, sem, lead=LEAD):
        self.sem, self.base = sem, lead

    def at(self, n):
        return self.base + n

    def close(self, n):
        self.base += n


def link(eng, done, ins, n):
    ins.then_inc(done.sem, 1)
    eng.wait_ge(done.sem, done.at(n))


def tile(buf, t, width=D):
    return buf[:, ds(t * width, width)]


def token_phase(nc, m, s, ins):
    rows = IMAGES * GRID
    parts = rows // P
    width = CHANNELS * SIDE
    with (
        nc.sbuf_tensor("image", [P, parts, CHANNELS, PATCH * SIDE], F32) as image,
        nc.sbuf_tensor("column_sum", [P, parts, width], F32) as column_sum,
        nc.sbuf_tensor("patch_sum", [P, parts, CHANNELS * GRID], F32) as patch_sum,
        nc.sbuf_tensor("patchT", [CHANNELS, TOKENS], F32) as patchT,
        nc.sbuf_tensor("patch_tile", [CHANNELS, 2, P], F32) as patch_tile,
        nc.Block(no_gpsimd_drain=True) as block,
    ):
        x = ins["x"]

        @block.sync
        def _(sp):
            for i in range(parts):
                for c in range(CHANNELS):
                    sp.dma_start(image[:, i, c, :], x[c, i * P:(i + 1) * P, :]).then_inc(s.image[i].sem, 16)
            sp.dma_start(m.attention_w[1][:, :, 0:4 * D], ins["rwkv"]).then_inc(s.attention_w.sem, 16)
            load_attention(sp, m, s, ins, 0)
            sp.wait_ge(s.patch.sem, s.patch.at(parts))
            for c in range(CHANNELS):
                sp.dma_start(
                    m.patch_dram[c:c + 1, :].rearrange("c (i r g) -> r (c i) g", i=parts, g=GRID),
                    patch_sum[:, :, c * GRID:(c + 1) * GRID],
                ).then_inc(s.patch_store.sem, 16)
            sp.wait_ge(s.patch_store.sem, s.patch_store.at(16 * CHANNELS))
            sp.dma_start(patchT[:, :], m.patch_dram[:, :]).then_inc(s.patch_load.sem, 16)

        @block.vector
        def _(vec):
            n = 0
            for i in range(parts):
                vec.wait_ge(s.image[i].sem, s.image[i].at(16 * CHANNELS))
                acc = column_sum[:, i, :].rearrange("p (c w) -> p c w", c=CHANNELS)
                for r in range(PATCH):
                    line = image[:, i, :, r * SIDE:(r + 1) * SIDE]
                    if r == 0:
                        last = vec.tensor_scalar(acc, line, m.W1[:, 0:1], m.b1[:, 0:1], ALU.mult, ALU.add)
                    else:
                        last = vec.scalar_tensor_tensor(acc, line, m.W1[:, r:r + 1], acc, ALU.mult, ALU.add)
                    n += 1
                    link(vec, s.vec, last, n)
                each = column_sum[:, i, :].rearrange("p (g q) -> p g q", q=PATCH)
                n += 1
                link(vec, s.vec, vec.tensor_tensor(
                    each, each, m.W2[:, :].unsqueeze(1).to_broadcast([P, CHANNELS * GRID, PATCH]), ALU.mult), n)
                n += 1
                link(vec, s.vec, vec.tensor_reduce(patch_sum[:, i, :], each, AX, ALU.add), n)
                vec.tensor_scalar(patch_sum[:, i, :], patch_sum[:, i, :], m.b2[:, 0:1], None,
                                  ALU.add).then_inc(s.patch.sem, 1)
            with vec.Fori(0, TILES - 1, 2) as t:
                for p in range(2):
                    vec.wait_ge(s.mm.sem, s.mm.at(t + p + 1))
                    vec.tensor_tensor(tile(m.h, t + p), m.ps[p][:, 0:D], m.b3[:, :], ALU.add).then_inc(s.out.sem, 1)
            m.vec_links = n

        @block.scalar
        def _(act):
            act.wait_ge(s.patch_load.sem, s.patch_load.at(16))
            with act.Fori(0, TILES - 1, 2) as t:
                for p in range(2):
                    act.wait_ge(s.mm.sem, s.mm.at(t + p - 1))
                    act.activation(patch_tile[:, p, :], patchT[:, ds((t + p) * P, P)], ACT.Copy).then_inc(s.stage.sem, 1)

        @block.tensor
        def _(pe):
            with pe.Fori(0, TILES - 1, 2) as t:
                for p in range(2):
                    pe.wait_ge(s.stage.sem, s.stage.at(t + p + 1))
                    pe.wait_ge(s.out.sem, s.out.at(t + p - 1))
                    pe.matmul(m.ps[p][:, 0:D], patch_tile[:, p, :], m.W3[:, :], start=True, stop=True).then_inc(s.mm.sem, 1)
    s.vec.close(m.vec_links)
    for signal, n in ((s.mm, TILES), (s.stage, TILES), (s.out, TILES)):
        signal.close(n)


def feature_phase(nc, m, s, src, norm=True, keep=None, scale=None, shift=None, router=None):
    experts = router[2] if router else 0
    with nc.Block(no_gpsimd_drain=True) as block:

        @block.vector
        def _(vec):
            if norm:
                with vec.Fori(0, TILES) as t:
                    vec.bn_stats(tile(m.stats, t, 6), tile(src, t)).then_inc(s.stats.sem, 1)
                vec.wait_ge(s.stats.sem, s.stats.at(TILES))
                half = m.stats[:, :].rearrange("p (t k) -> p t k", k=6)
                mean, other, rstd = m.mean[:, :], m.other[:, :], m.rstd[:, :]
                link(vec, s.vec, vec.tensor_tensor(mean, half[:, :, 1], half[:, :, 4], ALU.add), 1)
                link(vec, s.vec, vec.tensor_tensor(other, half[:, :, 1], half[:, :, 4], ALU.subtract), 2)
                link(vec, s.vec, vec.tensor_scalar(mean, mean, 0.5, None, ALU.mult), 3)
                link(vec, s.vec, vec.scalar_tensor_tensor(other, other, 0.25, other, ALU.mult, ALU.mult), 4)
                link(vec, s.vec, vec.tensor_tensor(rstd, half[:, :, 2], half[:, :, 5], ALU.add), 5)
                link(vec, s.vec, vec.scalar_tensor_tensor(rstd, rstd, 1.0 / D, other, ALU.mult, ALU.add), 6)
                vec.tensor_scalar(rstd, rstd, EPS, None, ALU.add).then_inc(s.var.sem, 1)
                vec.wait_ge(s.std.sem, s.std.at(1))
                link(vec, s.vec, vec.reciprocal(rstd, rstd), 7)

            def logits(t, p):
                vec.wait_ge(s.route.sem, s.route.at(t + 1))
                out = m.logits[:, ds(t * experts, experts)]
                if router[1] is None:
                    vec.tensor_copy(out, m.ps[2 + p][:, 0:experts]).then_inc(s.logit.sem, 1)
                else:
                    vec.tensor_tensor(out, m.ps[2 + p][:, 0:experts], router[1], ALU.add).then_inc(s.logit.sem, 1)

            with vec.Fori(0, TILES - 1, 2) as t:
                for p in range(2):
                    vec.wait_ge(s.turned.sem, s.turned.at(t + p - 1))
                    x = m.x_tile[:, p, :]
                    if norm:
                        vec.tensor_scalar(x, tile(src, t + p), m.mean[:, ds(t + p, 1)], m.rstd[:, ds(t + p, 1)],
                                          ALU.subtract, ALU.mult).then_inc(s.x.sem, 1)
                    else:
                        vec.tensor_copy(x, tile(src, t + p)).then_inc(s.x.sem, 1)
                    if keep is not None:
                        vec.wait_ge(s.x.sem, s.x.at(t + p + 1))
                        vec.tensor_copy(tile(keep, t + p), x).then_inc(s.kept.sem, 1)
                if router:
                    for p in range(2):
                        logits(t + p, p)

        @block.scalar
        def _(act):
            if norm:
                act.wait_ge(s.var.sem, s.var.at(1))
                act.activation(m.rstd[:, :], m.rstd[:, :], ACT.Sqrt).then_inc(s.std.sem, 1)
            with act.Fori(0, TILES - 1, 2) as t:
                for p in range(2):
                    act.wait_ge(s.turned.sem, s.turned.at(t + p + 1))
                    if router:
                        act.wait_ge(s.route.sem, s.route.at(t + p - 1))
                    bank = m.ps[p][0:FP, 0:FC * P].rearrange("f (c k) -> f c k", c=FC)
                    for c in range(FC):
                        outs = [m.xT[:, c, ds((t + p) * P, P)]]
                        if router:
                            outs.insert(0, m.xs[:, p, c, :])
                        for out in outs:
                            if scale is None:
                                last = act.activation(out, bank[:, c, :], ACT.Copy)
                            else:
                                last = act.activation(out, bank[:, c, :], ACT.Identity,
                                                      bias=shift[:, c:c + 1], scale=scale[:, c:c + 1])
                    last.then_inc(s.xT.sem, 1)

        @block.tensor
        def _(pe):
            def route(t, p):
                pe.wait_ge(s.xT.sem, s.xT.at(t + 1))
                pe.wait_ge(s.logit.sem, s.logit.at(t - 1))
                for c in range(FC):
                    last = pe.matmul(m.ps[2 + p][:, 0:experts], m.xs[:, p, c, :], router[0][:, c, :],
                                     start=(c == 0), stop=(c == FC - 1))
                last.then_inc(s.route.sem, 1)

            with pe.Fori(0, TILES - 1, 2) as t:
                for p in range(2):
                    pe.wait_ge(s.x.sem, s.x.at(t + p + 1))
                    pe.wait_ge(s.xT.sem, s.xT.at(t + p - 1))
                    for c in range(FC):
                        last = pe.matmul(m.ps[p][0:FP, c * P:(c + 1) * P], m.x_tile[:, p, c * FP:(c + 1) * FP],
                                         m.ident[:, :], start=True, stop=True, is_transpose=True)
                    last.then_inc(s.turned.sem, 1)
                if router:
                    for p in range(2):
                        route(t + p, p)
    closing = [(s.x, TILES), (s.turned, TILES), (s.xT, TILES)]
    if norm:
        closing += [(s.vec, 7), (s.stats, TILES), (s.var, 1), (s.std, 1)]
    if keep is not None:
        closing += [(s.kept, TILES)]
    if router:
        closing += [(s.route, TILES), (s.logit, TILES)]
    for signal, n in closing:
        signal.close(n)


def project_phase(nc, m, s, weights, dst, bias=None, ready=None):
    with nc.Block(no_gpsimd_drain=True) as block:

        @block.scalar
        def _(act):
            with act.Fori(0, TILES - 1, 2) as t:
                for p in range(2):
                    act.wait_ge(s.mm.sem, s.mm.at(t + p - 1))
                    act.activation(m.xs[:, p, :, :], m.xT[:, :, ds((t + p) * P, P)], ACT.Copy).then_inc(s.stage.sem, 1)

        @block.tensor
        def _(pe):
            with pe.Fori(0, TILES - 1, 2) as t:
                for p in range(2):
                    pe.wait_ge(s.stage.sem, s.stage.at(t + p + 1))
                    pe.wait_ge(s.out.sem, s.out.at(t + p - 1))
                    if bias is not None:
                        pe.matmul(m.ps[p][:, 0:D], m.ones[0:1, 0:P], bias, start=True, stop=False)
                    for c in range(FC):
                        last = pe.matmul(m.ps[p][:, 0:D], m.xs[:, p, c, :], weights[:, c, :],
                                         start=(c == 0 and bias is None), stop=(c == FC - 1))
                    last.then_inc(s.mm.sem, 1)

        @block.vector
        def _(vec):
            with vec.Fori(0, TILES - 1, 2) as t:
                for p in range(2):
                    vec.wait_ge(s.mm.sem, s.mm.at(t + p + 1))
                    vec.tensor_tensor(tile(dst, t + p), m.ps[p][:, 0:D], tile(dst, t + p),
                                      ALU.add).then_inc(s.out.sem, 1)
    for signal, n in ((s.mm, TILES), (s.stage, TILES), (s.out, TILES)):
        signal.close(n)


def store_phase(nc, s, src, out):
    with nc.Block(no_gpsimd_drain=True) as block:

        @block.sync
        def _(sp):
            sp.dma_start(out.rearrange("(t p) d -> p t d", p=P),
                         src[:, :].rearrange("p (t d) -> p t d", d=D)).then_inc(s.store.sem, 16)
            sp.wait_ge(s.store.sem, 16)


def add_phase(nc, m, s, dst, src):
    with nc.Block(no_gpsimd_drain=True) as block:

        @block.vector
        def _(vec):
            vec.tensor_tensor(dst[:, :], dst[:, :], src[:, :], ALU.add).then_inc(s.out.sem, 1)
            vec.wait_ge(s.out.sem, s.out.at(1))
    s.out.close(1)


def load_attention(sp, m, s, ins, layer):
    n = ins[f"attention{layer}"].shape[2]
    sp.dma_start(m.attention_w[layer % 2][:, :, 0:n], ins[f"attention{layer}"]).then_inc(s.attention_w.sem, 16)


def attention_phase(nc, m, s, layer, kind, bias=None, prefetch=None):
    w = m.attention_w[layer % 2]
    Wq, Wk, Wv = (w[:, :, j * D:(j + 1) * D] for j in range(3))
    Wq_turned, Wk_turned = (w[:, :, j * D:(j + 1) * D] for j in (4, 5))
    rotary = kind == "erf"
    qbias, kbias, vbias = bias or (m.zero_bias,) * 3
    psQ, psK, psV, psS, psT, psC, psX, psR = m.ps
    spread = [FP, HPC, PAIR]
    read = s.shifted if kind == "plain" else s.scored
    lanes = HPC * SEQ

    def both(bank):
        return bank[0:FP, 0:FC * PAIR].rearrange("f (c k) -> f c k", c=FC)

    with (
        nc.sbuf_tensor(f"x_pair_{layer}", [FP, 2, FC, PAIR], F32) as x_pair,
        nc.sbuf_tensor(f"x_tripled_{layer}", [FP, 2, FC, 2, GROUP * SEQ], F32) as x_tripled,
        nc.sbuf_tensor(f"qT_{layer}", [FP, 2, FC, SECOND + SEQ], F32) as qT,
        nc.sbuf_tensor(f"k_rot_{layer}", [FP, 2, FC, PAIR], F32) as k_rot,
        nc.sbuf_tensor(f"rot_tmp_{layer}", [FP, 4, FC, PAIR], F32) as rot_tmp,
        nc.sbuf_tensor(f"k_spread_{layer}", [FP, 2, FC, HPC, PAIR], F32) as k_spread,
        nc.sbuf_tensor(f"v_spread_{layer}", [GROUP * SEQ, 2, 2, D], F32) as v_spread,
        nc.sbuf_tensor(f"weight_{layer}", [P, 2, HEADS * SEQ], F32) as weight,
        nc.sbuf_tensor(f"erf_tmp_{layer}", [P, 2, HEADS * SEQ], F32) as erf_tmp,
        nc.sbuf_tensor(f"weightT_{layer}", [GROUP * SEQ, 2, GROUPS, P], F32) as weightT,
        nc.sbuf_tensor(f"row_max_{layer}", [P, 2, HEADS], F32) as row_max,
        nc.sbuf_tensor(f"row_sum_{layer}", [P, 2, HEADS], F32) as row_sum,
        nc.sbuf_tensor(f"context_{layer}", [P, 2, D], F32) as context,
        nc.Block(no_gpsimd_drain=True) as block,
    ):
        FIRST, LAST = 4, 30

        def turns(eng, turn):
            for i in range(FIRST):
                turn(i, i % 2)
            with eng.Fori(FIRST, LAST - 1, 2) as i:
                for p in range(2):
                    turn(i + p, p)
            for i in range(LAST, PAIRS + 3):
                turn(i, i % 2)

        def has(i):
            return not isinstance(i, int) or 0 <= i < PAIRS

        @block.tensor
        def _(pe):
            def scores(i, p):
                pe.wait_ge(s.q.sem, s.q.at(i + 1))
                pe.wait_ge(s.k.sem, s.k.at(i + 1))
                pe.wait_ge(read.sem, read.at(i))
                for b in range(2):
                    for c in range(FC):
                        last = pe.matmul(psS[b * SECOND:b * SECOND + SECOND, c * lanes:(c + 1) * lanes],
                                         qT[:, p, c, b * SEQ:b * SEQ + SECOND],
                                         k_spread[:, p, c, :, b * SEQ:(b + 1) * SEQ], start=True, stop=True)
                last.then_inc(s.scores.sem, 1)

            def turn_weights(i, p):
                pe.wait_ge(s.weight.sem, s.weight.at(i + 1))
                pe.wait_ge(s.weightT.sem, s.weightT.at(i))
                for g in range(GROUPS):
                    n = GROUP * SEQ
                    last = pe.matmul(psT[0:n, g * P:(g + 1) * P], weight[:, p, g * n:(g + 1) * n], m.ident[:, :],
                                     start=True, stop=True, is_transpose=True)
                last.then_inc(s.turned.sem, 1)

            def projections(i, p):
                pe.wait_ge(s.stage.sem, s.stage.at(i + 1))
                pe.wait_ge(s.q.sem, s.q.at(i))
                pe.wait_ge(s.k.sem, s.k.at(i))
                pe.wait_ge(s.v.sem, s.v.at(i))
                pairs = [(psQ, Wq), (psK, Wk)] + [(psX, Wq_turned), (psR, Wk_turned)] * rotary
                for bank, weights in pairs:
                    if bank is psX:
                        pe.wait_ge(s.context_out.sem, s.context_out.at(i - 3))
                    for out in range(FC):
                        for c in range(FC):
                            pe.matmul(both(bank)[:, out, :], weights[:, c, out * FP:(out + 1) * FP],
                                      x_pair[:, p, c, :], start=(c == 0), stop=(c == FC - 1))
                pe.wait_ge(s.tripled.sem, s.tripled.at(i + 1))
                for b in range(2):
                    for c in range(FC):
                        last = pe.matmul(psV[0:GROUP * SEQ, b * D:(b + 1) * D], x_tripled[:, p, c, b, :], Wv[:, c, :],
                                         start=(c == 0), stop=(c == FC - 1))
                last.then_inc(s.projected.sem, 1)

            def weigh(i, p):
                pe.wait_ge(s.weightT.sem, s.weightT.at(i + 1))
                pe.wait_ge(s.v.sem, s.v.at(i + 1))
                pe.wait_ge(s.context.sem, s.context.at(i))
                for b in range(2):
                    for g in range(GROUPS):
                        cols = slice(g * GROUP * HEAD, (g + 1) * GROUP * HEAD)
                        last = pe.matmul(psC[b * SECOND:b * SECOND + SECOND, cols],
                                         weightT[:, p, g, b * SECOND:b * SECOND + SECOND],
                                         v_spread[:, p, b, cols], start=True, stop=True)
                last.then_inc(s.weighed.sem, 1)

            def turn_context(i, p):
                pe.wait_ge(s.context.sem, s.context.at(i + 1))
                pe.wait_ge(s.context_out.sem, s.context_out.at(i))
                if rotary:
                    pe.wait_ge(s.q.sem, s.q.at(min(i + 4, PAIRS) if isinstance(i, int) else i + 4))
                for c in range(FC):
                    last = pe.matmul(psX[0:FP, c * P:(c + 1) * P], context[:, p, c * FP:(c + 1) * FP], m.ident[:, :],
                                     start=True, stop=True, is_transpose=True)
                last.then_inc(s.context_turned.sem, 1)

            def turn(i, p):
                if has(i - 1):
                    scores(i - 1, 1 - p)
                if has(i - 2):
                    turn_weights(i - 2, p)
                if has(i):
                    projections(i, p)
                if has(i - 2):
                    weigh(i - 2, p)
                if has(i - 3):
                    turn_context(i - 3, 1 - p)

            pe.wait_ge(s.attention_w.sem, s.attention_w.at(16 * (layer + 2)))
            turns(pe, turn)

        @block.gpsimd
        def _(pool):
            def triple(i, p):
                pool.wait_ge(s.projected.sem, s.projected.at(i - 1))
                for c in range(FC):
                    for b in range(2):
                        last = pool.tensor_copy(
                            x_tripled[:, p, c, b, :].rearrange("f (r k) -> f r k", r=GROUP),
                            m.xT[:, c, ds(i * PAIR + b * SEQ, SEQ)].unsqueeze(1).to_broadcast([FP, GROUP, SEQ]))
                last.then_inc(s.tripled.sem, 1)

            turns(pool, lambda i, p: triple(i, p) if has(i) else None)

        @block.scalar
        def _(act):
            def stage(i, p):
                act.wait_ge(s.projected.sem, s.projected.at(i - 1))
                act.activation(x_pair[:, p, :, :], m.xT[:, :, ds(i * PAIR, PAIR)], ACT.Copy).then_inc(s.stage.sem, 1)

            def queries(i, p):
                act.wait_ge(s.projected.sem, s.projected.at(i + 1))
                act.wait_ge(s.scores.sem, s.scores.at(i - 1))
                for c in range(FC):
                    last = act.activation(qT[:, p, c, 0:PAIR], both(psQ)[:, c, :], ACT.Identity,
                                          bias=qbias[:, c:c + 1])
                last.then_inc(s.q.sem, 1)

            def exponentials(i, p):
                act.wait_ge(s.shifted.sem, s.shifted.at(i + 1))
                if kind == "erf":
                    act.activation(erf_tmp[:, p, :], weight[:, p, :], ACT.Gelu).then_inc(s.gelu.sem, 1)
                else:
                    act.activation(weight[:, p, :], weight[:, p, :], ACT.Exp, scale=0.25).then_inc(s.weight.sem, 1)

            def weights_out(i, p):
                act.wait_ge(s.turned.sem, s.turned.at(i + 1))
                act.wait_ge(s.weighed.sem, s.weighed.at(i - 1))
                act.activation(weightT[:, p, :, :], psT[0:GROUP * SEQ, 0:GROUPS * P].rearrange("k (g q) -> k g q", g=GROUPS),
                               ACT.Copy).then_inc(s.weightT.sem, 1)

            def context_out(i, p):
                act.wait_ge(s.context_turned.sem, s.context_turned.at(i + 1))
                for c in range(FC):
                    rows = psX[0:FP, c * P:(c + 1) * P].rearrange("f (b k) -> f b k", b=2)[:, :, 0:SEQ]
                    last = act.activation(m.xT[:, c, ds(i * PAIR, PAIR)].rearrange("f (b k) -> f b k", b=2), rows,
                                          ACT.Identity, bias=vbias[:, c:c + 1])
                last.then_inc(s.context_out.sem, 1)

            def turn(i, p):
                if has(i - 2):
                    weights_out(i - 2, p)
                if has(i - 1):
                    exponentials(i - 1, 1 - p)
                if has(i + 1):
                    stage(i + 1, 1 - p)
                if has(i) and not rotary:
                    queries(i, p)
                if has(i - 3):
                    context_out(i - 3, 1 - p)

            stage(0, 0)
            turns(act, turn)

        @block.vector
        def _(vec):
            vec.memset(qT[:, :, :, PAIR:SECOND + SEQ], 0.0).then_inc(s.vec.sem, 1)
            count = 0 if kind == "plain" else {"causal": 1, "erf": 4}[kind]

            def spread_keys(i, p):
                vec.wait_ge(s.projected.sem, s.projected.at(i + 1))
                vec.wait_ge(s.scores.sem, s.scores.at(i - 1))
                for c in range(FC):
                    key = both(psK)[:, c, :] if not rotary else k_rot[:, p, c, :]
                    last = vec.scalar_tensor_tensor(
                        k_spread[:, p, c, :, :], key.unsqueeze(1).to_broadcast(spread), kbias[:, c:c + 1],
                        m.head_mask[:, :].unsqueeze(2).to_broadcast(spread), ALU.add, ALU.mult)
                last.then_inc(s.k.sem, 1)

            def rotate(i, p):
                vec.wait_ge(s.projected.sem, s.projected.at(i + 1))
                vec.wait_ge(s.scores.sem, s.scores.at(i - 1))
                shape = [FP, FC * 2, SEQ]
                cos = m.cos[:, :].unsqueeze(1).to_broadcast(shape)
                sin = m.sin[:, :].unsqueeze(1).to_broadcast(shape)

                def flat(a):
                    return a.rearrange("f (x k) -> f x k", k=SEQ)
                t = [rot_tmp[:, j, :, :].rearrange("f c (b k) -> f (c b) k", b=2) for j in range(4)]
                vec.tensor_tensor(t[0], flat(psQ[0:FP, 0:FC * PAIR]), cos, ALU.mult)
                vec.tensor_tensor(t[1], flat(psX[0:FP, 0:FC * PAIR]), sin, ALU.mult)
                vec.tensor_tensor(t[2], flat(psK[0:FP, 0:FC * PAIR]), cos, ALU.mult)
                vec.tensor_tensor(t[3], flat(psR[0:FP, 0:FC * PAIR]), sin, ALU.mult).then_inc(s.rot.sem, 1)
                vec.wait_ge(s.rot.sem, s.rot.at(2 * i + 1))
                vec.tensor_tensor(qT[:, p, :, 0:PAIR], rot_tmp[:, 0, :, :], rot_tmp[:, 1, :, :], ALU.add).then_inc(s.q.sem, 1)
                vec.tensor_tensor(k_rot[:, p, :, :], rot_tmp[:, 2, :, :], rot_tmp[:, 3, :, :], ALU.add).then_inc(s.rot.sem, 1)
                vec.wait_ge(s.rot.sem, s.rot.at(2 * i + 2))

            def spread_values(i, p):
                vec.wait_ge(s.weighed.sem, s.weighed.at(i - 1))
                shape = [GROUP * SEQ, 2 * GROUPS, GROUP * HEAD]
                vec.tensor_tensor(v_spread[:, p, :, :].rearrange("k b (g n) -> k (b g) n", g=GROUPS),
                                  psV[0:GROUP * SEQ, 0:2 * D].rearrange("k (x n) -> k x n", n=GROUP * HEAD),
                                  m.value_mask[:, :].unsqueeze(1).to_broadcast(shape), ALU.mult).then_inc(s.v.sem, 1)

            by_head = [P, HEADS, SEQ]

            def shift(i, p):
                vec.wait_ge(s.scores.sem, s.scores.at(i + 1))
                vec.wait_ge(s.turned.sem, s.turned.at(i - 1))
                x = weight[:, p, :].rearrange("q (h k) -> q h k", h=HEADS)
                ps = psS[:, 0:HEADS * SEQ].rearrange("q (h k) -> q h k", h=HEADS)
                mask = m.causal[:, :].unsqueeze(1).to_broadcast(by_head)
                if kind == "erf":
                    vec.tensor_scalar(weight[:, p, :], psS[:, 0:HEADS * SEQ], 0.25 * 2.0 ** 0.5, None,
                                      ALU.mult).then_inc(s.scored.sem, 1)
                    vec.wait_ge(s.scored.sem, s.scored.at(i + 1))
                    link(vec, s.soft, vec.tensor_scalar(erf_tmp[:, p, :], weight[:, p, :], 0.0, 1e-20,
                                                        ALU.is_equal, ALU.mult), 5 * i + 1)
                    vec.tensor_tensor(weight[:, p, :], weight[:, p, :], erf_tmp[:, p, :], ALU.add).then_inc(s.shifted.sem, 1)
                    return
                src = ps
                if kind == "causal":
                    vec.tensor_tensor(x, ps, mask, ALU.add).then_inc(s.scored.sem, 1)
                    vec.wait_ge(s.scored.sem, s.scored.at(i + 1))
                    src = x
                link(vec, s.soft, vec.tensor_reduce(row_max[:, p, :], src, AX, ALU.max), 2 * i + 1)
                last = vec.tensor_tensor(x, src, row_max[:, p, :].unsqueeze(2).to_broadcast(by_head), ALU.subtract)
                last.then_inc(s.shifted.sem, 1)

            def total(i, p):
                x = weight[:, p, :].rearrange("q (h k) -> q h k", h=HEADS)
                if kind == "erf":
                    vec.wait_ge(s.gelu.sem, s.gelu.at(i + 1))
                    link(vec, s.soft, vec.reciprocal(weight[:, p, :], weight[:, p, :]), 5 * i + 2)
                    link(vec, s.soft, vec.tensor_tensor(weight[:, p, :], weight[:, p, :], erf_tmp[:, p, :], ALU.mult),
                         5 * i + 3)
                    vec.tensor_tensor(x, x, m.causal_two[:, :].unsqueeze(1).to_broadcast(by_head),
                                      ALU.mult).then_inc(s.weight.sem, 1)
                vec.wait_ge(s.weight.sem, s.weight.at(i + 1))
                per, at = (5, 4) if kind == "erf" else (2, 2)
                link(vec, s.soft, vec.tensor_reduce(row_sum[:, p, :], x, AX, ALU.add), per * i + at)
                if kind == "erf":
                    link(vec, s.soft, vec.tensor_scalar(row_sum[:, p, :], row_sum[:, p, :], 1e-6, None, ALU.max),
                         5 * i + 5)
                vec.reciprocal(row_sum[:, p, :], row_sum[:, p, :]).then_inc(s.inverse.sem, 1)

            def normalise(i, p):
                vec.wait_ge(s.inverse.sem, s.inverse.at(i + 1))
                vec.wait_ge(s.weighed.sem, s.weighed.at(i + 1))
                vec.wait_ge(s.context_turned.sem, s.context_turned.at(i - 1))
                shape = [P, HEADS, HEAD]
                vec.tensor_tensor(context[:, p, :].rearrange("q (h d) -> q h d", h=HEADS),
                                  psC[:, 0:D].rearrange("q (h d) -> q h d", h=HEADS),
                                  row_sum[:, p, :].unsqueeze(2).to_broadcast(shape), ALU.mult).then_inc(s.context.sem, 1)

            def turn(i, p):
                if has(i - 1):
                    shift(i - 1, 1 - p)
                if has(i):
                    if rotary:
                        rotate(i, p)
                    spread_keys(i, p)
                    spread_values(i, p)
                if has(i - 1):
                    total(i - 1, 1 - p)
                if has(i - 2):
                    normalise(i - 2, p)

            vec.wait_ge(s.vec.sem, s.vec.at(1))
            turns(vec, turn)

        @block.sync
        def _(sp):
            if prefetch:
                prefetch(sp)
    n = PAIRS
    for signal in (s.q, s.k, s.v, s.tripled, s.scores, s.weight, s.weightT, s.turned, s.stage, s.projected,
                   s.context, s.context_turned, s.context_out, s.weighed, s.shifted, s.inverse):
        signal.close(n)
    if kind != "plain":
        s.scored.close(n)
    s.vec.close(1)
    s.soft.close((5 if kind == "erf" else 2) * n)
    if kind == "erf":
        s.gelu.close(n)
        s.rot.close(2 * n)


def rwkv_phase(nc, m, s):
    at_once = 16
    turns = IMAGES // at_once
    n_tok = at_once * SEQ
    width = SEQ + 1
    half = at_once // 2
    w = m.attention_w[1]
    STEPS = 15
    with ExitStack() as ctx:
        def buf(name, shape):
            return ctx.enter_context(nc.sbuf_tensor("rwkv_" + name, shape, F32))

        xpad = buf("xpad", [FP, FC, IMAGES, width])
        mixed = buf("mixed", [FP, 3, FC, at_once, SEQ])
        decay, kp, vp, mx, ea, eb, num, den = (
            buf(x, [FP, FC, at_once, width]) for x in ("decay", "kp", "vp", "mx", "ea", "eb", "num", "den"))
        er, t1, t2, t3 = (buf(x, [FP, FC, at_once, SEQ]) for x in ("er", "t1", "t2", "t3"))
        block = ctx.enter_context(nc.Block(no_gpsimd_drain=True))

        def rows(b):
            return b[:, :, :, :].rearrange("f c b k -> f (c b) k")

        def now(b):
            return rows(b)[:, :, 1:width]

        def before(b):
            return rows(b)[:, :, 0:SEQ]

        def line(b):
            return b[:, :, :, :].rearrange("f c b k -> f (c b k)")

        @block.vector
        def _(vec):
            vec.memset(xpad[:, :, :, 0:1], 0.0)
            for b, value in ((kp, -1e38), (vp, 0.0), (ea, 0.0), (eb, 0.0), (decay, -2e38)):
                vec.memset(b[:, :, :, 0:1], value)
            vec.wait_ge(s.exps.sem, s.exps.at(1))
            for c in range(FC):
                vec.tensor_scalar(decay[:, c, :, 1:width], m.decay[:, c:c + 1].unsqueeze(2).to_broadcast([FP, at_once, SEQ]),
                                  -1.0, None, ALU.mult)
                vec.tensor_copy(xpad[:, c, :, 1:width], m.xT[:, c, :].rearrange("f (b k) -> f b k", k=SEQ))
            link(vec, s.vec, vec.tensor_scalar(m.unmix[:, :], m.mix[:, :], -1.0, 1.0, ALU.mult, ALU.add), 1)
            with vec.Fori(0, turns) as g:
                def step(n, ins):
                    link(vec, s.vec, ins, g * STEPS + (n + 1))

                vec.wait_ge(s.mm.sem, s.mm.at(3 * g))
                for j in range(3):
                    for c in range(FC):
                        last = vec.tensor_scalar(mixed[:, j, c, :, :], xpad[:, c, ds(g * at_once, at_once), 1:width],
                                                 m.mix[:, j * FC + c:j * FC + c + 1], None, ALU.mult)
                step(1, last)
                for j in range(3):
                    for c in range(FC):
                        last = vec.scalar_tensor_tensor(
                            mixed[:, j, c, :, :], xpad[:, c, ds(g * at_once, at_once), 0:SEQ],
                            m.unmix[:, j * FC + c:j * FC + c + 1], mixed[:, j, c, :, :], ALU.mult, ALU.add)
                last.then_inc(s.stage.sem, 1)
                vec.wait_ge(s.k.sem, s.k.at(g + 1))
                step(2, vec.tensor_tensor_scan(line(mx), line(decay), line(kp), 0.0, ALU.add, ALU.max))
                step(3, vec.tensor_tensor(now(ea), before(mx), now(decay), ALU.add))
                vec.tensor_tensor(now(ea), now(ea), now(mx), ALU.subtract)
                vec.tensor_tensor(now(eb), now(kp), now(mx), ALU.subtract).then_inc(s.shifted.sem, 1)
                for c in range(FC):
                    last = vec.tensor_scalar(t1[:, c, :, :], kp[:, c, :, 1:width], m.first[:, c:c + 1], None, ALU.add)
                step(4, last)
                step(5, vec.tensor_tensor(rows(t2), before(mx), rows(t1), ALU.max))
                vec.tensor_tensor(rows(t1), rows(t1), rows(t2), ALU.subtract)
                vec.tensor_tensor(rows(t2), before(mx), rows(t2), ALU.subtract).then_inc(s.scored.sem, 1)
                vec.wait_ge(s.exps.sem, s.exps.at(2 * g + 2))
                step(6, vec.tensor_tensor_scan(line(den), line(ea), line(eb), 0.0, ALU.mult, ALU.add))
                step(7, vec.tensor_tensor(now(eb), now(eb), now(vp), ALU.mult))
                step(8, vec.tensor_tensor_scan(line(num), line(ea), line(eb), 0.0, ALU.mult, ALU.add))
                vec.wait_ge(s.exps.sem, s.exps.at(2 * g + 3))
                step(9, vec.tensor_tensor(rows(t3), rows(t2), before(num), ALU.mult))
                step(10, vec.tensor_tensor(rows(t2), rows(t2), before(den), ALU.mult))
                step(11, vec.tensor_tensor(rows(t2), rows(t2), rows(t1), ALU.add))
                step(12, vec.tensor_tensor(rows(t1), rows(t1), now(vp), ALU.mult))
                step(13, vec.tensor_tensor(rows(t3), rows(t3), rows(t1), ALU.add))
                step(14, vec.scalar_tensor_tensor(rows(t2), rows(er), 1.0, rows(t2), ALU.add, ALU.mult))
                step(15, vec.reciprocal(rows(t2), rows(t2)))
                for c in range(FC):
                    last = vec.tensor_tensor(m.xT[:, c, ds(g * n_tok, n_tok)].rearrange("f (b k) -> f b k", k=SEQ),
                                             t3[:, c, :, :], t2[:, c, :, :], ALU.mult)
                last.then_inc(s.out.sem, 1)

        @block.tensor
        def _(pe):
            pe.wait_ge(s.attention_w.sem, s.attention_w.at(32))
            with pe.Fori(0, turns) as g:
                pe.wait_ge(s.stage.sem, s.stage.at(g + 1))
                for j in range(3):
                    if j == 0:
                        pe.wait_ge(s.r.sem, s.r.at(g))
                    elif j == 1:
                        pe.wait_ge(s.k.sem, s.k.at(g))
                    else:
                        pe.wait_ge(s.key_out.sem, s.key_out.at(g + 1))
                    for out in range(FC):
                        for b in range(2):
                            for c in range(FC):
                                last = pe.matmul(
                                    m.ps[4 * (j % 2) + 2 * out + b][0:FP, 0:half * SEQ],
                                    w[:, c, j * D + out * FP:j * D + (out + 1) * FP],
                                    mixed[:, j, c, b * half:(b + 1) * half, :].rearrange("f b k -> f (b k)"),
                                    start=(c == 0), stop=(c == FC - 1))
                    last.then_inc(s.mm.sem, 1)

        @block.scalar
        def _(act):
            act.activation(m.decay[:, :], m.decay[:, :], ACT.Exp).then_inc(s.exps.sem, 1)
            with act.Fori(0, turns) as g:
                def images(j, out, b):
                    return m.ps[4 * (j % 2) + 2 * out + b][0:FP, 0:half * SEQ].rearrange("f (b k) -> f b k", k=SEQ)

                for j, (dst, first) in enumerate(((kp, 1), (vp, 1), (er, 0))):
                    act.wait_ge(s.mm.sem, s.mm.at(3 * g + j + 1))
                    if j == 0:
                        act.wait_ge(s.out.sem, s.out.at(g))
                    for out in range(FC):
                        for b in range(2):
                            to = dst[:, out, b * half:(b + 1) * half, first:first + SEQ]
                            if j < 2:
                                last = act.activation(to, images(j, out, b), ACT.Copy)
                            else:
                                last = act.activation(to, images(j, out, b), ACT.Exp, scale=-1.0)
                    last.then_inc((s.key_out, s.k, s.r)[j].sem, 1)
                act.wait_ge(s.shifted.sem, s.shifted.at(g + 1))
                act.activation(now(ea), now(ea), ACT.Exp)
                act.activation(now(eb), now(eb), ACT.Exp).then_inc(s.exps.sem, 1)
                act.wait_ge(s.scored.sem, s.scored.at(g + 1))
                act.activation(rows(t1), rows(t1), ACT.Exp)
                act.activation(rows(t2), rows(t2), ACT.Exp).then_inc(s.exps.sem, 1)
    s.vec.close(1 + turns * STEPS)
    for signal in (s.stage, s.k, s.shifted, s.scored, s.out, s.r, s.key_out):
        signal.close(turns)
    s.mm.close(3 * turns)
    s.exps.close(2 * turns + 1)


def load_expert(sp, m, s, ins, ffn, e, p):
    w1, w2 = ins[ffn.name + "_w1"], ins[ffn.name + "_w2"]
    sp.dma_start(m.w1[p][:, :, 0:w1.shape[3]], w1[ds(e, 1), :, :, :].rearrange("e f c n -> (e f) c n")).then_inc(s.w[p].sem, 16)
    sp.dma_start(m.w2[p][0:w2.shape[1], 0:w2.shape[2], :],
                 w2[ds(e, 1), :, :, :].rearrange("e f c n -> (e f) c n")).then_inc(s.w[p].sem, 16)
    if ffn.biased:
        b1, b2 = ins[ffn.name + "_b1"], ins[ffn.name + "_b2"]
        sp.dma_start(m.hidden_bias[p][0:b1.shape[1], 0:b1.shape[2]],
                     b1[ds(e, 1), :, :].rearrange("e f n -> (e f) n")).then_inc(s.w[p].sem, 16)
        sp.dma_start(m.out_bias[p][:, :], b2[ds(e, 1), :].to_broadcast([P, D])).then_inc(s.w[p].sem, 16)


def load_first(sp, m, s, ins, ffn):
    for e in range(min(2, ffn.experts)):
        load_expert(sp, m, s, ins, ffn, e, e)


def expert_phase(nc, m, s, ins, ffn, dst, prefetch=None, following=None):
    gated = ffn.kind == "gate"
    func = {"gelu": ACT.Gelu, "silu": ACT.Silu, "gate": ACT.Silu}[ffn.kind]
    blocks = ffn.width // ffn.block
    experts, rows = ffn.experts, ffn.block
    tiles = CHUNK // P
    summed = s.summed if ffn.biased else s.out
    hidden_done = s.up_read if gated else s.act
    loads = 16 * (4 if ffn.biased else 2)
    turn_blocks = CHUNKS * blocks
    BANKS = 2
    with (
        nc.sbuf_tensor(f"hT_{ffn.name}", [P, 2, blocks, CHUNK], F32) as hT,
        nc.sbuf_tensor(f"gate_{ffn.name}", [P, 2, CHUNK], F32) as gate,
        nc.sbuf_tensor(f"biased_{ffn.name}", [P, tiles, D], F32) as biased,
        nc.Block(no_gpsimd_drain=True) as block,
    ):

        def over_experts(eng, run):
            if experts == 1:
                return run(0, 0)
            with eng.Fori(0, experts - 1, 2) as e:
                for p in range(2):
                    run(e + p, p)

        def over_chunks(eng, run):
            with eng.Fori(0, CHUNKS - 1, 2) as c:
                for p in range(2):
                    run(c + p, p)

        def loaded(eng, e, p):
            if experts == 1:
                eng.wait_ge(s.w[p].sem, s.w[p].at(loads))
            else:
                eng.wait_ge(s.w[p].sem, s.w[p].at((e - p) * (loads // 2) + loads))

        def turn_of(cp, j):
            return (cp * blocks + j) % BANKS

        def bank(kind, cp, j):
            return m.ps[(0 if kind == "hidden" else BANKS) + turn_of(cp, j)]

        @block.tensor
        def _(pe):
            def expert(e, ep):

                def hidden(c, cp):
                    n = e * turn_blocks + c * blocks
                    for j in range(blocks):
                        x = [m.xT[:, k, ds(c * CHUNK, CHUNK)] for k in range(FC)]
                        pe.wait_ge(s.act.sem, s.act.at(n + (j - 1)))
                        if gated:
                            pe.wait_ge(s.up_read.sem, s.up_read.at(n + (j - 1)))
                        first = ffn.gate_at + j * rows if gated else j * rows
                        for k in range(FC):
                            last = pe.matmul(bank("hidden", cp, j)[0:rows, 0:CHUNK], m.w1[ep][:, k, first:first + rows], x[k],
                                             start=(k == 0), stop=(k == FC - 1))
                        if gated:
                            up = ffn.up_at + j * rows
                            for k in range(FC):
                                last = pe.matmul(bank("up", cp, j)[0:rows, 0:CHUNK], m.w1[ep][:, k, up:up + rows], x[k],
                                                 start=(k == 0), stop=(k == FC - 1))
                        last.then_inc(s.hidden.sem, 1)

                def output(c, cp):
                    n = e * CHUNKS + c
                    pe.wait_ge(hidden_done.sem, hidden_done.at(n * blocks + blocks))
                    for i in range(tiles):
                        pe.wait_ge(s.out.sem, s.out.at(n * tiles + (i - tiles + 1)))
                        for j in range(blocks):
                            last = pe.matmul(m.ps[2 * BANKS + i][:, 0:D], hT[0:rows, cp, j, i * P:(i + 1) * P],
                                             m.w2[ep][0:rows, j, :], start=(j == 0), stop=(j == blocks - 1))
                        last.then_inc(s.mm.sem, 1)

                with pe.Fori(0, CHUNKS - 1, 2) as c:
                    loaded(pe, e, ep)
                    hidden(c, 0)
                    hidden(c + 1, 1)
                    output(c, 0)
                    output(c + 1, 1)

            over_experts(pe, expert)

        @block.scalar
        def _(act):
            def expert(e, ep):
                def chunk(c, cp):
                    n = e * turn_blocks + c * blocks
                    act.wait_ge(s.mm.sem, s.mm.at((e * CHUNKS + c) * tiles - tiles))
                    for j in range(blocks):
                        act.wait_ge(s.hidden.sem, s.hidden.at(n + (j + 1)))
                        kw = {"bias": m.hidden_bias[ep][0:rows, j:j + 1]} if ffn.biased else {}
                        to = hT[0:rows, cp, j, :]
                        if gated:
                            act.wait_ge(s.up_read.sem, s.up_read.at(n + (j - 1)))
                            to = gate[0:rows, turn_of(cp, j), :]
                        act.activation(to, bank("hidden", cp, j)[0:rows, 0:CHUNK], func, **kw).then_inc(s.act.sem, 1)

                over_chunks(act, chunk)

            over_experts(act, expert)

        @block.vector
        def _(vec):
            def expert(e, ep):
                def gates(c, cp):
                    n = e * turn_blocks + c * blocks
                    vec.wait_ge(s.mm.sem, s.mm.at((e * CHUNKS + c) * tiles - tiles))
                    for j in range(blocks):
                        vec.wait_ge(s.hidden.sem, s.hidden.at(n + (j + 1)))
                        vec.wait_ge(s.act.sem, s.act.at(n + (j + 1)))
                        to, g = hT[0:rows, cp, j, :], gate[0:rows, turn_of(cp, j), :]
                        up = bank("up", cp, j)[0:rows, 0:CHUNK]
                        if ffn.biased:
                            up_bias = m.hidden_bias[ep][0:rows, blocks + j:blocks + j + 1]
                            vec.scalar_tensor_tensor(to, up, up_bias, g, ALU.add, ALU.mult).then_inc(s.up_read.sem, 1)
                        else:
                            vec.tensor_tensor(to, up, g, ALU.mult).then_inc(s.up_read.sem, 1)

                def outputs(c, cp):
                    n = (e * CHUNKS + c) * tiles
                    for i in range(tiles):
                        vec.wait_ge(s.mm.sem, s.mm.at(n + (i + 1)))
                        to, t = tile(dst, c * tiles + i), c * tiles + i
                        got = m.ps[2 * BANKS + i][:, 0:D]
                        if ffn.biased:
                            vec.tensor_tensor(biased[:, i, :], got, m.out_bias[ep][:, :], ALU.add).then_inc(s.out.sem, 1)
                            got = biased[:, i, :]
                            vec.wait_ge(s.out.sem, s.out.at(n + (i + 1)))
                        if ffn.comb is None:
                            last = vec.tensor_tensor(to, got, to, ALU.add)
                        else:
                            last = vec.scalar_tensor_tensor(to, got, ffn.comb[:, ds(t * experts + e, 1)], to,
                                                            ALU.mult, ALU.add)
                        last.then_inc(summed.sem, 1)

                with vec.Fori(0, CHUNKS - 1, 2) as c:
                    if ffn.biased:
                        loaded(vec, e, ep)
                    if gated:
                        gates(c, 0)
                        gates(c + 1, 1)
                    outputs(c, 0)
                    outputs(c + 1, 1)

            over_experts(vec, expert)

        @block.sync
        def _(sp):
            if experts > 2:
                with sp.Fori(2, experts - 1, 2) as e:
                    for p in range(2):
                        sp.wait_ge(summed.sem, summed.at((e + (p - 1)) * (CHUNKS * tiles)))
                        load_expert(sp, m, s, ins, ffn, e + p, p)
            if prefetch:
                prefetch(sp)
            done = experts * CHUNKS * tiles
            sp.wait_ge(summed.sem, summed.at(done))
            if following:
                load_first(sp, m, s, ins, following)
    for signal, n in ((s.hidden, experts * turn_blocks), (s.act, experts * turn_blocks),
                      (s.mm, experts * CHUNKS * tiles), (s.out, experts * CHUNKS * tiles)):
        signal.close(n)
    if gated:
        s.up_read.close(experts * turn_blocks)
    if ffn.biased:
        s.summed.close(experts * CHUNKS * tiles)
    s.w[0].close(loads * ((experts + 1) // 2))
    s.w[1].close(loads * (experts // 2))


class Steps:

    def __init__(self, vec, done, n=0):
        self.vec, self.done, self.n = vec, done, n

    def __call__(self, ins):
        self.n += 1
        link(self.vec, self.done, ins, self.n)


def pick_largest(vec, step, m, x, onehot, experts):
    shape = [P, TILES, experts]
    most = m.most[:, :]
    step(vec.tensor_reduce(most, x, AX, ALU.max))
    step(vec.tensor_tensor(onehot, x, most.unsqueeze(2).to_broadcast(shape), ALU.is_equal))
    step(vec.tensor_tensor(onehot, onehot, m.rank[:, 0:experts].unsqueeze(1).to_broadcast(shape), ALU.mult))
    step(vec.tensor_reduce(most, onehot, AX, ALU.max))
    step(vec.tensor_tensor(onehot, onehot, most.unsqueeze(2).to_broadcast(shape), ALU.is_equal))


def weigh_by(vec, step, m, out, x, per_token, experts, op=ALU.mult):
    step(vec.tensor_tensor(out, x, per_token.unsqueeze(2).to_broadcast([P, TILES, experts]), op))


def route_top2_phase(nc, m, s, experts, capacity=None):
    def view(buf, k=experts):
        return buf[:, 0:TILES * k].rearrange("p (t e) -> p t e", e=k)

    x, first, second, other = (view(b) for b in (m.logits, m.pick[0], m.pick[1], m.pick[2]))
    comb = view(m.comb)
    v1, v2, inv = m.token[:, 0, :], m.token[:, 1, :], m.token[:, 2, :]
    cols = TILES * experts
    with nc.Block(no_gpsimd_drain=True) as block:

        @block.vector
        def _(vec):
            step = Steps(vec, s.vec)
            pick_largest(vec, step, m, x, first, experts)
            step(vec.tensor_tensor(other, x, first, ALU.mult))
            step(vec.tensor_reduce(v1, other, AX, ALU.add))
            step(vec.scalar_tensor_tensor(other, first, NEG, x, ALU.mult, ALU.add))
            pick_largest(vec, step, m, other, second, experts)
            step(vec.tensor_tensor(other, x, second, ALU.mult))
            step(vec.tensor_reduce(v2, other, AX, ALU.add))
            vec.tensor_tensor(v2, v2, v1, ALU.subtract).then_inc(s.x.sem, 1)
            if capacity:
                tiles_of = m.prefix[:, 0:cols]
                for j, pick in enumerate((first, second)):
                    vec.wait_ge(s.mm.sem, s.mm.at(j + 1))
                    before = view(m.pick[2])
                    step(vec.tensor_copy(tiles_of.rearrange("p (e t) -> p t e", t=TILES),
                                         m.ps[2 + j][:, 0:cols].rearrange("p (t e) -> p t e", e=experts)))
                    step(vec.tensor_tensor_scan(m.running[:, 0:cols], m.restart[:, 0:cols], tiles_of, 0.0, ALU.mult, ALU.add))
                    step(vec.tensor_tensor(tiles_of, m.running[:, 0:cols], tiles_of, ALU.subtract))
                    step(vec.tensor_tensor(before, m.ps[j][:, 0:cols].rearrange("p (t e) -> p t e", e=experts),
                                           tiles_of.rearrange("p (e t) -> p t e", t=TILES), ALU.add))
                    step(vec.tensor_scalar(before, before, float(capacity), None, ALU.is_le))
                    step(vec.tensor_tensor(pick, pick, before, ALU.mult))
            vec.wait_ge(s.exps.sem, s.exps.at(1))
            step(vec.tensor_scalar(inv, v2, 1.0, None, ALU.add))
            step(vec.reciprocal(inv, inv))
            step(vec.tensor_tensor(v2, v2, inv, ALU.mult))
            weigh_by(vec, step, m, comb, first, inv, experts)
            weigh_by(vec, step, m, other, second, v2, experts)
            step(vec.tensor_tensor(comb, comb, other, ALU.add))
            m.vec_links = step.n

        @block.scalar
        def _(act):
            act.wait_ge(s.x.sem, s.x.at(1))
            act.activation(v2, v2, ACT.Exp).then_inc(s.exps.sem, 1)

        @block.tensor
        def _(pe):
            if capacity:
                pe.wait_ge(s.x.sem, s.x.at(1))
                for j in range(2):
                    pick = m.pick[j][:, 0:cols]
                    pe.matmul(m.ps[j][:, 0:cols], m.triangle[:, :], pick, start=True, stop=True)
                    pe.matmul(m.ps[2 + j][:, 0:cols], m.ones[:, :], pick, start=True, stop=True).then_inc(s.mm.sem, 1)
    s.vec.close(m.vec_links)
    s.x.close(1)
    s.exps.close(1)
    if capacity:
        s.mm.close(2)


def route_top1_phase(nc, m, s, experts):
    def view(buf):
        return buf[:, 0:TILES * experts].rearrange("p (t e) -> p t e", e=experts)

    x, first, comb = view(m.logits), view(m.pick[0]), view(m.comb)
    most = m.token[:, 0, :]
    with nc.Block(no_gpsimd_drain=True) as block:

        @block.vector
        def _(vec):
            step = Steps(vec, s.vec)
            step(vec.tensor_reduce(most, x, AX, ALU.max))
            vec.tensor_tensor(x, x, most.unsqueeze(2).to_broadcast([P, TILES, experts]), ALU.subtract).then_inc(s.x.sem, 1)
            vec.wait_ge(s.exps.sem, s.exps.at(1))
            step(vec.tensor_reduce(most, x, AX, ALU.add))
            step(vec.reciprocal(most, most))
            weigh_by(vec, step, m, x, x, most, experts)
            pick_largest(vec, step, m, x, first, experts)
            step(vec.tensor_tensor(comb, x, first, ALU.mult))
            m.vec_links = step.n

        @block.scalar
        def _(act):
            act.wait_ge(s.x.sem, s.x.at(1))
            act.activation(x, x, ACT.Exp).then_inc(s.exps.sem, 1)
    s.vec.close(m.vec_links)
    s.x.close(1)
    s.exps.close(1)


def route_groups_phase(nc, m, s, experts, groups, top_groups, top, scaling, shared):
    per = experts // groups
    rows = TILES * groups

    def view(buf, k=experts):
        return buf[:, 0:TILES * k].rearrange("p (t e) -> p t e", e=k)

    def grouped(buf):
        return buf[:, 0:TILES * experts].rearrange("p (t k) -> p t k", k=per)

    score, sfc, one, left, taken = (m.logits, *m.pick[0:3], m.running)
    comb = m.comb[:, 0:TILES * (experts + shared)].rearrange("p (t e) -> p t e", e=experts + shared)
    total = m.token[:, 0, :]
    with nc.Block(no_gpsimd_drain=True) as block:

        @block.vector
        def _(vec):
            step = Steps(vec, s.vec)
            vec.wait_ge(s.exps.sem, s.exps.at(1))
            step(vec.tensor_tensor(view(sfc), view(score), m.correction[:, :].unsqueeze(1).to_broadcast([P, TILES, experts]),
                                   ALU.add))
            best = m.group[:, 0, :]
            wide = [P, rows, per]
            step(vec.tensor_reduce(best, grouped(sfc), AX, ALU.max))
            step(vec.tensor_tensor(grouped(one), grouped(sfc), best.unsqueeze(2).to_broadcast(wide), ALU.is_equal))
            step(vec.tensor_tensor(grouped(one), grouped(one), m.rank[:, 0:per].unsqueeze(1).to_broadcast(wide), ALU.mult))
            step(vec.tensor_reduce(m.group[:, 1, :], grouped(one), AX, ALU.max))
            step(vec.tensor_tensor(grouped(one), grouped(one), m.group[:, 1, :].unsqueeze(2).to_broadcast(wide), ALU.is_equal))
            step(vec.scalar_tensor_tensor(left[:, 0:TILES * experts], one[:, 0:TILES * experts], NEG,
                                          sfc[:, 0:TILES * experts], ALU.mult, ALU.add))
            step(vec.tensor_reduce(m.group[:, 1, :], grouped(left), AX, ALU.max))
            step(vec.tensor_tensor(best, best, m.group[:, 1, :], ALU.add))
            def by_group(j):
                return m.group[:, j, :].rearrange("p (t g) -> p t g", g=groups)
            for n in range(top_groups):
                pick_largest(vec, step, m, by_group(0), by_group(1), groups)
                if n == 0:
                    step(vec.tensor_copy(m.group[:, 2, :], m.group[:, 1, :]))
                else:
                    step(vec.tensor_tensor(m.group[:, 2, :], m.group[:, 2, :], m.group[:, 1, :], ALU.add))
                if n < top_groups - 1:
                    step(vec.scalar_tensor_tensor(best, m.group[:, 1, :], NEG, best, ALU.mult, ALU.add))
            step(vec.tensor_tensor(grouped(sfc), grouped(sfc), m.group[:, 2, :].unsqueeze(2).to_broadcast(wide), ALU.mult))
            for n in range(top):
                pick_largest(vec, step, m, view(sfc), view(one), experts)
                if n == 0:
                    step(vec.tensor_copy(view(taken), view(one)))
                else:
                    step(vec.tensor_tensor(view(taken), view(taken), view(one), ALU.add))
                if n < top - 1:
                    step(vec.scalar_tensor_tensor(sfc[:, 0:TILES * experts], one[:, 0:TILES * experts], NEG,
                                                  sfc[:, 0:TILES * experts], ALU.mult, ALU.add))
            step(vec.tensor_tensor(view(taken), view(taken), view(score), ALU.mult))
            step(vec.tensor_reduce(total, view(taken), AX, ALU.add))
            step(vec.tensor_scalar(total, total, 1e-20, None, ALU.add))
            step(vec.reciprocal(total, total))
            step(vec.memset(comb[:, :, experts:experts + shared], 1.0))
            weigh_by(vec, step, m, view(taken), view(taken), total, experts)
            step(vec.tensor_scalar(comb[:, :, 0:experts], view(taken), scaling, None, ALU.mult))
            m.vec_links = step.n

        @block.scalar
        def _(act):
            act.activation(m.logits[:, 0:TILES * experts], m.logits[:, 0:TILES * experts], ACT.Sigmoid).then_inc(s.exps.sem, 1)
    s.vec.close(m.vec_links)
    s.exps.close(1)


class Signals:

    def __init__(self, make):
        def signal(name):
            return Signal(make(name))

        def arrival(name):
            return Signal(make(name), 0)

        self.vec = signal("vec")
        self.soft = signal("soft")
        self.rot = signal("rot")
        self.stats = signal("stats")
        self.var = signal("var")
        self.std = signal("std")
        self.x = signal("x")
        self.kept = signal("kept")
        self.turned = signal("turned")
        self.xT = signal("xT")
        self.route = signal("route")
        self.logit = signal("logit")
        self.stage = signal("stage")
        self.mm = signal("mm")
        self.out = signal("out")
        self.q = signal("q")
        self.k = signal("k")
        self.v = signal("v")
        self.r = signal("r")
        self.key_out = signal("key_out")
        self.projected = signal("projected")
        self.tripled = signal("tripled")
        self.scores = signal("scores")
        self.scored = signal("scored")
        self.shifted = signal("shifted")
        self.gelu = signal("gelu")
        self.exps = signal("exps")
        self.weight = signal("weight")
        self.weightT = signal("weightT")
        self.inverse = signal("inverse")
        self.weighed = signal("weighed")
        self.context = signal("context")
        self.context_turned = signal("context_turned")
        self.context_out = signal("context_out")
        self.hidden = signal("hidden")
        self.act = signal("act")
        self.up_read = signal("up_read")
        self.summed = signal("summed")
        self.patch = signal("patch")
        self.lead = [self.vec, self.soft, self.rot, self.stats, self.var, self.std, self.x, self.kept, self.turned,
                     self.xT, self.route, self.logit, self.stage, self.mm, self.out, self.q, self.k, self.v, self.r,
                     self.key_out, self.projected, self.tripled, self.scores, self.scored, self.shifted, self.gelu,
                     self.exps, self.weight, self.weightT, self.inverse, self.weighed, self.context,
                     self.context_turned, self.context_out, self.hidden, self.act, self.up_read, self.summed,
                     self.patch]
        self.consts = arrival("consts")
        self.image = [arrival(f"image{i}") for i in range(IMAGES * GRID // P)]
        self.patch_store = arrival("patch_store")
        self.patch_load = arrival("patch_load")
        self.attention_w = arrival("attention_w")
        self.w = [arrival(f"expert_w{i}") for i in range(2)]
        self.store = arrival("store")


class Memory:

    def __init__(self, nc, ctx):
        def sb(name, *shape):
            return ctx.enter_context(nc.sbuf_tensor(name, list(shape), F32))

        self.loads = []

        def const(name, *shape):
            buf = sb(name, *shape)
            self.loads.append((name, buf))
            return buf

        self.ident, self.triangle, self.ones = const("ident", P, P), const("triangle", P, P), const("ones", P, P)
        self.rank, self.restart = const("rank", P, 16), const("restart", P, 8 * TILES)
        self.head_mask = const("head_mask", FP, HPC)
        self.value_mask = const("value_mask", GROUP * SEQ, GROUP * HEAD)
        self.causal, self.causal_two = const("causal", P, SEQ), const("causal_two", P, SEQ)
        self.cos, self.sin, self.zero_bias = const("cos", FP, SEQ), const("sin", FP, SEQ), const("zero_bias", FP, FC)
        self.W1, self.b1, self.W2, self.b2 = const("W1", P, PATCH), const("b1", P, 1), const("W2", P, PATCH), const("b2", P, 1)
        self.W3, self.b3 = const("W3", CHANNELS, D), const("b3", P, D)
        self.mix, self.decay, self.first = const("mix", FP, 3 * FC), const("decay", FP, FC), const("first", FP, FC)
        self.ln = const("ln", FP, 4 * FC)
        self.qkv0, self.qkv1 = const("qkv0", FP, 3 * FC), const("qkv1", FP, 3 * FC)
        self.out0, self.out1 = const("out0", 1, D), const("out1", 1, D)
        self.router0, self.router_b0 = const("router0", FP, FC, 4), const("router_b0", P, 4)
        self.router1, self.router2 = const("router1", FP, FC, 8), const("router2", FP, FC, 8)
        self.router3, self.router_b3 = const("router3", FP, FC, 16), const("router_b3", P, 16)
        self.correction = const("correction", P, 16)
        self.h, self.z, self.xT = sb("h", P, TILES * D), sb("z", P, TILES * D), sb("xT", FP, FC, TOKENS)
        self.xs, self.x_tile = sb("xs", FP, 2, FC, P), sb("x_tile", P, 2, D)
        self.stats, self.mean = sb("stats", P, TILES * 6), sb("mean", P, TILES)
        self.other, self.rstd, self.unmix = sb("other", P, TILES), sb("rstd", P, TILES), sb("unmix", FP, 3 * FC)
        self.logits, self.comb = sb("logits", P, TILES * 16), sb("comb", P, TILES * 18)
        self.pick = [sb(f"pick{i}", P, TILES * 16) for i in range(3)]
        self.most, self.token, self.group = sb("most", P, TILES), sb("token", P, 3, TILES), sb("group", P, 3, TILES * 4)
        self.prefix, self.running = sb("prefix", P, TILES * 8), sb("running", P, TILES * 16)
        self.attention_w = [sb(f"attention_w{i}", FP, FC, 6 * D) for i in range(2)]
        self.w1 = [sb(f"w1_{i}", FP, FC, 1024) for i in range(2)]
        self.w2 = [sb(f"w2_{i}", P, 6, D) for i in range(2)]
        self.out_bias = [sb(f"out_bias{i}", P, D) for i in range(2)]
        self.hidden_bias = [sb(f"hidden_bias{i}", P, 6) for i in range(2)]
        self.ps = [ctx.enter_context(nc.psum_tensor(f"bank{i}", [P, 512], F32)) for i in range(8)]


class FeedForward:

    def __init__(self, name, experts, kind, width, biased=True, comb=None, block=P, gate_at=0, up_at=0):
        self.name, self.experts, self.kind, self.width, self.biased = name, experts, kind, width, biased
        self.comb, self.block, self.gate_at, self.up_at = comb, block, gate_at, up_at


def start_phase(nc, m, s, ins):
    with nc.Block(no_gpsimd_drain=True) as block:

        @block.vector
        def _(vec):
            for signal in s.lead:
                vec.sem_inc(signal.sem, LEAD)

        @block.sync
        def _(sp):
            for name, buf in m.loads:
                shape = list(buf.shape)
                src = ins[name] if ins[name].shape[0] == shape[0] else ins[name].to_broadcast(shape)
                sp.dma_start(buf[:, :] if len(shape) == 2 else buf[:, :, :], src).then_inc(s.consts.sem, 16)
            sp.wait_ge(s.consts.sem, 16 * len(m.loads))


def tower(nc, ins, out, patch_dram):
    with ExitStack() as ctx:
        m = Memory(nc, ctx)
        s = Signals(lambda name: ctx.enter_context(nc.semaphore(name)))
        m.patch_dram = patch_dram

        def three(buf, first=0):
            return [buf[:, (first + j) * FC:(first + j + 1) * FC] for j in range(3)]

        def output_w(layer):
            return m.attention_w[layer % 2][:, :, 3 * D:4 * D]

        g1, b1, g2, b2 = (m.ln[:, j * FC:(j + 1) * FC] for j in range(4))
        mlp = FeedForward("mlp", 1, "gelu", 768)
        ffn0 = FeedForward("ffn0", 4, "gelu", 768, comb=m.comb)
        ffn1 = FeedForward("ffn1", 8, "silu", 768, comb=m.comb)
        ffn2 = FeedForward("ffn2", 8, "gate", 512, biased=False, comb=m.comb, gate_at=512)
        ffn3 = FeedForward("ffn3", 18, "gate", 96, comb=m.comb, block=96, up_at=96)

        start_phase(nc, m, s, ins)
        token_phase(nc, m, s, ins)

        feature_phase(nc, m, s, m.h)
        rwkv_phase(nc, m, s)
        project_phase(nc, m, s, output_w(1), m.h)
        feature_phase(nc, m, s, m.h, keep=m.z)
        feature_phase(nc, m, s, m.z, scale=g1, shift=b1)
        attention_phase(nc, m, s, 0, "plain", three(m.qkv0), lambda sp: load_first(sp, m, s, ins, mlp))
        project_phase(nc, m, s, output_w(0), m.z, m.out0[0:1, :])
        feature_phase(nc, m, s, m.z, norm=False)
        expert_phase(nc, m, s, ins, mlp, m.z, lambda sp: load_attention(sp, m, s, ins, 1), ffn0)
        feature_phase(nc, m, s, m.z, scale=g2, shift=b2, router=(m.router0, m.router_b0[:, :], 4))
        route_top2_phase(nc, m, s, 4)
        expert_phase(nc, m, s, ins, ffn0, m.z, following=ffn1)
        add_phase(nc, m, s, m.h, m.z)

        feature_phase(nc, m, s, m.h)
        attention_phase(nc, m, s, 1, "causal", three(m.qkv1))
        project_phase(nc, m, s, output_w(1), m.h, m.out1[0:1, :])
        feature_phase(nc, m, s, m.h, router=(m.router1, None, 8))
        route_top1_phase(nc, m, s, 8)
        expert_phase(nc, m, s, ins, ffn1, m.h, lambda sp: load_attention(sp, m, s, ins, 2), ffn2)

        feature_phase(nc, m, s, m.h)
        attention_phase(nc, m, s, 2, "erf")
        project_phase(nc, m, s, output_w(2), m.h)
        feature_phase(nc, m, s, m.h, router=(m.router2, None, 8))
        route_top2_phase(nc, m, s, 8, capacity=int(1.2 * TOKENS / 8))
        expert_phase(nc, m, s, ins, ffn2, m.h, lambda sp: load_attention(sp, m, s, ins, 3), ffn3)

        feature_phase(nc, m, s, m.h)
        attention_phase(nc, m, s, 3, "causal")
        project_phase(nc, m, s, output_w(3), m.h)
        feature_phase(nc, m, s, m.h, router=(m.router3, m.router_b3[:, :], 16))
        route_groups_phase(nc, m, s, experts=16, groups=4, top_groups=2, top=4, scaling=2.5, shared=2)
        expert_phase(nc, m, s, ins, ffn3, m.h)

        store_phase(nc, s, m.h, out)


def constants():
    f = np.float32
    p = np.arange(P)
    query = np.where(p < SEQ, p, np.where((p >= SECOND) & (p < SECOND + SEQ), p - SECOND, SEQ))
    seen = np.arange(SEQ)[None, :] <= query[:, None]
    half = HEAD // 2
    freq = (f(1.0) / f(10000.0) ** (np.arange(half, dtype=f) / f(half))).astype(f)
    angle = freq[:, None] * np.arange(SEQ, dtype=f)[None, :]
    pair = (np.arange(FP) % HEAD) // 2
    sign = np.where(np.arange(FP) % 2 == 0, f(-1), f(1))
    return {
        "ident": np.eye(P, dtype=f),
        "triangle": (p[:, None] <= p[None, :]).astype(f),
        "ones": np.ones((P, P), f),
        "rank": np.tile(np.arange(16, 0, -1).astype(f), (P, 1)),
        "restart": np.tile((np.arange(8 * TILES) % TILES != 0).astype(f), (P, 1)),
        "head_mask": (np.arange(FP)[:, None] // HEAD == np.arange(HPC)[None, :]).astype(f),
        "value_mask": (np.arange(GROUP * SEQ)[:, None] // SEQ == np.arange(GROUP * HEAD)[None, :] // HEAD).astype(f),
        "causal": np.where(seen, f(0), f(NEG)).astype(f),
        "causal_two": np.where(seen, f(2), f(0)).astype(f),
        "cos": np.cos(angle)[pair].astype(f),
        "sin": (np.sin(angle)[pair] * sign[:, None]).astype(f),
        "zero_bias": np.zeros((FP, FC), f),
    }


def layout(a):
    def feature(w):
        return w.reshape(FC, FP, -1).transpose(1, 0, 2)

    def column(*v):
        return np.concatenate([x.reshape(FC, FP).T for x in v], axis=1)

    def hidden(v, rows):
        return v.reshape(v.shape[0], -1, rows).transpose(0, 2, 1)

    def first(w):
        return w.reshape(w.shape[0], FC, FP, -1).transpose(0, 2, 1, 3)

    def second(w, rows):
        return w.reshape(w.shape[0], -1, rows, D).transpose(0, 2, 1, 3)

    def side(*w):
        return feature(np.concatenate(w, axis=1))

    turned = np.arange(D) ^ 1
    wide = D // 2
    t = constants()
    x = a["x"].reshape(IMAGES, CHANNELS, GRID, PATCH * SIDE).transpose(1, 0, 2, 3)
    t.update({
        "x": x.reshape(CHANNELS, IMAGES * GRID, PATCH * SIDE),
        "W1": a["L0_tok_W1"], "b1": a["L0_tok_b1"].reshape(1, 1), "W2": a["L0_tok_W2"],
        "b2": a["L0_tok_b2"].reshape(1, 1), "W3": a["L0_tok_W3"].T, "b3": a["L0_tok_b3"].reshape(1, D),
        "mix": column(a["L0_attn_mix_k"], a["L0_attn_mix_v"], a["L0_attn_mix_r"]),
        "decay": column(a["L0_attn_time_decay"]), "first": column(a["L0_attn_time_first"]),
        "rwkv": side(*(a[f"L0_attn_W{k}"].T for k in "kvro")),
        "ln": column(a["L0_ffn_ln1_g"], a["L0_ffn_ln1_b"], a["L0_ffn_ln2_g"], a["L0_ffn_ln2_b"]),
        "attention0": side(a["L0_ffn_in_w"].T, a["L0_ffn_out_w"].T),
        "attention1": side(a["L1_attn_W_attn"], a["L1_attn_W_proj"]),
        "attention2": side(*(a[f"L2_attn_W{k}"].T for k in ("q", "k", "v", "proj")),
                           a["L2_attn_Wq"].T[:, turned], a["L2_attn_Wk"].T[:, turned]),
        "attention3": side(*(a[f"L3_attn_w{k}"].T for k in "qkvo")),
        "qkv0": column(*a["L0_ffn_in_b"].reshape(3, D)), "qkv1": column(*a["L1_attn_b_attn"].reshape(3, D)),
        "out0": a["L0_ffn_out_b"].reshape(1, D), "out1": a["L1_attn_b_proj"].reshape(1, D),
        "router0": feature(a["L0_ffn_gate_w"].T), "router_b0": a["L0_ffn_gate_b"].reshape(1, -1),
        "router1": feature(a["L1_ffn_Wg"]), "router2": feature(a["L2_ffn_Wg"]),
        "router3": feature(a["L3_ffn_router_w"].T), "router_b3": a["L3_ffn_router_b"].reshape(1, -1),
        "correction": a["L3_ffn_corr_bias"].reshape(1, -1),
        "mlp_w1": first(a["L0_ffn_mlp_w1"][None]), "mlp_w2": second(a["L0_ffn_mlp_w2"][None], P),
        "mlp_b1": hidden(a["L0_ffn_mlp_b1"][None], P), "mlp_b2": a["L0_ffn_mlp_b2"].reshape(1, D),
        "ffn0_w1": first(a["L0_ffn_exp_w1"]), "ffn0_w2": second(a["L0_ffn_exp_w2"], P),
        "ffn0_b1": hidden(a["L0_ffn_exp_b1"], P), "ffn0_b2": a["L0_ffn_exp_b2"],
        "ffn1_w1": first(a["L1_ffn_W1"]), "ffn1_w2": second(a["L1_ffn_W2"], P),
        "ffn1_b1": hidden(a["L1_ffn_b1"], P), "ffn1_b2": a["L1_ffn_b2"],
        "ffn2_w1": first(a["L2_ffn_W1"]), "ffn2_w2": second(a["L2_ffn_W2"], P),
        "ffn3_w1": first(np.concatenate([
            np.concatenate([a["L3_ffn_gWg"], a["L3_ffn_gWu"]], axis=2),
            np.stack([np.concatenate([a["L3_ffn_sWg"][:, h], a["L3_ffn_sWu"][:, h]], axis=1)
                      for h in (slice(0, wide), slice(wide, D))])])),
        "ffn3_w2": second(np.concatenate([a["L3_ffn_gWd"], a["L3_ffn_sWd"].reshape(2, wide, D)]), wide),
        "ffn3_b1": hidden(np.concatenate([
            np.concatenate([a["L3_ffn_gbg"], a["L3_ffn_gbu"]], axis=1),
            np.concatenate([a["L3_ffn_sbg"].reshape(2, wide), a["L3_ffn_sbu"].reshape(2, wide)], axis=1)]), wide),
        "ffn3_b2": np.concatenate([a["L3_ffn_gbd"], a["L3_ffn_sbd"].reshape(1, D), np.zeros((1, D), np.float32)]),
    })
    return {k: np.ascontiguousarray(v) for k, v in t.items()}


def kernel(**inputs):
    import concourse.bacc as bacc
    from concourse.bass_utils import run_bass_kernel_spmd

    arrays = layout({k: np.asarray(v) for k, v in inputs.items()})
    nc = bacc.Bacc("TRN2", target_bir_lowering=False, num_devices=1)
    ins = {k: nc.dram_tensor(f"in_{k}", v.shape, F32, kind="ExternalInput").ap() for k, v in arrays.items()}
    out = nc.dram_tensor("tokens", (TOKENS, D), F32, kind="ExternalOutput").ap()
    patch_dram = nc.dram_tensor("patch_sums", (CHANNELS, TOKENS), F32, kind="Internal").ap()
    tower(nc, ins, out, patch_dram)
    result = run_bass_kernel_spmd(nc, [{f"in_{k}": v for k, v in arrays.items()}], core_ids=[0])
    return result.results[0]["tokens"].reshape(IMAGES, SEQ, D)
```

```python
from contextlib import ExitStack

import concourse.bass as bass
import concourse.mybir as mybir
import numpy as np

F32, U32, I32 = mybir.dt.float32, mybir.dt.uint32, mybir.dt.int32
ALU = mybir.AluOpType
ACT = mybir.ActivationFunctionType
AX = mybir.AxisListType.X
ds = bass.ds

IMAGES, CHANNELS, SIDE, PATCH = 64, 3, 96, 16
GRID = SIDE // PATCH
SEQ = GRID * GRID
TOKENS = IMAGES * SEQ
D = 192
FP = 96
FC = D // FP
P = 128
TILES = TOKENS // P
HEADS, HEAD = 12, 16
PAIRS = IMAGES // 2
PAIR = 2 * SEQ
HPC = FP // HEAD
GROUP = 3
GROUPS = HEADS // GROUP
SECOND = 64
CHUNK = 384
CHUNKS = TOKENS // CHUNK
NEG = -1e30
EPS = 1e-5


RING = 6
FILL = 4


def most_places(experts, top):
    tiles = top * TILES + experts - 1
    return tiles + tiles % 2


MOST_PLACES = most_places(16, 4)


LEAD = 4


class Signal:

    def __init__(self, sem, lead=LEAD):
        self.sem, self.base = sem, lead

    def at(self, n):
        return self.base + n

    def close(self, n):
        self.base += n


def link(eng, done, ins, n):
    ins.then_inc(done.sem, 1)
    eng.wait_ge(done.sem, done.at(n))


def tile(buf, t, width=D):
    return buf[:, ds(t * width, width)]


def token_phase(nc, m, s, ins):
    rows = IMAGES * GRID
    parts = rows // P
    width = CHANNELS * SIDE
    with (
        nc.sbuf_tensor("image", [P, parts, CHANNELS, PATCH * SIDE], F32) as image,
        nc.sbuf_tensor("column_sum", [P, parts, width], F32) as column_sum,
        nc.sbuf_tensor("patch_sum", [P, parts, CHANNELS * GRID], F32) as patch_sum,
        nc.sbuf_tensor("patchT", [CHANNELS, TOKENS], F32) as patchT,
        nc.sbuf_tensor("patch_tile", [CHANNELS, 2, P], F32) as patch_tile,
        nc.Block(no_gpsimd_drain=True) as block,
    ):
        x = ins["x"]

        @block.sync
        def _(sp):
            for i in range(parts):
                for c in range(CHANNELS):
                    sp.dma_start(image[:, i, c, :], x[c, i * P:(i + 1) * P, :]).then_inc(s.image[i].sem, 16)
            sp.dma_start(m.attention_w[1][:, :, 0:4 * D], ins["rwkv"]).then_inc(s.attention_w.sem, 16)
            load_attention(sp, m, s, ins, 0)
            sp.wait_ge(s.patch.sem, s.patch.at(parts))
            for c in range(CHANNELS):
                sp.dma_start(
                    m.patch_dram[c:c + 1, :].rearrange("c (i r g) -> r (c i) g", i=parts, g=GRID),
                    patch_sum[:, :, c * GRID:(c + 1) * GRID],
                ).then_inc(s.patch_store.sem, 16)
            sp.wait_ge(s.patch_store.sem, s.patch_store.at(16 * CHANNELS))
            sp.dma_start(patchT[:, :], m.patch_dram[:, :]).then_inc(s.patch_load.sem, 16)

        @block.vector
        def _(vec):
            n = 0
            for i in range(parts):
                vec.wait_ge(s.image[i].sem, s.image[i].at(16 * CHANNELS))
                acc = column_sum[:, i, :].rearrange("p (c w) -> p c w", c=CHANNELS)
                for r in range(PATCH):
                    line = image[:, i, :, r * SIDE:(r + 1) * SIDE]
                    if r == 0:
                        last = vec.tensor_scalar(acc, line, m.W1[:, 0:1], m.b1[:, 0:1], ALU.mult, ALU.add)
                    else:
                        last = vec.scalar_tensor_tensor(acc, line, m.W1[:, r:r + 1], acc, ALU.mult, ALU.add)
                    n += 1
                    link(vec, s.vec, last, n)
                each = column_sum[:, i, :].rearrange("p (g q) -> p g q", q=PATCH)
                n += 1
                link(vec, s.vec, vec.tensor_tensor(
                    each, each, m.W2[:, :].unsqueeze(1).to_broadcast([P, CHANNELS * GRID, PATCH]), ALU.mult), n)
                n += 1
                link(vec, s.vec, vec.tensor_reduce(patch_sum[:, i, :], each, AX, ALU.add), n)
                vec.tensor_scalar(patch_sum[:, i, :], patch_sum[:, i, :], m.b2[:, 0:1], None,
                                  ALU.add).then_inc(s.patch.sem, 1)
            with vec.Fori(0, TILES - 1, 2) as t:
                for p in range(2):
                    vec.wait_ge(s.mm.sem, s.mm.at(t + p + 1))
                    vec.tensor_tensor(tile(m.h, t + p), m.ps[p][:, 0:D], m.b3[:, :], ALU.add).then_inc(s.out.sem, 1)
            m.vec_links = n

        @block.scalar
        def _(act):
            act.wait_ge(s.patch_load.sem, s.patch_load.at(16))
            with act.Fori(0, TILES - 1, 2) as t:
                for p in range(2):
                    act.wait_ge(s.mm.sem, s.mm.at(t + p - 1))
                    act.activation(patch_tile[:, p, :], patchT[:, ds((t + p) * P, P)], ACT.Copy).then_inc(s.stage.sem, 1)

        @block.tensor
        def _(pe):
            with pe.Fori(0, TILES - 1, 2) as t:
                for p in range(2):
                    pe.wait_ge(s.stage.sem, s.stage.at(t + p + 1))
                    pe.wait_ge(s.out.sem, s.out.at(t + p - 1))
                    pe.matmul(m.ps[p][:, 0:D], patch_tile[:, p, :], m.W3[:, :], start=True, stop=True).then_inc(s.mm.sem, 1)
    s.vec.close(m.vec_links)
    for signal, n in ((s.mm, TILES), (s.stage, TILES), (s.out, TILES)):
        signal.close(n)


def feature_phase(nc, m, s, src, norm=True, keep=None, scale=None, shift=None, router=None):
    experts = router[2] if router else 0
    with nc.Block(no_gpsimd_drain=True) as block:

        @block.vector
        def _(vec):
            if norm:
                with vec.Fori(0, TILES) as t:
                    vec.bn_stats(tile(m.stats, t, 6), tile(src, t)).then_inc(s.stats.sem, 1)
                vec.wait_ge(s.stats.sem, s.stats.at(TILES))
                half = m.stats[:, :].rearrange("p (t k) -> p t k", k=6)
                mean, other, rstd = m.mean[:, :], m.other[:, :], m.rstd[:, :]
                link(vec, s.vec, vec.tensor_tensor(mean, half[:, :, 1], half[:, :, 4], ALU.add), 1)
                link(vec, s.vec, vec.tensor_tensor(other, half[:, :, 1], half[:, :, 4], ALU.subtract), 2)
                link(vec, s.vec, vec.tensor_scalar(mean, mean, 0.5, None, ALU.mult), 3)
                link(vec, s.vec, vec.scalar_tensor_tensor(other, other, 0.25, other, ALU.mult, ALU.mult), 4)
                link(vec, s.vec, vec.tensor_tensor(rstd, half[:, :, 2], half[:, :, 5], ALU.add), 5)
                link(vec, s.vec, vec.scalar_tensor_tensor(rstd, rstd, 1.0 / D, other, ALU.mult, ALU.add), 6)
                vec.tensor_scalar(rstd, rstd, EPS, None, ALU.add).then_inc(s.var.sem, 1)
                vec.wait_ge(s.std.sem, s.std.at(1))
                link(vec, s.vec, vec.reciprocal(rstd, rstd), 7)

            def logits(t, p):
                vec.wait_ge(s.route.sem, s.route.at(t + 1))
                out = m.logits[:, ds(t * experts, experts)]
                if router[1] is None:
                    vec.tensor_copy(out, m.ps[2 + p][:, 0:experts]).then_inc(s.logit.sem, 1)
                else:
                    vec.tensor_tensor(out, m.ps[2 + p][:, 0:experts], router[1], ALU.add).then_inc(s.logit.sem, 1)

            with vec.Fori(0, TILES - 1, 2) as t:
                for p in range(2):
                    vec.wait_ge(s.turned.sem, s.turned.at(t + p - 1))
                    x = m.x_tile[:, p, :]
                    if norm:
                        vec.tensor_scalar(x, tile(src, t + p), m.mean[:, ds(t + p, 1)], m.rstd[:, ds(t + p, 1)],
                                          ALU.subtract, ALU.mult).then_inc(s.x.sem, 1)
                    else:
                        vec.tensor_copy(x, tile(src, t + p)).then_inc(s.x.sem, 1)
                    if keep is not None:
                        vec.wait_ge(s.x.sem, s.x.at(t + p + 1))
                        vec.tensor_copy(tile(keep, t + p), x).then_inc(s.kept.sem, 1)
                if router:
                    for p in range(2):
                        logits(t + p, p)

        @block.scalar
        def _(act):
            if norm:
                act.wait_ge(s.var.sem, s.var.at(1))
                act.activation(m.rstd[:, :], m.rstd[:, :], ACT.Sqrt).then_inc(s.std.sem, 1)
            with act.Fori(0, TILES - 1, 2) as t:
                for p in range(2):
                    act.wait_ge(s.turned.sem, s.turned.at(t + p + 1))
                    if router:
                        act.wait_ge(s.route.sem, s.route.at(t + p - 1))
                    bank = m.ps[p][0:FP, 0:FC * P].rearrange("f (c k) -> f c k", c=FC)
                    for c in range(FC):
                        outs = [m.xT[:, c, ds((t + p) * P, P)]]
                        if router:
                            outs.insert(0, m.xs[:, p, c, :])
                        for out in outs:
                            if scale is None:
                                last = act.activation(out, bank[:, c, :], ACT.Copy)
                            else:
                                last = act.activation(out, bank[:, c, :], ACT.Identity,
                                                      bias=shift[:, c:c + 1], scale=scale[:, c:c + 1])
                    last.then_inc(s.xT.sem, 1)

        @block.tensor
        def _(pe):
            def route(t, p):
                pe.wait_ge(s.xT.sem, s.xT.at(t + 1))
                pe.wait_ge(s.logit.sem, s.logit.at(t - 1))
                for c in range(FC):
                    last = pe.matmul(m.ps[2 + p][:, 0:experts], m.xs[:, p, c, :], router[0][:, c, :],
                                     start=(c == 0), stop=(c == FC - 1))
                last.then_inc(s.route.sem, 1)

            with pe.Fori(0, TILES - 1, 2) as t:
                for p in range(2):
                    pe.wait_ge(s.x.sem, s.x.at(t + p + 1))
                    pe.wait_ge(s.xT.sem, s.xT.at(t + p - 1))
                    for c in range(FC):
                        last = pe.matmul(m.ps[p][0:FP, c * P:(c + 1) * P], m.x_tile[:, p, c * FP:(c + 1) * FP],
                                         m.ident[:, :], start=True, stop=True, is_transpose=True)
                    last.then_inc(s.turned.sem, 1)
                if router:
                    for p in range(2):
                        route(t + p, p)
    closing = [(s.x, TILES), (s.turned, TILES), (s.xT, TILES)]
    if norm:
        closing += [(s.vec, 7), (s.stats, TILES), (s.var, 1), (s.std, 1)]
    if keep is not None:
        closing += [(s.kept, TILES)]
    if router:
        closing += [(s.route, TILES), (s.logit, TILES)]
    for signal, n in closing:
        signal.close(n)


def project_phase(nc, m, s, weights, dst, bias=None, ready=None):
    with nc.Block(no_gpsimd_drain=True) as block:

        @block.scalar
        def _(act):
            with act.Fori(0, TILES - 1, 2) as t:
                for p in range(2):
                    act.wait_ge(s.mm.sem, s.mm.at(t + p - 1))
                    act.activation(m.xs[:, p, :, :], m.xT[:, :, ds((t + p) * P, P)], ACT.Copy).then_inc(s.stage.sem, 1)

        @block.tensor
        def _(pe):
            with pe.Fori(0, TILES - 1, 2) as t:
                for p in range(2):
                    pe.wait_ge(s.stage.sem, s.stage.at(t + p + 1))
                    pe.wait_ge(s.out.sem, s.out.at(t + p - 1))
                    if bias is not None:
                        pe.matmul(m.ps[p][:, 0:D], m.ones[0:1, 0:P], bias, start=True, stop=False)
                    for c in range(FC):
                        last = pe.matmul(m.ps[p][:, 0:D], m.xs[:, p, c, :], weights[:, c, :],
                                         start=(c == 0 and bias is None), stop=(c == FC - 1))
                    last.then_inc(s.mm.sem, 1)

        @block.vector
        def _(vec):
            with vec.Fori(0, TILES - 1, 2) as t:
                for p in range(2):
                    vec.wait_ge(s.mm.sem, s.mm.at(t + p + 1))
                    vec.tensor_tensor(tile(dst, t + p), m.ps[p][:, 0:D], tile(dst, t + p),
                                      ALU.add).then_inc(s.out.sem, 1)
    for signal, n in ((s.mm, TILES), (s.stage, TILES), (s.out, TILES)):
        signal.close(n)


def store_phase(nc, s, src, out):
    with nc.Block(no_gpsimd_drain=True) as block:

        @block.sync
        def _(sp):
            sp.dma_start(out.rearrange("(t p) d -> p t d", p=P),
                         src[:, :].rearrange("p (t d) -> p t d", d=D)).then_inc(s.store.sem, 16)
            sp.wait_ge(s.store.sem, 16)


def add_phase(nc, m, s, dst, src):
    with nc.Block(no_gpsimd_drain=True) as block:

        @block.vector
        def _(vec):
            vec.tensor_tensor(dst[:, :], dst[:, :], src[:, :], ALU.add).then_inc(s.out.sem, 1)
            vec.wait_ge(s.out.sem, s.out.at(1))
    s.out.close(1)


def load_attention(sp, m, s, ins, layer):
    n = ins[f"attention{layer}"].shape[2]
    sp.dma_start(m.attention_w[layer % 2][:, :, 0:n], ins[f"attention{layer}"]).then_inc(s.attention_w.sem, 16)


def attention_phase(nc, m, s, layer, kind, bias=None, prefetch=None):
    w = m.attention_w[layer % 2]
    Wq, Wk, Wv = (w[:, :, j * D:(j + 1) * D] for j in range(3))
    Wq_turned, Wk_turned = (w[:, :, j * D:(j + 1) * D] for j in (4, 5))
    rotary = kind == "erf"
    qbias, kbias, vbias = bias or (m.zero_bias,) * 3
    psQ, psK, psV, psS, psT, psC, psX, psR = m.ps
    spread = [FP, HPC, PAIR]
    read = s.scored if kind == "causal" else s.shifted
    lanes = HPC * SEQ

    def both(bank):
        return bank[0:FP, 0:FC * PAIR].rearrange("f (c k) -> f c k", c=FC)

    with (
        nc.sbuf_tensor(f"x_pair_{layer}", [FP, 2, FC, PAIR], F32) as x_pair,
        nc.sbuf_tensor(f"x_tripled_{layer}", [FP, 2, FC, 2, GROUP * SEQ], F32) as x_tripled,
        nc.sbuf_tensor(f"qT_{layer}", [FP, 2, FC, SECOND + SEQ], F32) as qT,
        nc.sbuf_tensor(f"k_rot_{layer}", [FP, 2, FC, PAIR], F32) as k_rot,
        nc.sbuf_tensor(f"rot_tmp_{layer}", [FP, 4, FC, PAIR], F32) as rot_tmp,
        nc.sbuf_tensor(f"k_spread_{layer}", [FP, 2, FC, HPC, PAIR], F32) as k_spread,
        nc.sbuf_tensor(f"v_spread_{layer}", [GROUP * SEQ, 2, 2, D], F32) as v_spread,
        nc.sbuf_tensor(f"weight_{layer}", [P, 2, HEADS * SEQ], F32) as weight,
        nc.sbuf_tensor(f"erf_tmp_{layer}", [P, 2, HEADS * SEQ], F32) as erf_tmp,
        nc.sbuf_tensor(f"inverse_{layer}", [P, 2, HEADS * SEQ if kind == "erf" else 1], F32) as inverse,
        nc.sbuf_tensor(f"weightT_{layer}", [GROUP * SEQ, 2, GROUPS, P], F32) as weightT,
        nc.sbuf_tensor(f"row_max_{layer}", [P, 2, HEADS], F32) as row_max,
        nc.sbuf_tensor(f"row_sum_{layer}", [P, 2, HEADS], F32) as row_sum,
        nc.sbuf_tensor(f"context_{layer}", [P, 2, D], F32) as context,
        nc.Block(no_gpsimd_drain=True) as block,
    ):
        FIRST, LAST = 4, 30

        def turns(eng, turn):
            for i in range(FIRST):
                turn(i, i % 2)
            with eng.Fori(FIRST, LAST - 1, 2) as i:
                for p in range(2):
                    turn(i + p, p)
            for i in range(LAST, PAIRS + 3):
                turn(i, i % 2)

        def has(i):
            return not isinstance(i, int) or 0 <= i < PAIRS

        @block.tensor
        def _(pe):
            def scores(i, p):
                pe.wait_ge(s.q.sem, s.q.at(i + 1))
                pe.wait_ge(s.k.sem, s.k.at(i + 1))
                pe.wait_ge(read.sem, read.at(i))
                for c in range(FC):
                    for b in range(2):
                        last = pe.matmul(psS[b * SECOND:b * SECOND + SECOND, c * lanes:(c + 1) * lanes],
                                         qT[:, p, c, b * SEQ:b * SEQ + SECOND],
                                         k_spread[:, p, c, :, b * SEQ:(b + 1) * SEQ], start=True, stop=True)
                last.then_inc(s.scores.sem, 1)

            def turn_weights(i, p):
                pe.wait_ge(s.weight.sem, s.weight.at(i + 1))
                pe.wait_ge(s.weightT.sem, s.weightT.at(i))
                for g in range(GROUPS):
                    n = GROUP * SEQ
                    last = pe.matmul(psT[0:n, g * P:(g + 1) * P], weight[:, p, g * n:(g + 1) * n], m.ident[:, :],
                                     start=True, stop=True, is_transpose=True)
                last.then_inc(s.turned.sem, 1)

            def projections(i, p):
                pe.wait_ge(s.stage.sem, s.stage.at(i + 1))
                pe.wait_ge(s.q.sem, s.q.at(i))
                pe.wait_ge(s.k.sem, s.k.at(i))
                pe.wait_ge(s.v.sem, s.v.at(i))
                pairs = [(psQ, Wq), (psK, Wk)] + [(psX, Wq_turned), (psR, Wk_turned)] * rotary
                for bank, weights in pairs:
                    if bank is psX:
                        pe.wait_ge(s.context_out.sem, s.context_out.at(i - 3))
                    for out in range(FC):
                        for c in range(FC):
                            pe.matmul(both(bank)[:, out, :], weights[:, c, out * FP:(out + 1) * FP],
                                      x_pair[:, p, c, :], start=(c == 0), stop=(c == FC - 1))
                pe.wait_ge(s.tripled.sem, s.tripled.at(i + 1))
                for b in range(2):
                    for c in range(FC):
                        last = pe.matmul(psV[0:GROUP * SEQ, b * D:(b + 1) * D], x_tripled[:, p, c, b, :], Wv[:, c, :],
                                         start=(c == 0), stop=(c == FC - 1))
                last.then_inc(s.projected.sem, 1)

            def weigh(i, p):
                pe.wait_ge(s.weightT.sem, s.weightT.at(i + 1))
                pe.wait_ge(s.v.sem, s.v.at(i + 1))
                pe.wait_ge(s.context.sem, s.context.at(i))
                for g in range(GROUPS):
                    for b in range(2):
                        cols = slice(g * GROUP * HEAD, (g + 1) * GROUP * HEAD)
                        last = pe.matmul(psC[b * SECOND:b * SECOND + SECOND, cols],
                                         weightT[:, p, g, b * SECOND:b * SECOND + SECOND],
                                         v_spread[:, p, b, cols], start=True, stop=True)
                last.then_inc(s.weighed.sem, 1)

            def turn_context(i, p):
                pe.wait_ge(s.context.sem, s.context.at(i + 1))
                pe.wait_ge(s.context_out.sem, s.context_out.at(i))
                if rotary:
                    pe.wait_ge(s.q.sem, s.q.at(min(i + 4, PAIRS) if isinstance(i, int) else i + 4))
                for c in range(FC):
                    last = pe.matmul(psX[0:FP, c * P:(c + 1) * P], context[:, p, c * FP:(c + 1) * FP], m.ident[:, :],
                                     start=True, stop=True, is_transpose=True)
                last.then_inc(s.context_turned.sem, 1)

            def turn(i, p):
                if has(i - 1):
                    scores(i - 1, 1 - p)
                if not rotary and has(i - 2):
                    turn_weights(i - 2, p)
                if has(i):
                    projections(i, p)
                if rotary and has(i - 2):
                    turn_weights(i - 2, p)
                if has(i - 2):
                    weigh(i - 2, p)
                if has(i - 3):
                    turn_context(i - 3, 1 - p)

            pe.wait_ge(s.attention_w.sem, s.attention_w.at(16 * (layer + 2)))
            turns(pe, turn)

        @block.gpsimd
        def _(pool):
            def triple(i, p):
                pool.wait_ge(s.projected.sem, s.projected.at(i - 1))
                for c in range(FC):
                    for b in range(2):
                        last = pool.tensor_copy(
                            x_tripled[:, p, c, b, :].rearrange("f (r k) -> f r k", r=GROUP),
                            m.xT[:, c, ds(i * PAIR + b * SEQ, SEQ)].unsqueeze(1).to_broadcast([FP, GROUP, SEQ]))
                last.then_inc(s.tripled.sem, 1)

            def weights(i, p):
                x = weight[:, p, :].rearrange("q (h k) -> q h k", h=HEADS)
                pool.wait_ge(s.gelu.sem, s.gelu.at(i + 1))
                pool.wait_ge(s.inverted.sem, s.inverted.at(i + 1))
                link(pool, s.soft, pool.tensor_tensor(weight[:, p, :], erf_tmp[:, p, :], inverse[:, p, :], ALU.mult), i + 1)
                pool.tensor_tensor(x, x, m.causal_two[:, :].unsqueeze(1).to_broadcast([P, HEADS, SEQ]),
                                   ALU.mult).then_inc(s.weight.sem, 1)

            def turn(i, p):
                if has(i):
                    triple(i, p)
                if rotary and has(i - 1):
                    weights(i - 1, 1 - p)

            turns(pool, turn)

        @block.scalar
        def _(act):
            def stage(i, p):
                act.wait_ge(s.projected.sem, s.projected.at(i - 1))
                act.activation(x_pair[:, p, :, :], m.xT[:, :, ds(i * PAIR, PAIR)], ACT.Copy).then_inc(s.stage.sem, 1)

            def queries(i, p):
                act.wait_ge(s.projected.sem, s.projected.at(i + 1))
                act.wait_ge(s.scores.sem, s.scores.at(i - 1))
                for c in range(FC):
                    last = act.activation(qT[:, p, c, 0:PAIR], both(psQ)[:, c, :], ACT.Identity,
                                          bias=qbias[:, c:c + 1])
                last.then_inc(s.q.sem, 1)

            def exponentials(i, p):
                act.wait_ge(s.shifted.sem, s.shifted.at(i + 1))
                if kind == "erf":
                    act.activation(erf_tmp[:, p, :], weight[:, p, :], ACT.Gelu).then_inc(s.gelu.sem, 1)
                else:
                    act.activation(weight[:, p, :], weight[:, p, :], ACT.Exp, scale=0.25).then_inc(s.weight.sem, 1)

            def weights_out(i, p):
                act.wait_ge(s.turned.sem, s.turned.at(i + 1))
                act.wait_ge(s.weighed.sem, s.weighed.at(i - 1))
                act.activation(weightT[:, p, :, :], psT[0:GROUP * SEQ, 0:GROUPS * P].rearrange("k (g q) -> k g q", g=GROUPS),
                               ACT.Copy).then_inc(s.weightT.sem, 1)

            def context_out(i, p):
                act.wait_ge(s.context_turned.sem, s.context_turned.at(i + 1))
                for c in range(FC):
                    rows = psX[0:FP, c * P:(c + 1) * P].rearrange("f (b k) -> f b k", b=2)[:, :, 0:SEQ]
                    last = act.activation(m.xT[:, c, ds(i * PAIR, PAIR)].rearrange("f (b k) -> f b k", b=2), rows,
                                          ACT.Identity, bias=vbias[:, c:c + 1])
                last.then_inc(s.context_out.sem, 1)

            def turn(i, p):
                if has(i - 2):
                    weights_out(i - 2, p)
                if has(i - 1):
                    exponentials(i - 1, 1 - p)
                if has(i + 1):
                    stage(i + 1, 1 - p)
                if has(i) and not rotary:
                    queries(i, p)
                if has(i - 3):
                    context_out(i - 3, 1 - p)

            stage(0, 0)
            turns(act, turn)

        @block.vector
        def _(vec):
            vec.memset(qT[:, :, :, PAIR:SECOND + SEQ], 0.0).then_inc(s.vec.sem, 1)
            count = 0 if kind == "plain" else {"causal": 1, "erf": 4}[kind]

            def spread_keys(i, p):
                vec.wait_ge(s.projected.sem, s.projected.at(i + 1))
                vec.wait_ge(s.scores.sem, s.scores.at(i - 1))
                for c in range(FC):
                    key = both(psK)[:, c, :] if not rotary else k_rot[:, p, c, :]
                    last = vec.scalar_tensor_tensor(
                        k_spread[:, p, c, :, :], key.unsqueeze(1).to_broadcast(spread), kbias[:, c:c + 1],
                        m.head_mask[:, :].unsqueeze(2).to_broadcast(spread), ALU.add, ALU.mult)
                last.then_inc(s.k.sem, 1)

            def rotate(i, p):
                vec.wait_ge(s.projected.sem, s.projected.at(i + 1))
                vec.wait_ge(s.scores.sem, s.scores.at(i - 1))
                shape = [FP, FC * 2, SEQ]
                cos = m.cos[:, :].unsqueeze(1).to_broadcast(shape)
                sin = m.sin[:, :].unsqueeze(1).to_broadcast(shape)

                def flat(a):
                    return a.rearrange("f (x k) -> f x k", k=SEQ)
                t = [rot_tmp[:, j, :, :].rearrange("f c (b k) -> f (c b) k", b=2) for j in range(4)]
                vec.tensor_tensor(t[0], flat(psQ[0:FP, 0:FC * PAIR]), cos, ALU.mult)
                vec.tensor_tensor(t[1], flat(psX[0:FP, 0:FC * PAIR]), sin, ALU.mult)
                vec.tensor_tensor(t[2], flat(psK[0:FP, 0:FC * PAIR]), cos, ALU.mult)
                vec.tensor_tensor(t[3], flat(psR[0:FP, 0:FC * PAIR]), sin, ALU.mult).then_inc(s.rot.sem, 1)
                vec.wait_ge(s.rot.sem, s.rot.at(2 * i + 1))
                vec.tensor_tensor(qT[:, p, :, 0:PAIR], rot_tmp[:, 0, :, :], rot_tmp[:, 1, :, :], ALU.add).then_inc(s.q.sem, 1)
                vec.tensor_tensor(k_rot[:, p, :, :], rot_tmp[:, 2, :, :], rot_tmp[:, 3, :, :], ALU.add).then_inc(s.rot.sem, 1)
                vec.wait_ge(s.rot.sem, s.rot.at(2 * i + 2))

            def spread_values(i, p):
                vec.wait_ge(s.weighed.sem, s.weighed.at(i - 1))
                shape = [GROUP * SEQ, 2 * GROUPS, GROUP * HEAD]
                vec.tensor_tensor(v_spread[:, p, :, :].rearrange("k b (g n) -> k (b g) n", g=GROUPS),
                                  psV[0:GROUP * SEQ, 0:2 * D].rearrange("k (x n) -> k x n", n=GROUP * HEAD),
                                  m.value_mask[:, :].unsqueeze(1).to_broadcast(shape), ALU.mult).then_inc(s.v.sem, 1)

            by_head = [P, HEADS, SEQ]

            def shift(i, p):
                vec.wait_ge(s.scores.sem, s.scores.at(i + 1))
                vec.wait_ge(s.turned.sem, s.turned.at(i - 1))
                x = weight[:, p, :].rearrange("q (h k) -> q h k", h=HEADS)
                ps = psS[:, 0:HEADS * SEQ].rearrange("q (h k) -> q h k", h=HEADS)
                mask = m.causal[:, :].unsqueeze(1).to_broadcast(by_head)
                if kind == "erf":
                    link(vec, s.scored, vec.tensor_scalar(erf_tmp[:, p, :], psS[:, 0:HEADS * SEQ], 0.0, 1e-20,
                                                          ALU.is_equal, ALU.mult), i + 1)
                    vec.scalar_tensor_tensor(weight[:, p, :], psS[:, 0:HEADS * SEQ], 0.25 * 2.0 ** 0.5,
                                             erf_tmp[:, p, :], ALU.mult, ALU.add).then_inc(s.shifted.sem, 1)
                    return
                src = ps
                if kind == "causal":
                    vec.tensor_tensor(x, ps, mask, ALU.add).then_inc(s.scored.sem, 1)
                    vec.wait_ge(s.scored.sem, s.scored.at(i + 1))
                    src = x
                link(vec, s.soft, vec.tensor_reduce(row_max[:, p, :], src, AX, ALU.max), 2 * i + 1)
                last = vec.tensor_tensor(x, src, row_max[:, p, :].unsqueeze(2).to_broadcast(by_head), ALU.subtract)
                last.then_inc(s.shifted.sem, 1)

            def invert(i, p):
                vec.wait_ge(s.shifted.sem, s.shifted.at(i + 1))
                vec.wait_ge(s.weight.sem, s.weight.at(i - 1))
                vec.reciprocal(inverse[:, p, :], weight[:, p, :]).then_inc(s.inverted.sem, 1)

            def total(i, p):
                x = weight[:, p, :].rearrange("q (h k) -> q h k", h=HEADS)
                vec.wait_ge(s.weight.sem, s.weight.at(i + 1))
                if kind == "erf":
                    link(vec, s.sums, vec.tensor_reduce(row_sum[:, p, :], x, AX, ALU.add), 2 * i + 1)
                    link(vec, s.sums, vec.tensor_scalar(row_sum[:, p, :], row_sum[:, p, :], 1e-6, None, ALU.max),
                         2 * i + 2)
                else:
                    link(vec, s.soft, vec.tensor_reduce(row_sum[:, p, :], x, AX, ALU.add), 2 * i + 2)
                vec.reciprocal(row_sum[:, p, :], row_sum[:, p, :]).then_inc(s.inverse.sem, 1)

            def normalise(i, p):
                vec.wait_ge(s.inverse.sem, s.inverse.at(i + 1))
                vec.wait_ge(s.weighed.sem, s.weighed.at(i + 1))
                vec.wait_ge(s.context_turned.sem, s.context_turned.at(i - 1))
                shape = [P, HEADS, HEAD]
                vec.tensor_tensor(context[:, p, :].rearrange("q (h d) -> q h d", h=HEADS),
                                  psC[:, 0:D].rearrange("q (h d) -> q h d", h=HEADS),
                                  row_sum[:, p, :].unsqueeze(2).to_broadcast(shape), ALU.mult).then_inc(s.context.sem, 1)

            def turn(i, p):
                if has(i - 1):
                    shift(i - 1, 1 - p)
                if rotary and has(i - 1):
                    invert(i - 1, 1 - p)
                if has(i):
                    if rotary:
                        rotate(i, p)
                    spread_keys(i, p)
                    spread_values(i, p)
                if rotary and has(i - 2):
                    total(i - 2, p)
                if not rotary and has(i - 1):
                    total(i - 1, 1 - p)
                if has(i - 2):
                    normalise(i - 2, p)

            vec.wait_ge(s.vec.sem, s.vec.at(1))
            turns(vec, turn)

        @block.sync
        def _(sp):
            if prefetch:
                prefetch(sp)
    n = PAIRS
    for signal in (s.q, s.k, s.v, s.tripled, s.scores, s.weight, s.weightT, s.turned, s.stage, s.projected,
                   s.context, s.context_turned, s.context_out, s.weighed, s.shifted, s.inverse):
        signal.close(n)
    if kind != "plain":
        s.scored.close(n)
    s.vec.close(1)
    s.soft.close((1 if kind == "erf" else 2) * n)
    if kind == "erf":
        s.gelu.close(n)
        s.inverted.close(n)
        s.sums.close(2 * n)
        s.rot.close(2 * n)


def rwkv_phase(nc, m, s):
    at_once = 16
    turns = IMAGES // at_once
    n_tok = at_once * SEQ
    width = SEQ + 1
    half = at_once // 2
    w = m.attention_w[1]
    STEPS = 15
    with ExitStack() as ctx:
        def buf(name, shape):
            return ctx.enter_context(nc.sbuf_tensor("rwkv_" + name, shape, F32))

        xpad = buf("xpad", [FP, FC, IMAGES, width])
        mixed = buf("mixed", [FP, 3, FC, at_once, SEQ])
        decay, kp, vp, mx, ea, eb, num, den = (
            buf(x, [FP, FC, at_once, width]) for x in ("decay", "kp", "vp", "mx", "ea", "eb", "num", "den"))
        zeros = buf("zeros", [P, FILL * D])
        er, t1, t2, t3 = (buf(x, [FP, FC, at_once, SEQ]) for x in ("er", "t1", "t2", "t3"))
        block = ctx.enter_context(nc.Block(no_gpsimd_drain=True))

        def rows(b):
            return b[:, :, :, :].rearrange("f c b k -> f (c b) k")

        def now(b):
            return rows(b)[:, :, 1:width]

        def before(b):
            return rows(b)[:, :, 0:SEQ]

        def line(b):
            return b[:, :, :, :].rearrange("f c b k -> f (c b k)")

        @block.sync
        def _(sp):
            sp.wait_ge(s.cleared.sem, s.cleared.at(1))
            with sp.Fori(0, MOST_PLACES // FILL) as i:
                sp.dma_start(m.rows[ds(i * (FILL * P), FILL * P), :].rearrange("(k p) d -> p k d", p=P),
                             zeros[:, :].rearrange("p (k d) -> p k d", d=D)).then_inc(s.filled.sem, 16)
            sp.wait_ge(s.filled.sem, 16 * (MOST_PLACES // FILL))

        @block.vector
        def _(vec):
            vec.memset(zeros[:, :], 0.0).then_inc(s.cleared.sem, 1)
            vec.memset(xpad[:, :, :, 0:1], 0.0)
            for b, value in ((kp, -1e38), (vp, 0.0), (ea, 0.0), (eb, 0.0), (decay, -2e38)):
                vec.memset(b[:, :, :, 0:1], value)
            vec.wait_ge(s.exps.sem, s.exps.at(1))
            for c in range(FC):
                vec.tensor_scalar(decay[:, c, :, 1:width], m.decay[:, c:c + 1].unsqueeze(2).to_broadcast([FP, at_once, SEQ]),
                                  -1.0, None, ALU.mult)
                vec.tensor_copy(xpad[:, c, :, 1:width], m.xT[:, c, :].rearrange("f (b k) -> f b k", k=SEQ))
            link(vec, s.vec, vec.tensor_scalar(m.unmix[:, :], m.mix[:, :], -1.0, 1.0, ALU.mult, ALU.add), 1)
            with vec.Fori(0, turns) as g:
                def step(n, ins):
                    link(vec, s.vec, ins, g * STEPS + (n + 1))

                vec.wait_ge(s.mm.sem, s.mm.at(3 * g))
                for j in range(3):
                    for c in range(FC):
                        last = vec.tensor_scalar(mixed[:, j, c, :, :], xpad[:, c, ds(g * at_once, at_once), 1:width],
                                                 m.mix[:, j * FC + c:j * FC + c + 1], None, ALU.mult)
                step(1, last)
                for j in range(3):
                    for c in range(FC):
                        last = vec.scalar_tensor_tensor(
                            mixed[:, j, c, :, :], xpad[:, c, ds(g * at_once, at_once), 0:SEQ],
                            m.unmix[:, j * FC + c:j * FC + c + 1], mixed[:, j, c, :, :], ALU.mult, ALU.add)
                last.then_inc(s.stage.sem, 1)
                vec.wait_ge(s.k.sem, s.k.at(g + 1))
                step(2, vec.tensor_tensor_scan(line(mx), line(decay), line(kp), 0.0, ALU.add, ALU.max))
                step(3, vec.tensor_tensor(now(ea), before(mx), now(decay), ALU.add))
                vec.tensor_tensor(now(ea), now(ea), now(mx), ALU.subtract)
                vec.tensor_tensor(now(eb), now(kp), now(mx), ALU.subtract).then_inc(s.shifted.sem, 1)
                for c in range(FC):
                    last = vec.tensor_scalar(t1[:, c, :, :], kp[:, c, :, 1:width], m.first[:, c:c + 1], None, ALU.add)
                step(4, last)
                step(5, vec.tensor_tensor(rows(t2), before(mx), rows(t1), ALU.max))
                vec.tensor_tensor(rows(t1), rows(t1), rows(t2), ALU.subtract)
                vec.tensor_tensor(rows(t2), before(mx), rows(t2), ALU.subtract).then_inc(s.scored.sem, 1)
                vec.wait_ge(s.exps.sem, s.exps.at(2 * g + 2))
                step(6, vec.tensor_tensor_scan(line(den), line(ea), line(eb), 0.0, ALU.mult, ALU.add))
                step(7, vec.tensor_tensor(now(eb), now(eb), now(vp), ALU.mult))
                step(8, vec.tensor_tensor_scan(line(num), line(ea), line(eb), 0.0, ALU.mult, ALU.add))
                vec.wait_ge(s.exps.sem, s.exps.at(2 * g + 3))
                step(9, vec.tensor_tensor(rows(t3), rows(t2), before(num), ALU.mult))
                step(10, vec.tensor_tensor(rows(t2), rows(t2), before(den), ALU.mult))
                step(11, vec.tensor_tensor(rows(t2), rows(t2), rows(t1), ALU.add))
                step(12, vec.tensor_tensor(rows(t1), rows(t1), now(vp), ALU.mult))
                step(13, vec.tensor_tensor(rows(t3), rows(t3), rows(t1), ALU.add))
                step(14, vec.scalar_tensor_tensor(rows(t2), rows(er), 1.0, rows(t2), ALU.add, ALU.mult))
                step(15, vec.reciprocal(rows(t2), rows(t2)))
                for c in range(FC):
                    last = vec.tensor_tensor(m.xT[:, c, ds(g * n_tok, n_tok)].rearrange("f (b k) -> f b k", k=SEQ),
                                             t3[:, c, :, :], t2[:, c, :, :], ALU.mult)
                last.then_inc(s.out.sem, 1)

        @block.tensor
        def _(pe):
            pe.wait_ge(s.attention_w.sem, s.attention_w.at(32))
            with pe.Fori(0, turns) as g:
                pe.wait_ge(s.stage.sem, s.stage.at(g + 1))
                for j in range(3):
                    if j == 0:
                        pe.wait_ge(s.r.sem, s.r.at(g))
                    elif j == 1:
                        pe.wait_ge(s.k.sem, s.k.at(g))
                    else:
                        pe.wait_ge(s.key_out.sem, s.key_out.at(g + 1))
                    for out in range(FC):
                        for b in range(2):
                            for c in range(FC):
                                last = pe.matmul(
                                    m.ps[4 * (j % 2) + 2 * out + b][0:FP, 0:half * SEQ],
                                    w[:, c, j * D + out * FP:j * D + (out + 1) * FP],
                                    mixed[:, j, c, b * half:(b + 1) * half, :].rearrange("f b k -> f (b k)"),
                                    start=(c == 0), stop=(c == FC - 1))
                    last.then_inc(s.mm.sem, 1)

        @block.scalar
        def _(act):
            act.activation(m.decay[:, :], m.decay[:, :], ACT.Exp).then_inc(s.exps.sem, 1)
            with act.Fori(0, turns) as g:
                def images(j, out, b):
                    return m.ps[4 * (j % 2) + 2 * out + b][0:FP, 0:half * SEQ].rearrange("f (b k) -> f b k", k=SEQ)

                for j, (dst, first) in enumerate(((kp, 1), (vp, 1), (er, 0))):
                    act.wait_ge(s.mm.sem, s.mm.at(3 * g + j + 1))
                    if j == 0:
                        act.wait_ge(s.out.sem, s.out.at(g))
                    for out in range(FC):
                        for b in range(2):
                            to = dst[:, out, b * half:(b + 1) * half, first:first + SEQ]
                            if j < 2:
                                last = act.activation(to, images(j, out, b), ACT.Copy)
                            else:
                                last = act.activation(to, images(j, out, b), ACT.Exp, scale=-1.0)
                    last.then_inc((s.key_out, s.k, s.r)[j].sem, 1)
                act.wait_ge(s.shifted.sem, s.shifted.at(g + 1))
                act.activation(now(ea), now(ea), ACT.Exp)
                act.activation(now(eb), now(eb), ACT.Exp).then_inc(s.exps.sem, 1)
                act.wait_ge(s.scored.sem, s.scored.at(g + 1))
                act.activation(rows(t1), rows(t1), ACT.Exp)
                act.activation(rows(t2), rows(t2), ACT.Exp).then_inc(s.exps.sem, 1)
    s.vec.close(1 + turns * STEPS)
    for signal in (s.stage, s.k, s.shifted, s.scored, s.out, s.r, s.key_out):
        signal.close(turns)
    s.mm.close(3 * turns)
    s.exps.close(2 * turns + 1)
    s.cleared.close(1)


def load_resident(sp, m, s, ins, ffn):
    w1, w2 = ins[ffn.name + "_w1"], ins[ffn.name + "_w2"]
    loads = 0
    for e in range(ffn.experts):
        sp.dma_start(m.expert_w1(ffn, e)[0:FP, :, :], w1[e, 0:FP, :, :]).then_inc(ffn.loaded.sem, 16)
        if w1.shape[1] > FP:
            sp.dma_start(m.expert_w1(ffn, e)[FP:FP + 1, :, :], w1[e, FP:FP + 1, :, :]).then_inc(ffn.loaded.sem, 16)
            loads += 1
        sp.dma_start(m.expert_w2(ffn, e)[0:ffn.block, :, :], w2[e, 0:ffn.block, :, :]).then_inc(ffn.loaded.sem, 16)
        if ffn.bias_row:
            sp.dma_start(m.expert_w2(ffn, e)[ffn.block:ffn.block + 1, :, :],
                         w2[e, ffn.block:ffn.block + 1, :, :]).then_inc(ffn.loaded.sem, 16)
            loads += 1
        loads += 2
    if ffn.out_bias is not None:
        n = ffn.out_bias.shape[1]
        sp.dma_start(ffn.out_bias[:, :], ins[ffn.name + "_b2"].to_broadcast([P, n])).then_inc(ffn.loaded.sem, 16)
        loads += 1
    if ffn.hidden_bias is not None:
        sp.dma_start(ffn.hidden_bias[:, :], ins[ffn.name + "_b1"]).then_inc(ffn.loaded.sem, 16)
        loads += 1
    ffn.loaded.close(16 * loads)


def expert_phase(nc, m, s, ffn, dst, first, experts, prefetch=None):
    gated = ffn.kind == "gate"
    func = {"gelu": ACT.Gelu, "silu": ACT.Silu, "gate": ACT.Silu}[ffn.kind]
    blocks = ffn.width // ffn.block
    rows = ffn.block
    w1 = [m.expert_w1(ffn, first + e) for e in range(experts)]
    w2 = [m.expert_w2(ffn, first + e) for e in range(experts)]
    tiles = CHUNK // P
    per = blocks * (2 if gated else 1)
    hidden_done = s.up_read if gated else s.act
    turn_blocks = CHUNKS * blocks
    BANKS = 2
    with (
        nc.sbuf_tensor(f"hT_{ffn.name}", [P, 2, blocks, CHUNK], F32) as hT,
        nc.sbuf_tensor(f"gate_{ffn.name}", [P, 2, CHUNK], F32) as gate,
        nc.sbuf_tensor(f"biased_{ffn.name}", [P, tiles, D], F32) as biased,
        nc.Block(no_gpsimd_drain=True) as block,
    ):

        def over_experts(eng, run):
            for e in range(experts):
                run(e)

        def over_chunks(eng, run):
            with eng.Fori(0, CHUNKS - 1, 2) as c:
                for p in range(2):
                    run(c + p, p)

        def turn_of(cp, j):
            return (cp * blocks + j) % BANKS

        def bank(kind, cp, j):
            return m.ps[(0 if kind == "hidden" else BANKS) + turn_of(cp, j)]

        @block.tensor
        def _(pe):
            pe.wait_ge(ffn.loaded.sem, ffn.loaded.base)

            def expert(e):

                def hidden(c, cp):
                    n = e * turn_blocks + c * blocks
                    for j in range(blocks):
                        x = [m.xT[:, k, ds(c * CHUNK, CHUNK)] for k in range(FC)]
                        pe.wait_ge(s.act.sem, s.act.at(n + (j - 1)))
                        if gated:
                            pe.wait_ge(s.up_read.sem, s.up_read.at(n + (j - 1)))
                        first = ffn.gate_at + j * rows if gated else j * rows
                        for k in range(FC):
                            last = pe.matmul(bank("hidden", cp, j)[0:rows, 0:CHUNK], w1[e][0:FP, k, first:first + rows], x[k],
                                             start=(k == 0), stop=(k == FC - 1))
                        if gated:
                            up = ffn.up_at + j * rows
                            for k in range(FC):
                                last = pe.matmul(bank("up", cp, j)[0:rows, 0:CHUNK], w1[e][0:FP, k, up:up + rows], x[k],
                                                 start=(k == 0), stop=(k == FC - 1))
                        last.then_inc(s.hidden.sem, 1)

                def output(c, cp):
                    n = e * CHUNKS + c
                    pe.wait_ge(hidden_done.sem, hidden_done.at(n * blocks + blocks))
                    for i in range(tiles):
                        pe.wait_ge(s.out.sem, s.out.at(n * tiles + (i - tiles + 1)))
                        for j in range(blocks):
                            last = pe.matmul(m.ps[2 * BANKS + i][:, 0:D], hT[0:rows, cp, j, i * P:(i + 1) * P],
                                             w2[e][0:rows, j, :], start=(j == 0), stop=(j == blocks - 1))
                        last.then_inc(s.mm.sem, 1)

                with pe.Fori(0, CHUNKS - 1, 2) as c:
                    hidden(c, 0)
                    hidden(c + 1, 1)
                    output(c, 0)
                    output(c + 1, 1)

            over_experts(pe, expert)

        @block.scalar
        def _(act):
            def expert(e):
                def chunk(c, cp):
                    n = e * turn_blocks + c * blocks
                    act.wait_ge(s.mm.sem, s.mm.at((e * CHUNKS + c) * tiles - tiles))
                    for j in range(blocks):
                        act.wait_ge(s.hidden.sem, s.hidden.at(n + (j + 1)))
                        b1 = ffn.hidden_bias[0:rows, e * per + j:e * per + j + 1]
                        to = hT[0:rows, cp, j, :]
                        if gated:
                            act.wait_ge(s.up_read.sem, s.up_read.at(n + (j - 1)))
                            to = gate[0:rows, turn_of(cp, j), :]
                        act.activation(to, bank("hidden", cp, j)[0:rows, 0:CHUNK], func, bias=b1).then_inc(s.act.sem, 1)

                over_chunks(act, chunk)

            over_experts(act, expert)

        @block.vector
        def _(vec):
            vec.wait_ge(ffn.loaded.sem, ffn.loaded.base)

            def expert(e):
                def gates(c, cp):
                    n = e * turn_blocks + c * blocks
                    vec.wait_ge(s.mm.sem, s.mm.at((e * CHUNKS + c) * tiles - tiles))
                    for j in range(blocks):
                        vec.wait_ge(s.hidden.sem, s.hidden.at(n + (j + 1)))
                        vec.wait_ge(s.act.sem, s.act.at(n + (j + 1)))
                        to, g = hT[0:rows, cp, j, :], gate[0:rows, turn_of(cp, j), :]
                        up = bank("up", cp, j)[0:rows, 0:CHUNK]
                        up_bias = ffn.hidden_bias[0:rows, e * per + blocks + j:e * per + blocks + j + 1]
                        vec.scalar_tensor_tensor(to, up, up_bias, g, ALU.add, ALU.mult).then_inc(s.up_read.sem, 1)

                def outputs(c, cp):
                    n = (e * CHUNKS + c) * tiles
                    for i in range(tiles):
                        vec.wait_ge(s.mm.sem, s.mm.at(n + (i + 1)))
                        to = tile(dst, c * tiles + i)
                        got = m.ps[2 * BANKS + i][:, 0:D]
                        vec.tensor_tensor(biased[:, i, :], got, ffn.out_bias[:, e * D:(e + 1) * D],
                                          ALU.add).then_inc(s.out.sem, 1)
                        vec.wait_ge(s.out.sem, s.out.at(n + (i + 1)))
                        vec.tensor_tensor(to, biased[:, i, :], to, ALU.add).then_inc(s.summed.sem, 1)

                with vec.Fori(0, CHUNKS - 1, 2) as c:
                    if gated:
                        gates(c, 0)
                        gates(c + 1, 1)
                    outputs(c, 0)
                    outputs(c + 1, 1)

            over_experts(vec, expert)

        @block.sync
        def _(sp):
            if prefetch:
                prefetch(sp)
    for signal, n in ((s.hidden, experts * turn_blocks), (s.act, experts * turn_blocks),
                      (s.mm, experts * CHUNKS * tiles), (s.out, experts * CHUNKS * tiles)):
        signal.close(n)
    if gated:
        s.up_read.close(experts * turn_blocks)
    s.summed.close(experts * CHUNKS * tiles)


def rows_phase(nc, m, s, ffn, src):
    k = ffn.top
    with (
        nc.sbuf_tensor(f"row_{ffn.name}", [P, RING, D], F32) as row,
        nc.sbuf_tensor(f"place_{ffn.name}", [P, RING, k], U32) as place,
        nc.sbuf_tensor(f"seen_{ffn.name}", [P, TILES * k], U32) as seen,
        nc.Block(no_gpsimd_drain=True) as block,
    ):
        @block.vector
        def _(vec):
            def stage(t, p):
                vec.tensor_copy(place[:, p, :], m.put[:, ds(t * k, k)])
                vec.tensor_scalar(row[:, p, :], tile(src, t), m.mean[:, ds(t, 1)], m.rstd[:, ds(t, 1)],
                                  ALU.subtract, ALU.mult).then_inc(s.x.sem, 1)

            for p in range(RING):
                stage(p, p)
            with vec.Fori(1, TILES // RING) as r:
                for p in range(RING):
                    vec.wait_ge(s.moved[p].sem, s.moved[p].at(r * (16 * k)))
                    stage(r * RING + p, p)

        @block.gpsimd
        def _(pool):
            with pool.Fori(0, TILES // RING) as r:
                for p in range(RING):
                    pool.wait_ge(s.x.sem, s.x.at(r * RING + (p + 1)))
                    t = r * RING + p
                    pool.tensor_copy(seen[:, ds(t * k, k)], m.put[:, ds(t * k, k)]).then_inc(s.seen.sem, 1)
                    for j in range(k):
                        pool.indirect_dma_start(m.rows, bass.IndirectOffsetOnAxis(ap=place[:, p, j:j + 1], axis=0),
                                                row[:, p, :], None).then_inc(s.moved[p].sem, 16)
            pool.wait_ge(s.seen.sem, s.seen.at(TILES))
            for p in range(RING):
                pool.wait_ge(s.moved[p].sem, s.moved[p].at(16 * k * (TILES // RING)))
    s.x.close(TILES)
    s.seen.close(TILES)
    for p in range(RING):
        s.moved[p].close(16 * k * (TILES // RING))


def mixture_phase(nc, m, s, ffn, scale=None, shift=None, prefetch=None):
    n = ffn.places
    gated = ffn.kind == "gate"
    func = {"gelu": ACT.Gelu, "silu": ACT.Silu, "gate": ACT.Silu}[ffn.kind]
    rows = FP + 1 if ffn.biased else FP
    block_rows = ffn.block + (1 if ffn.bias_row else 0)
    blocks = ffn.width // ffn.block
    wide = 2 * ffn.width if gated else ffn.width
    per_bank = 512 // P
    hidden_done = s.up_read if gated else s.act
    W1 = m.w1_all[0:rows, :]
    W2 = m.w2_all[0:block_rows, :]
    with (
        nc.sbuf_tensor(f"slots_{ffn.name}", [P, 2, D], F32) as slots,
        nc.sbuf_tensor(f"slotsT_{ffn.name}", [FP + 1, 2, FC, P], F32) as slotsT,
        nc.sbuf_tensor(f"w1_{ffn.name}", [FP + 1, 2, FC * wide], F32) as w1,
        nc.sbuf_tensor(f"hiddenT_{ffn.name}", [P, 2, blocks, P], F32) as hT,
        nc.sbuf_tensor(f"gates_{ffn.name}", [P, 2, blocks if gated else 1, P], F32) as gate,
        nc.sbuf_tensor(f"result_{ffn.name}", [P, 2, D], F32) as result,
        nc.Block(no_gpsimd_drain=True) as block,
    ):
        def turns(eng, turn):
            for i in range(4):
                turn(i, i % 2)
            with eng.Fori(4, n - 1, 2) as i:
                for p in range(2):
                    turn(i + p, p)
            for i in range(n, n + 2):
                turn(i, i % 2)

        def has(i):
            return i not in (-2, -1, n, n + 1) if isinstance(i, int) else True

        def expert_of(eng, i):
            return eng.value_load(m.ids[0:1, ds(i, 1)], min_val=0, max_val=ffn.experts - 1)

        def hidden_bank(p, j):
            return m.ps[2 + 2 * p + j // per_bank][0:ffn.block, (j % per_bank) * P:(j % per_bank + 1) * P]

        @block.sync
        def _(sp):
            for i in range(2):
                sp.dma_start(slots[:, i, :], m.rows[i * P:(i + 1) * P, :]).then_inc(s.fetched[i].sem, 16)
            with sp.Fori(2, n - 1, 2) as i:
                for p in range(2):
                    sp.wait_ge(s.turned.sem, s.turned.at(i + (p - 1)))
                    sp.dma_start(slots[:, p, :], m.rows[ds((i + p) * P, P), :]).then_inc(s.fetched[p].sem, 16)
            if prefetch:
                prefetch(sp)

        @block.tensor
        def _(pe):
            pe.wait_ge(ffn.loaded.sem, ffn.loaded.base)

            def turn_slots(i, p):
                pe.wait_ge(s.fetched[p].sem, s.fetched[p].at((i - p) * 8 + 16))
                pe.wait_ge(s.xT.sem, s.xT.at(i - 1))
                for c in range(FC):
                    last = pe.matmul(m.ps[p][0:FP, c * P:(c + 1) * P], slots[:, p, c * FP:(c + 1) * FP],
                                     m.ident[:, :], start=True, stop=True, is_transpose=True)
                last.then_inc(s.turned.sem, 1)

            def hidden(i, p):
                pe.wait_ge(s.xT.sem, s.xT.at(i + 1))
                pe.wait_ge(s.copied.sem, s.copied.at(i + 1))
                pe.wait_ge(hidden_done.sem, hidden_done.at(i - 1))
                for half in range(2 if gated else 1):
                    for j in range(blocks):
                        to = hidden_bank(p, j + half * per_bank)
                        first = (half * ffn.up_at + (1 - half) * ffn.gate_at) if gated else 0
                        for c in range(FC):
                            high = rows if c == 0 else FP
                            at = c * wide + first + j * ffn.block
                            last = pe.matmul(to, w1[0:high, p, at:at + ffn.block], slotsT[0:high, p, c, :],
                                             start=(c == 0), stop=(c == FC - 1))
                last.then_inc(s.hidden.sem, 1)

            def output(i, p):
                e = expert_of(pe, i)
                pe.wait_ge(hidden_done.sem, hidden_done.at(i + 1))
                pe.wait_ge(s.out.sem, s.out.at(i - 1))
                for j in range(blocks):
                    last = pe.matmul(m.ps[6 + p][:, 0:D], hT[0:block_rows, p, j, :],
                                     W2[:, ds(e * (blocks * D) + j * D, D)], start=(j == 0), stop=(j == blocks - 1))
                last.then_inc(s.mm.sem, 1)

            def turn(i, p):
                if has(i):
                    turn_slots(i, p)
                if has(i - 1):
                    hidden(i - 1, 1 - p)
                if has(i - 2):
                    output(i - 2, p)

            turns(pe, turn)

        @block.scalar
        def _(act):
            act.wait_ge(ffn.loaded.sem, ffn.loaded.base)

            def features(i, p):
                act.wait_ge(s.hidden.sem, s.hidden.at(i - 1))
                act.wait_ge(s.turned.sem, s.turned.at(i + 1))
                if scale is None:
                    act.activation(slotsT[0:FP, p, :, :], m.ps[p][0:FP, 0:FC * P].rearrange("f (c k) -> f c k", c=FC),
                                   ACT.Copy).then_inc(s.xT.sem, 1)
                else:
                    for c in range(FC):
                        last = act.activation(slotsT[0:FP, p, c, :], m.ps[p][0:FP, c * P:(c + 1) * P], ACT.Identity,
                                              bias=shift[:, c:c + 1], scale=scale[:, c:c + 1])
                    last.then_inc(s.xT.sem, 1)

            def activate(i, p):
                act.wait_ge(s.hidden.sem, s.hidden.at(i + 1))
                act.wait_ge(s.mm.sem, s.mm.at(i - 1))
                to = gate if gated else hT
                for b in range(0, blocks, per_bank):
                    k = min(per_bank, blocks - b)
                    last = act.activation(to[0:ffn.block, p, b:b + k, :].rearrange("f j k -> f (j k)"),
                                          m.ps[2 + 2 * p + b // per_bank][0:ffn.block, 0:k * P], func)
                last.then_inc(s.act.sem, 1)

            def turn(i, p):
                if has(i):
                    features(i, p)
                if has(i - 1):
                    activate(i - 1, 1 - p)

            turns(act, turn)

        @block.vector
        def _(vec):
            vec.wait_ge(ffn.loaded.sem, ffn.loaded.base)
            if ffn.biased:
                vec.memset(slotsT[FP:FP + 1, :, 0, :], 1.0)
            if ffn.bias_row:
                vec.memset(hT[ffn.block:ffn.block + 1, :, :, :], 1.0)

            def copy(i, p):
                e = expert_of(vec, i)
                vec.wait_ge(s.hidden.sem, s.hidden.at(i - 1))
                vec.tensor_copy(w1[0:rows, p, :], W1[:, ds(e * (FC * wide), FC * wide)]).then_inc(s.copied.sem, 1)

            def gates(i, p):
                vec.wait_ge(s.act.sem, s.act.at(i + 1))
                vec.tensor_tensor(hT[0:ffn.block, p, :, :].rearrange("f j k -> f (j k)"),
                                  m.ps[3 + 2 * p][0:ffn.block, 0:blocks * P],
                                  gate[0:ffn.block, p, :, :].rearrange("f j k -> f (j k)"), ALU.mult).then_inc(s.up_read.sem, 1)

            def output(i, p):
                if ffn.biased and not ffn.bias_row:
                    e = expert_of(vec, i)
                vec.wait_ge(s.mm.sem, s.mm.at(i + 1))
                if not (isinstance(i, int) and i < 2):
                    vec.wait_ge(s.stored[p].sem, s.stored[p].at((i - p) * 8))
                if ffn.biased and not ffn.bias_row:
                    vec.tensor_tensor(result[:, p, :], m.ps[6 + p][:, 0:D], ffn.out_bias[:, ds(e * D, D)],
                                      ALU.add).then_inc(s.out.sem, 1)
                else:
                    vec.tensor_copy(result[:, p, :], m.ps[6 + p][:, 0:D]).then_inc(s.out.sem, 1)

            def turn(i, p):
                if has(i):
                    copy(i, p)
                if has(i - 1) and gated:
                    gates(i - 1, 1 - p)
                if has(i - 2):
                    output(i - 2, p)

            turns(vec, turn)

        @block.gpsimd
        def _(pool):
            with pool.Fori(0, n - 1, 2) as i:
                for p in range(2):
                    pool.wait_ge(s.out.sem, s.out.at(i + (p + 1)))
                    pool.dma_start(m.results[ds((i + p) * P, P), :], result[:, p, :]).then_inc(s.stored[p].sem, 16)
            for p in range(2):
                pool.wait_ge(s.stored[p].sem, s.stored[p].at(8 * n))
    for signal in (s.turned, s.xT, s.hidden, s.act, s.copied, s.mm, s.out):
        signal.close(n)
    if gated:
        s.up_read.close(n)
    for p in range(2):
        s.fetched[p].close(8 * n)
        s.stored[p].close(8 * n)


def combine_phase(nc, m, s, ffn, dst):
    k = ffn.top
    turns = TILES // RING
    with (
        nc.sbuf_tensor(f"gathered_{ffn.name}", [P, RING, k, D], F32) as gathered,
        nc.sbuf_tensor(f"from_{ffn.name}", [P, RING, k], U32) as place,
        nc.sbuf_tensor(f"seen_back_{ffn.name}", [P, TILES * k], U32) as seen,
        nc.Block(no_gpsimd_drain=True) as block,
    ):
        @block.vector
        def _(vec):
            def stage(r, p):
                vec.tensor_copy(place[:, p, :], m.get[:, ds((r * RING + p) * k, k)]).then_inc(s.stage.sem, 1)

            def add(r, p):
                vec.wait_ge(s.moved[p].sem, s.moved[p].at((r + 1) * (16 * k)))
                for j in range(k):
                    t = r * RING + p
                    if j > 0:
                        vec.wait_ge(s.summed.sem, s.summed.at(t * k + j))
                    vec.scalar_tensor_tensor(tile(dst, t), gathered[:, p, j, :], m.gates[:, ds(t * k + j, 1)],
                                             tile(dst, t), ALU.mult, ALU.add).then_inc(s.summed.sem, 1)

            for p in range(RING):
                vec.tensor_copy(place[:, p, :], m.get[:, p * k:(p + 1) * k]).then_inc(s.stage.sem, 1)
            with vec.Fori(0, turns - 1) as r:
                for p in range(RING):
                    add(r, p)
                    vec.wait_ge(s.summed.sem, s.summed.at((r * RING + (p + 1)) * k))
                    stage(r + 1, p)
            for p in range(RING):
                add(turns - 1, p)

        @block.gpsimd
        def _(pool):
            with pool.Fori(0, turns) as r:
                for p in range(RING):
                    pool.wait_ge(s.stage.sem, s.stage.at(r * RING + (p + 1)))
                    t = r * RING + p
                    pool.tensor_copy(seen[:, ds(t * k, k)], m.get[:, ds(t * k, k)]).then_inc(s.seen.sem, 1)
                    for j in range(k):
                        pool.indirect_dma_start(gathered[:, p, j, :], None, m.results[0:ffn.places * P, :],
                                                bass.IndirectOffsetOnAxis(ap=place[:, p, j:j + 1], axis=0),
                                                ).then_inc(s.moved[p].sem, 16)
            pool.wait_ge(s.seen.sem, s.seen.at(TILES))
    s.stage.close(TILES)
    s.summed.close(TILES * k)
    s.seen.close(TILES)
    for p in range(RING):
        s.moved[p].close(16 * k * turns)


class Steps:

    def __init__(self, vec, done, n=0):
        self.vec, self.done, self.n = vec, done, n

    def __call__(self, ins):
        self.n += 1
        link(self.vec, self.done, ins, self.n)


def pick_largest(vec, step, m, most, x, onehot, experts):
    shape = [P, TILES, experts]
    step(vec.tensor_reduce(most, x, AX, ALU.max))
    step(vec.tensor_tensor(onehot, x, most.unsqueeze(2).to_broadcast(shape), ALU.is_equal))
    step(vec.tensor_tensor(onehot, onehot, m.rank[:, 0:experts].unsqueeze(1).to_broadcast(shape), ALU.mult))
    step(vec.tensor_reduce(most, onehot, AX, ALU.max))
    step(vec.tensor_tensor(onehot, onehot, most.unsqueeze(2).to_broadcast(shape), ALU.is_equal))


class Scratch:

    def __init__(self, nc, ctx, ffn):
        def sb(name, *shape, dtype=F32):
            return ctx.enter_context(nc.sbuf_tensor(f"{name}_{ffn.name}", list(shape), dtype))

        cols = TILES * ffn.experts
        self.pick = [sb(f"pick{i}", P, cols) for i in range(max(2, ffn.top))]
        self.other, self.union, self.place = sb("other", P, cols), sb("union", P, cols), sb("place_of", P, cols)
        self.most, self.token = sb("most", P, TILES), sb("token", P, 3, TILES)
        self.group = sb("group", P, 3, TILES * 4)
        self.prefix, self.running = sb("prefix", P, cols), sb("running", P, cols)
        self.over, self.full = sb("over", P, ffn.experts, TILES), sb("full", P, ffn.experts)
        self.end, self.start = sb("end", P, ffn.experts), sb("start", P, ffn.experts)
        self.past, self.id = sb("past", 1, ffn.places, ffn.experts), sb("id", 1, ffn.places)
        self.flat, self.put = sb("flat", P, TILES), sb("put_f", P, TILES * ffn.top)


def view(buf, k):
    return buf[:, 0:TILES * k].rearrange("p (t e) -> p t e", e=k)


def before_tile(vec, step, m, w, counts, experts):
    cols = TILES * experts
    step(vec.tensor_copy(w.prefix[:, :].rearrange("p (e t) -> p t e", t=TILES), counts.rearrange("p (t e) -> p t e", e=experts)))
    step(vec.tensor_tensor_scan(w.running[:, :], m.restart[:, 0:cols], w.prefix[:, :], 0.0, ALU.mult, ALU.add))
    step(vec.tensor_tensor(w.prefix[:, :], w.running[:, :], w.prefix[:, :], ALU.subtract))


def count_union(pe, m, s, w, cols):
    pe.wait_ge(s.union.sem, s.union.at(1))
    pe.matmul(m.ps[4][:, 0:cols], m.triangle[:, :], w.union[:, :], start=True, stop=True)
    pe.matmul(m.ps[5][:, 0:cols], m.ones[:, :], w.union[:, :], start=True, stop=True).then_inc(s.counted.sem, 1)


def give_places(vec, step, m, s, w, ffn):
    experts, k, cols = ffn.experts, ffn.top, TILES * ffn.experts
    wide = [P, TILES, experts]
    if k == 1:
        vec.tensor_copy(w.union[:, :], w.pick[0][:, :]).then_inc(s.union.sem, 1)
    else:
        have = w.pick[0]
        for j in range(1, k):
            last = vec.tensor_tensor(w.union[:, :], have[:, :], w.pick[j][:, :], ALU.add)
            if j == k - 1:
                last.then_inc(s.union.sem, 1)
            else:
                step(last)
            have = w.union
    vec.wait_ge(s.counted.sem, s.counted.at(1))
    before_tile(vec, step, m, w, m.ps[5][:, 0:cols], experts)
    step(vec.tensor_tensor(view(w.place, experts), m.ps[4][:, 0:cols].rearrange("p (t e) -> p t e", e=experts),
                           w.prefix[:, :].rearrange("p (e t) -> p t e", t=TILES), ALU.add))
    count = w.running[:, :].rearrange("p (e t) -> p e t", t=TILES)[:, :, TILES - 1]
    step(vec.tensor_scalar(w.full[:, :], count, 1.0 / P, None, ALU.mult))
    many = [P, experts, TILES]
    step(vec.tensor_tensor(w.over[:, :, :], w.full[:, :].unsqueeze(2).to_broadcast(many),
                           m.index[:, 0:TILES].unsqueeze(1).to_broadcast(many), ALU.is_gt))
    step(vec.tensor_reduce(w.full[:, :], w.over[:, :, :], AX, ALU.add))
    step(vec.tensor_tensor_scan(w.end[:, :], m.ones[:, 0:experts], w.full[:, :], 0.0, ALU.mult, ALU.add))
    step(vec.tensor_tensor(w.start[:, :], w.end[:, :], w.full[:, :], ALU.subtract))
    step(vec.tensor_scalar(w.start[:, :], w.start[:, :], float(P), -1.0, ALU.mult, ALU.add))
    step(vec.tensor_tensor(view(w.place, experts), view(w.place, experts), w.start[:, :].unsqueeze(1).to_broadcast(wide), ALU.add))
    get = w.put[:, :].rearrange("p (t k) -> p t k", k=k)
    for j in range(k):
        step(vec.tensor_tensor(w.other[:, :], w.place[:, :], w.pick[j][:, :], ALU.mult))
        step(vec.tensor_reduce(get[:, :, j], view(w.other, experts), AX, ALU.add))
    step(vec.tensor_copy(m.get[:, 0:TILES * k], w.put[:, :]))
    if ffn.capacity:
        for j in range(k):
            step(vec.tensor_reduce(w.flat[:, :], view(w.pick[j], experts), AX, ALU.add))
            step(vec.tensor_scalar(w.flat[:, :], w.flat[:, :], -1.0, 1.0, ALU.mult, ALU.add))
            step(vec.tensor_scalar(w.most[:, :], m.token_id[:, :], float(ffn.places * P + j * TOKENS), None, ALU.add))
            step(vec.tensor_tensor(w.flat[:, :], w.flat[:, :], w.most[:, :], ALU.mult))
            step(vec.tensor_tensor(get[:, :, j], get[:, :, j], w.flat[:, :], ALU.add))
    step(vec.tensor_copy(m.put[:, 0:TILES * k], w.put[:, :]))
    three = [1, ffn.places, experts]
    step(vec.tensor_tensor(w.past[:, :, :], m.index[0:1, 0:ffn.places].unsqueeze(2).to_broadcast(three),
                           w.end[0:1, :].unsqueeze(1).to_broadcast(three), ALU.is_ge))
    step(vec.tensor_reduce(w.id[:, :], w.past[:, :, :], AX, ALU.add))
    step(vec.tensor_scalar(w.id[:, :], w.id[:, :], float(experts - 1), None, ALU.min))
    step(vec.tensor_copy(m.ids[:, 0:ffn.places], w.id[:, :]))


def route_top2_phase(nc, m, s, ffn):
    experts, cols = ffn.experts, TILES * ffn.experts
    x = view(m.logits, experts)
    with ExitStack() as ctx:
        w = Scratch(nc, ctx, ffn)
        first, second, other = (view(b, experts) for b in (w.pick[0], w.pick[1], w.other))
        v1, v2, inv = w.token[:, 0, :], w.token[:, 1, :], w.token[:, 2, :]
        gates = m.gates[:, 0:TILES * 2].rearrange("p (t k) -> p t k", k=2)
        block = ctx.enter_context(nc.Block(no_gpsimd_drain=True))

        @block.vector
        def _(vec):
            step = Steps(vec, s.vec)
            pick_largest(vec, step, m, w.most[:, :], x, first, experts)
            step(vec.tensor_tensor(other, x, first, ALU.mult))
            step(vec.tensor_reduce(v1, other, AX, ALU.add))
            step(vec.scalar_tensor_tensor(other, first, NEG, x, ALU.mult, ALU.add))
            pick_largest(vec, step, m, w.most[:, :], other, second, experts)
            step(vec.tensor_tensor(other, x, second, ALU.mult))
            step(vec.tensor_reduce(v2, other, AX, ALU.add))
            vec.tensor_tensor(v2, v2, v1, ALU.subtract).then_inc(s.x.sem, 1)
            if ffn.capacity:
                for j in range(2):
                    vec.wait_ge(s.mm.sem, s.mm.at(j + 1))
                    before_tile(vec, step, m, w, m.ps[2 + j][:, 0:cols], experts)
                    step(vec.tensor_tensor(other, m.ps[j][:, 0:cols].rearrange("p (t e) -> p t e", e=experts),
                                           w.prefix[:, :].rearrange("p (e t) -> p t e", t=TILES), ALU.add))
                    step(vec.tensor_scalar(other, other, float(ffn.capacity), None, ALU.is_le))
                    step(vec.tensor_tensor(w.pick[j][:, :], w.pick[j][:, :], w.other[:, :], ALU.mult))
            vec.wait_ge(s.exps.sem, s.exps.at(1))
            step(vec.tensor_scalar(inv, v2, 1.0, None, ALU.add))
            step(vec.reciprocal(inv, inv))
            step(vec.tensor_tensor(v2, v2, inv, ALU.mult))
            for j, gate in enumerate((inv, v2)):
                if ffn.capacity:
                    step(vec.tensor_reduce(w.flat[:, :], view(w.pick[j], experts), AX, ALU.add))
                    step(vec.tensor_tensor(gates[:, :, j], gate, w.flat[:, :], ALU.mult))
                else:
                    step(vec.tensor_copy(gates[:, :, j], gate))
            give_places(vec, step, m, s, w, ffn)
            m.vec_links = step.n

        @block.scalar
        def _(act):
            act.wait_ge(s.x.sem, s.x.at(1))
            act.activation(v2, v2, ACT.Exp).then_inc(s.exps.sem, 1)

        @block.tensor
        def _(pe):
            if ffn.capacity:
                pe.wait_ge(s.x.sem, s.x.at(1))
                for j in range(2):
                    pick = w.pick[j][:, :]
                    pe.matmul(m.ps[j][:, 0:cols], m.triangle[:, :], pick, start=True, stop=True)
                    pe.matmul(m.ps[2 + j][:, 0:cols], m.ones[:, :], pick, start=True, stop=True).then_inc(s.mm.sem, 1)
            count_union(pe, m, s, w, cols)
    s.vec.close(m.vec_links)
    for signal in (s.x, s.exps, s.union, s.counted):
        signal.close(1)
    if ffn.capacity:
        s.mm.close(2)


def route_top1_phase(nc, m, s, ffn):
    experts, cols = ffn.experts, TILES * ffn.experts
    x = view(m.logits, experts)
    with ExitStack() as ctx:
        w = Scratch(nc, ctx, ffn)
        first, most = view(w.pick[0], experts), w.token[:, 0, :]
        block = ctx.enter_context(nc.Block(no_gpsimd_drain=True))

        @block.vector
        def _(vec):
            step = Steps(vec, s.vec)
            step(vec.tensor_reduce(most, x, AX, ALU.max))
            vec.tensor_tensor(x, x, most.unsqueeze(2).to_broadcast([P, TILES, experts]), ALU.subtract).then_inc(s.x.sem, 1)
            vec.wait_ge(s.exps.sem, s.exps.at(1))
            step(vec.tensor_reduce(most, x, AX, ALU.add))
            step(vec.reciprocal(most, most))
            step(vec.tensor_tensor(x, x, most.unsqueeze(2).to_broadcast([P, TILES, experts]), ALU.mult))
            step(vec.tensor_reduce(m.gates[:, 0:TILES], x, AX, ALU.max))
            pick_largest(vec, step, m, w.most[:, :], x, first, experts)
            give_places(vec, step, m, s, w, ffn)
            m.vec_links = step.n

        @block.scalar
        def _(act):
            act.wait_ge(s.x.sem, s.x.at(1))
            act.activation(x, x, ACT.Exp).then_inc(s.exps.sem, 1)

        @block.tensor
        def _(pe):
            count_union(pe, m, s, w, cols)
    s.vec.close(m.vec_links)
    for signal in (s.x, s.exps, s.union, s.counted):
        signal.close(1)


def route_groups_phase(nc, m, s, ffn, groups, top_groups, scaling):
    experts, top, cols = ffn.experts, ffn.top, TILES * ffn.experts
    per = experts // groups
    rows = TILES * groups
    with ExitStack() as ctx:
        w = Scratch(nc, ctx, ffn)
        score, sfc, one, left = m.logits, w.other, w.union, w.place
        total = w.token[:, 0, :]
        gates = m.gates[:, 0:TILES * top].rearrange("p (t k) -> p t k", k=top)
        block = ctx.enter_context(nc.Block(no_gpsimd_drain=True))

        def grouped(buf):
            return buf[:, 0:cols].rearrange("p (t k) -> p t k", k=per)

        def by_group(j):
            return w.group[:, j, :].rearrange("p (t g) -> p t g", g=groups)

        @block.vector
        def _(vec):
            step = Steps(vec, s.vec)
            vec.wait_ge(s.exps.sem, s.exps.at(1))
            step(vec.tensor_tensor(view(sfc, experts), view(score, experts),
                                   m.correction[:, :].unsqueeze(1).to_broadcast([P, TILES, experts]), ALU.add))
            best, second = w.group[:, 0, :], w.group[:, 1, :]
            wide = [P, rows, per]
            step(vec.tensor_reduce(best, grouped(sfc), AX, ALU.max))
            step(vec.tensor_tensor(grouped(one), grouped(sfc), best.unsqueeze(2).to_broadcast(wide), ALU.is_equal))
            step(vec.tensor_tensor(grouped(one), grouped(one), m.rank[:, 0:per].unsqueeze(1).to_broadcast(wide), ALU.mult))
            step(vec.tensor_reduce(second, grouped(one), AX, ALU.max))
            step(vec.tensor_tensor(grouped(one), grouped(one), second.unsqueeze(2).to_broadcast(wide), ALU.is_equal))
            step(vec.scalar_tensor_tensor(left[:, :], one[:, :], NEG, sfc[:, :], ALU.mult, ALU.add))
            step(vec.tensor_reduce(second, grouped(left), AX, ALU.max))
            step(vec.tensor_tensor(best, best, second, ALU.add))
            chosen = w.group[:, 2, :]
            for n in range(top_groups):
                pick_largest(vec, step, m, w.most[:, :], by_group(0), by_group(1), groups)
                if n == 0:
                    step(vec.tensor_copy(chosen, second))
                else:
                    step(vec.tensor_tensor(chosen, chosen, second, ALU.add))
                if n < top_groups - 1:
                    step(vec.scalar_tensor_tensor(best, second, NEG, best, ALU.mult, ALU.add))
            step(vec.tensor_tensor(grouped(sfc), grouped(sfc), chosen.unsqueeze(2).to_broadcast(wide), ALU.mult))
            for n in range(top):
                pick_largest(vec, step, m, w.most[:, :], view(sfc, experts), view(w.pick[n], experts), experts)
                if n < top - 1:
                    step(vec.scalar_tensor_tensor(sfc[:, :], w.pick[n][:, :], NEG, sfc[:, :], ALU.mult, ALU.add))
                step(vec.tensor_tensor(left[:, :], w.pick[n][:, :], score[:, 0:cols], ALU.mult))
                step(vec.tensor_reduce(gates[:, :, n], view(left, experts), AX, ALU.add))
            step(vec.tensor_reduce(total, gates, AX, ALU.add))
            step(vec.tensor_scalar(total, total, 1e-20, None, ALU.add))
            step(vec.reciprocal(total, total))
            step(vec.tensor_tensor(gates, gates, total.unsqueeze(2).to_broadcast([P, TILES, top]), ALU.mult))
            step(vec.tensor_scalar(gates, gates, scaling, None, ALU.mult))
            give_places(vec, step, m, s, w, ffn)
            m.vec_links = step.n

        @block.scalar
        def _(act):
            act.activation(m.logits[:, 0:cols], m.logits[:, 0:cols], ACT.Sigmoid).then_inc(s.exps.sem, 1)

        @block.tensor
        def _(pe):
            count_union(pe, m, s, w, cols)
    s.vec.close(m.vec_links)
    for signal in (s.exps, s.union, s.counted):
        signal.close(1)


class Signals:

    def __init__(self, make):
        def signal(name):
            return Signal(make(name))

        def arrival(name):
            return Signal(make(name), 0)

        self.vec = signal("vec")
        self.soft = signal("soft")
        self.rot = signal("rot")
        self.stats = signal("stats")
        self.var = signal("var")
        self.std = signal("std")
        self.x = signal("x")
        self.kept = signal("kept")
        self.turned = signal("turned")
        self.xT = signal("xT")
        self.route = signal("route")
        self.logit = signal("logit")
        self.stage = signal("stage")
        self.mm = signal("mm")
        self.out = signal("out")
        self.q = signal("q")
        self.k = signal("k")
        self.v = signal("v")
        self.r = signal("r")
        self.key_out = signal("key_out")
        self.projected = signal("projected")
        self.tripled = signal("tripled")
        self.scores = signal("scores")
        self.scored = signal("scored")
        self.shifted = signal("shifted")
        self.gelu = signal("gelu")
        self.exps = signal("exps")
        self.weight = signal("weight")
        self.weightT = signal("weightT")
        self.inverse = signal("inverse")
        self.weighed = signal("weighed")
        self.context = signal("context")
        self.context_turned = signal("context_turned")
        self.context_out = signal("context_out")
        self.hidden = signal("hidden")
        self.act = signal("act")
        self.up_read = signal("up_read")
        self.summed = signal("summed")
        self.patch = signal("patch")
        self.inverted = signal("inverted")
        self.sums = signal("sums")
        self.seen = signal("seen")
        self.union = signal("union")
        self.counted = signal("counted")
        self.copied = signal("copied")
        self.cleared = signal("cleared")
        self.lead = [self.vec, self.soft, self.rot, self.stats, self.var, self.std, self.x, self.kept, self.turned,
                     self.xT, self.route, self.logit, self.stage, self.mm, self.out, self.q, self.k, self.v, self.r,
                     self.key_out, self.projected, self.tripled, self.scores, self.scored, self.shifted, self.gelu,
                     self.exps, self.weight, self.weightT, self.inverse, self.weighed, self.context,
                     self.context_turned, self.context_out, self.hidden, self.act, self.up_read, self.summed,
                     self.patch, self.inverted, self.sums, self.seen, self.union, self.counted, self.copied, self.cleared]
        self.consts = arrival("consts")
        self.image = [arrival(f"image{i}") for i in range(IMAGES * GRID // P)]
        self.patch_store = arrival("patch_store")
        self.patch_load = arrival("patch_load")
        self.attention_w = arrival("attention_w")
        self.expert_w = [arrival(f"expert_w{i}") for i in range(2)]
        self.filled = arrival("filled")
        self.moved = [arrival(f"moved{i}") for i in range(RING)]
        self.fetched = [arrival(f"fetched{i}") for i in range(2)]
        self.stored = [arrival(f"stored{i}") for i in range(2)]
        self.store = arrival("store")


class Memory:

    def __init__(self, nc, ctx):
        def sb(name, *shape):
            return ctx.enter_context(nc.sbuf_tensor(name, list(shape), F32))

        self.loads = []

        def const(name, *shape):
            buf = sb(name, *shape)
            self.loads.append((name, buf))
            return buf

        self.ident, self.triangle, self.ones = const("ident", P, P), const("triangle", P, P), const("ones", P, P)
        self.rank, self.restart = const("rank", P, 16), const("restart", P, 16 * TILES)
        self.index, self.token_id = const("index", P, MOST_PLACES), const("token_id", P, TILES)
        self.head_mask = const("head_mask", FP, HPC)
        self.value_mask = const("value_mask", GROUP * SEQ, GROUP * HEAD)
        self.causal, self.causal_two = const("causal", P, SEQ), const("causal_two", P, SEQ)
        self.cos, self.sin, self.zero_bias = const("cos", FP, SEQ), const("sin", FP, SEQ), const("zero_bias", FP, FC)
        self.W1, self.b1, self.W2, self.b2 = const("W1", P, PATCH), const("b1", P, 1), const("W2", P, PATCH), const("b2", P, 1)
        self.W3, self.b3 = const("W3", CHANNELS, D), const("b3", P, D)
        self.mix, self.decay, self.first = const("mix", FP, 3 * FC), const("decay", FP, FC), const("first", FP, FC)
        self.ln = const("ln", FP, 4 * FC)
        self.qkv0, self.qkv1 = const("qkv0", FP, 3 * FC), const("qkv1", FP, 3 * FC)
        self.out0, self.out1 = const("out0", 1, D), const("out1", 1, D)
        self.router0, self.router_b0 = const("router0", FP, FC, 4), const("router_b0", P, 4)
        self.router1, self.router2 = const("router1", FP, FC, 8), const("router2", FP, FC, 8)
        self.router3, self.router_b3 = const("router3", FP, FC, 16), const("router_b3", P, 16)
        self.correction = const("correction", P, 16)
        self.h, self.xT = sb("h", P, TILES * D), sb("xT", FP, FC, TOKENS)
        self.xs, self.x_tile = sb("xs", FP, 2, FC, P), sb("x_tile", P, 2, D)
        self.stats, self.mean = sb("stats", P, TILES * 6), sb("mean", P, TILES)
        self.other, self.rstd, self.unmix = sb("other", P, TILES), sb("rstd", P, TILES), sb("unmix", FP, 3 * FC)
        self.logits, self.gates = sb("logits", P, TILES * 16), sb("gates", P, TILES * 4)
        self.put = ctx.enter_context(nc.sbuf_tensor("put", [P, TILES * 4], U32))
        self.get = ctx.enter_context(nc.sbuf_tensor("get", [P, TILES * 4], U32))
        self.ids = ctx.enter_context(nc.sbuf_tensor("ids", [1, MOST_PLACES], I32))
        self.attention_w = [sb(f"attention_w{i}", FP, FC, 6 * D) for i in range(2)]
        self.ps = [ctx.enter_context(nc.psum_tensor(f"bank{i}", [P, 512], F32)) for i in range(8)]


    def grow(self, nc, ctx):
        self.w1_all = ctx.enter_context(nc.sbuf_tensor("expert_w1", [P, 8 * FC * 1024], F32))
        self.w2_all = ctx.enter_context(nc.sbuf_tensor("expert_w2", [P, 8 * 6 * D], F32))
        self.out_bias = ctx.enter_context(nc.sbuf_tensor("out_bias", [P, 8 * D], F32))
        self.hidden_bias = ctx.enter_context(nc.sbuf_tensor("hidden_bias", [P, 6], F32))
        whole = 8 * FC * 1024
        self.z = self.w1_all[:, whole - TILES * D:whole]

    def expert_w1(self, ffn, e):
        n = FC * ffn.columns
        at = ffn.first + e * n
        return self.w1_all[0:P, at:at + n].rearrange("f (c k) -> f c k", c=FC)

    def expert_w2(self, ffn, e):
        n = ffn.width // ffn.block * D
        at = ffn.second + e * n
        return self.w2_all[0:P, at:at + n].rearrange("f (j k) -> f j k", k=D)


class FeedForward:

    def __init__(self, loaded, name, experts, kind, width, top=0, biased=True, block=P, gate_at=0, up_at=0, capacity=None,
                 first=0, second=0, bias_row=False, out_bias=None, hidden_bias=None):
        self.loaded = loaded
        self.name, self.experts, self.kind, self.width, self.top = name, experts, kind, width, top
        self.biased, self.block, self.gate_at, self.up_at = biased, block, gate_at, up_at
        self.columns = 2 * width if kind == "gate" else width
        self.capacity, self.first, self.second, self.bias_row = capacity, first, second, bias_row
        self.out_bias, self.hidden_bias = out_bias, hidden_bias
        self.places = most_places(experts, top)


def start_phase(nc, m, s, ins):
    with nc.Block(no_gpsimd_drain=True) as block:

        @block.vector
        def _(vec):
            for signal in s.lead:
                vec.sem_inc(signal.sem, signal.base)

        @block.sync
        def _(sp):
            for name, buf in m.loads:
                shape = list(buf.shape)
                src = ins[name] if ins[name].shape[0] == shape[0] else ins[name].to_broadcast(shape)
                sp.dma_start(buf[:, :] if len(shape) == 2 else buf[:, :, :], src).then_inc(s.consts.sem, 16)
            sp.wait_ge(s.consts.sem, 16 * len(m.loads))


def tower(nc, ins, out, patch_dram, rows, results):
    with ExitStack() as ctx:
        m = Memory(nc, ctx)
        s = Signals(lambda name: ctx.enter_context(nc.semaphore(name)))
        m.patch_dram, m.rows, m.results = patch_dram, rows, results

        def three(buf, first=0):
            return [buf[:, (first + j) * FC:(first + j + 1) * FC] for j in range(3)]

        def output_w(layer):
            return m.attention_w[layer % 2][:, :, 3 * D:4 * D]

        g1, b1, g2, b2 = (m.ln[:, j * FC:(j + 1) * FC] for j in range(4))

        start_phase(nc, m, s, ins)
        token_phase(nc, m, s, ins)

        feature_phase(nc, m, s, m.h)
        rwkv_phase(nc, m, s)
        m.grow(nc, ctx)
        ffn0 = FeedForward(s.expert_w[1], "ffn0", 4, "gelu", 768, top=2, out_bias=m.out_bias[:, 0:4 * D])
        mlp = FeedForward(s.expert_w[0], "mlp", 1, "gelu", 768, first=4 * FC * 768, second=4 * 6 * D,
                          out_bias=m.out_bias[:, 4 * D:5 * D], hidden_bias=m.hidden_bias[:, :])
        ffn1 = FeedForward(s.expert_w[0], "ffn1", 8, "silu", 768, top=1, out_bias=m.out_bias[:, :])
        ffn2 = FeedForward(s.expert_w[1], "ffn2", 8, "gate", 512, top=2, biased=False, gate_at=512, capacity=int(1.2 * TOKENS / 8))
        ffn3 = FeedForward(s.expert_w[0], "ffn3", 16, "gate", 96, top=4, block=96, up_at=96, bias_row=True)
        shared = FeedForward(s.expert_w[0], "shared", 2, "gate", 96, block=96, up_at=96, first=16 * FC * D, second=16 * D,
                             out_bias=m.out_bias[:, 0:2 * D], hidden_bias=m.hidden_bias[0:FP, 0:4])

        project_phase(nc, m, s, output_w(1), m.h)
        feature_phase(nc, m, s, m.h, keep=m.z)
        feature_phase(nc, m, s, m.z, scale=g1, shift=b1)
        attention_phase(nc, m, s, 0, "plain", three(m.qkv0), lambda sp: load_resident(sp, m, s, ins, mlp))
        project_phase(nc, m, s, output_w(0), m.z, m.out0[0:1, :])
        feature_phase(nc, m, s, m.z, norm=False)

        def load_next(sp):
            load_attention(sp, m, s, ins, 1)
            load_resident(sp, m, s, ins, ffn0)

        expert_phase(nc, m, s, mlp, m.z, 0, 1, load_next)
        feature_phase(nc, m, s, m.z, scale=g2, shift=b2, router=(m.router0, m.router_b0[:, :], 4))
        route_top2_phase(nc, m, s, ffn0)
        rows_phase(nc, m, s, ffn0, m.z)
        mixture_phase(nc, m, s, ffn0, scale=g2, shift=b2)
        combine_phase(nc, m, s, ffn0, m.z)
        add_phase(nc, m, s, m.h, m.z)

        feature_phase(nc, m, s, m.h)
        attention_phase(nc, m, s, 1, "causal", three(m.qkv1), lambda sp: load_resident(sp, m, s, ins, ffn1))
        project_phase(nc, m, s, output_w(1), m.h, m.out1[0:1, :])
        feature_phase(nc, m, s, m.h, router=(m.router1, None, 8))
        route_top1_phase(nc, m, s, ffn1)
        rows_phase(nc, m, s, ffn1, m.h)
        mixture_phase(nc, m, s, ffn1, prefetch=lambda sp: load_attention(sp, m, s, ins, 2))
        combine_phase(nc, m, s, ffn1, m.h)

        feature_phase(nc, m, s, m.h)
        attention_phase(nc, m, s, 2, "erf", prefetch=lambda sp: load_resident(sp, m, s, ins, ffn2))
        project_phase(nc, m, s, output_w(2), m.h)
        feature_phase(nc, m, s, m.h, router=(m.router2, None, 8))
        route_top2_phase(nc, m, s, ffn2)
        rows_phase(nc, m, s, ffn2, m.h)
        mixture_phase(nc, m, s, ffn2, prefetch=lambda sp: load_attention(sp, m, s, ins, 3))
        combine_phase(nc, m, s, ffn2, m.h)

        def load_last(sp):
            load_resident(sp, m, s, ins, ffn3)
            load_resident(sp, m, s, ins, shared)

        feature_phase(nc, m, s, m.h)
        attention_phase(nc, m, s, 3, "causal", prefetch=load_last)
        project_phase(nc, m, s, output_w(3), m.h)
        feature_phase(nc, m, s, m.h, router=(m.router3, m.router_b3[:, :], 16))
        route_groups_phase(nc, m, s, ffn3, groups=4, top_groups=2, scaling=2.5)
        rows_phase(nc, m, s, ffn3, m.h)
        mixture_phase(nc, m, s, ffn3)
        expert_phase(nc, m, s, shared, m.h, 0, 2)
        combine_phase(nc, m, s, ffn3, m.h)

        store_phase(nc, s, m.h, out)


def constants():
    f = np.float32
    p = np.arange(P)
    query = np.where(p < SEQ, p, np.where((p >= SECOND) & (p < SECOND + SEQ), p - SECOND, SEQ))
    seen = np.arange(SEQ)[None, :] <= query[:, None]
    half = HEAD // 2
    freq = (f(1.0) / f(10000.0) ** (np.arange(half, dtype=f) / f(half))).astype(f)
    angle = freq[:, None] * np.arange(SEQ, dtype=f)[None, :]
    pair = (np.arange(FP) % HEAD) // 2
    sign = np.where(np.arange(FP) % 2 == 0, f(-1), f(1))
    return {
        "ident": np.eye(P, dtype=f),
        "triangle": (p[:, None] <= p[None, :]).astype(f),
        "ones": np.ones((P, P), f),
        "rank": np.tile(np.arange(16, 0, -1).astype(f), (P, 1)),
        "restart": np.tile((np.arange(16 * TILES) % TILES != 0).astype(f), (P, 1)),
        "index": np.tile(np.arange(MOST_PLACES, dtype=f), (P, 1)),
        "token_id": (np.arange(TILES)[None, :] * P + p[:, None]).astype(f),
        "head_mask": (np.arange(FP)[:, None] // HEAD == np.arange(HPC)[None, :]).astype(f),
        "value_mask": (np.arange(GROUP * SEQ)[:, None] // SEQ == np.arange(GROUP * HEAD)[None, :] // HEAD).astype(f),
        "causal": np.where(seen, f(0), f(NEG)).astype(f),
        "causal_two": np.where(seen, f(2), f(0)).astype(f),
        "cos": np.cos(angle)[pair].astype(f),
        "sin": (np.sin(angle)[pair] * sign[:, None]).astype(f),
        "zero_bias": np.zeros((FP, FC), f),
    }


def layout(a):
    def feature(w):
        return w.reshape(FC, FP, -1).transpose(1, 0, 2)

    def column(*v):
        return np.concatenate([x.reshape(FC, FP).T for x in v], axis=1)

    def hidden(v, rows):
        return v.reshape(-1, rows).T

    def first(w, bias=None):
        w = w.reshape(w.shape[0], FC, FP, -1).transpose(0, 2, 1, 3)
        if bias is None:
            return w
        return np.concatenate([w, np.stack([bias, np.zeros_like(bias)], axis=1)[:, None]], axis=1)

    def second(w, rows):
        return w.reshape(w.shape[0], -1, rows, D).transpose(0, 2, 1, 3)

    def side(*w):
        return feature(np.concatenate(w, axis=1))

    turned = np.arange(D) ^ 1
    wide = D // 2
    t = constants()
    x = a["x"].reshape(IMAGES, CHANNELS, GRID, PATCH * SIDE).transpose(1, 0, 2, 3)
    t.update({
        "x": x.reshape(CHANNELS, IMAGES * GRID, PATCH * SIDE),
        "W1": a["L0_tok_W1"], "b1": a["L0_tok_b1"].reshape(1, 1), "W2": a["L0_tok_W2"],
        "b2": a["L0_tok_b2"].reshape(1, 1), "W3": a["L0_tok_W3"].T, "b3": a["L0_tok_b3"].reshape(1, D),
        "mix": column(a["L0_attn_mix_k"], a["L0_attn_mix_v"], a["L0_attn_mix_r"]),
        "decay": column(a["L0_attn_time_decay"]), "first": column(a["L0_attn_time_first"]),
        "rwkv": side(*(a[f"L0_attn_W{k}"].T for k in "kvro")),
        "ln": column(a["L0_ffn_ln1_g"], a["L0_ffn_ln1_b"], a["L0_ffn_ln2_g"], a["L0_ffn_ln2_b"]),
        "attention0": side(a["L0_ffn_in_w"].T, a["L0_ffn_out_w"].T),
        "attention1": side(a["L1_attn_W_attn"], a["L1_attn_W_proj"]),
        "attention2": side(*(a[f"L2_attn_W{k}"].T for k in ("q", "k", "v", "proj")),
                           a["L2_attn_Wq"].T[:, turned], a["L2_attn_Wk"].T[:, turned]),
        "attention3": side(*(a[f"L3_attn_w{k}"].T for k in "qkvo")),
        "qkv0": column(*a["L0_ffn_in_b"].reshape(3, D)), "qkv1": column(*a["L1_attn_b_attn"].reshape(3, D)),
        "out0": a["L0_ffn_out_b"].reshape(1, D), "out1": a["L1_attn_b_proj"].reshape(1, D),
        "router0": feature(a["L0_ffn_gate_w"].T), "router_b0": a["L0_ffn_gate_b"].reshape(1, -1),
        "router1": feature(a["L1_ffn_Wg"]), "router2": feature(a["L2_ffn_Wg"]),
        "router3": feature(a["L3_ffn_router_w"].T), "router_b3": a["L3_ffn_router_b"].reshape(1, -1),
        "correction": a["L3_ffn_corr_bias"].reshape(1, -1),
        "mlp_w1": first(a["L0_ffn_mlp_w1"][None]), "mlp_w2": second(a["L0_ffn_mlp_w2"][None], P),
        "mlp_b1": hidden(a["L0_ffn_mlp_b1"][None], P), "mlp_b2": a["L0_ffn_mlp_b2"].reshape(1, D),
        "ffn0_w1": first(a["L0_ffn_exp_w1"], a["L0_ffn_exp_b1"]), "ffn0_w2": second(a["L0_ffn_exp_w2"], P),
        "ffn0_b2": a["L0_ffn_exp_b2"].reshape(1, -1),
        "ffn1_w1": first(a["L1_ffn_W1"], a["L1_ffn_b1"]), "ffn1_w2": second(a["L1_ffn_W2"], P),
        "ffn1_b2": a["L1_ffn_b2"].reshape(1, -1),
        "ffn2_w1": first(a["L2_ffn_W1"]), "ffn2_w2": second(a["L2_ffn_W2"], P),
        "ffn3_w1": first(np.concatenate([a["L3_ffn_gWg"], a["L3_ffn_gWu"]], axis=2),
                         np.concatenate([a["L3_ffn_gbg"], a["L3_ffn_gbu"]], axis=1)),
        "ffn3_w2": np.concatenate([second(a["L3_ffn_gWd"], wide), a["L3_ffn_gbd"][:, None, None, :]], axis=1),
        "shared_w1": first(np.stack([np.concatenate([a["L3_ffn_sWg"][:, h], a["L3_ffn_sWu"][:, h]], axis=1)
                                     for h in (slice(0, wide), slice(wide, D))])),
        "shared_w2": second(a["L3_ffn_sWd"].reshape(2, wide, D), wide),
        "shared_b1": np.stack([a["L3_ffn_sbg"][:wide], a["L3_ffn_sbu"][:wide],
                               a["L3_ffn_sbg"][wide:], a["L3_ffn_sbu"][wide:]], axis=1),
        "shared_b2": np.concatenate([a["L3_ffn_sbd"], np.zeros(D, np.float32)]).reshape(1, -1),
    })
    return {k: np.ascontiguousarray(v) for k, v in t.items()}


def kernel(**inputs):
    import concourse.bacc as bacc
    from concourse.bass_utils import run_bass_kernel_spmd

    arrays = layout({k: np.asarray(v) for k, v in inputs.items()})
    nc = bacc.Bacc("TRN2", target_bir_lowering=False, num_devices=1)
    ins = {k: nc.dram_tensor(f"in_{k}", v.shape, F32, kind="ExternalInput").ap() for k, v in arrays.items()}
    out = nc.dram_tensor("tokens", (TOKENS, D), F32, kind="ExternalOutput").ap()
    patch_dram = nc.dram_tensor("patch_sums", (CHANNELS, TOKENS), F32, kind="Internal").ap()
    rows = nc.dram_tensor("placed_rows", (MOST_PLACES * P, D), F32, kind="Internal").ap()
    results = nc.dram_tensor("results", (MOST_PLACES * P, D), F32, kind="Internal").ap()
    tower(nc, ins, out, patch_dram, rows, results)
    result = run_bass_kernel_spmd(nc, [{f"in_{k}": v for k, v in arrays.items()}], core_ids=[0])
    return result.results[0]["tokens"].reshape(IMAGES, SEQ, D)
```

```python
from contextlib import ExitStack

import concourse.bass as bass
import concourse.mybir as mybir
import numpy as np

F32, U32, I32 = mybir.dt.float32, mybir.dt.uint32, mybir.dt.int32
ALU = mybir.AluOpType
ACT = mybir.ActivationFunctionType
AX = mybir.AxisListType.X
ds = bass.ds

IMAGES, CHANNELS, SIDE, PATCH = 64, 3, 96, 16
GRID = SIDE // PATCH
SEQ = GRID * GRID
TOKENS = IMAGES * SEQ
D = 192
FP = 96
FC = D // FP
P = 128
TILES = TOKENS // P
HEADS, HEAD = 12, 16
PAIRS = IMAGES // 2
PAIR = 2 * SEQ
HPC = FP // HEAD
GROUP = 3
GROUPS = HEADS // GROUP
SECOND = 64
CHUNK = 384
CHUNKS = TOKENS // CHUNK
NEG = -1e30
EPS = 1e-5


RING = 6
FILL = 4


def most_places(experts, top):
    tiles = top * TILES + experts - 1
    return tiles + tiles % 2


MOST_PLACES = most_places(16, 4)


LEAD = 4


class Signal:

    def __init__(self, sem, lead=LEAD):
        self.sem, self.base = sem, lead

    def at(self, n):
        return self.base + n

    def close(self, n):
        self.base += n


def link(eng, done, ins, n):
    ins.then_inc(done.sem, 1)
    eng.wait_ge(done.sem, done.at(n))


def tile(buf, t, width=D):
    return buf[:, ds(t * width, width)]


def token_phase(nc, m, s, ins):
    rows = IMAGES * GRID
    parts = rows // P
    width = CHANNELS * SIDE
    with (
        nc.sbuf_tensor("image", [P, parts, CHANNELS, PATCH * SIDE], F32) as image,
        nc.sbuf_tensor("column_sum", [P, parts, width], F32) as column_sum,
        nc.sbuf_tensor("patch_sum", [P, parts, CHANNELS * GRID], F32) as patch_sum,
        nc.sbuf_tensor("patchT", [CHANNELS, TOKENS], F32) as patchT,
        nc.sbuf_tensor("patch_tile", [CHANNELS, 2, P], F32) as patch_tile,
        nc.Block(no_gpsimd_drain=True) as block,
    ):
        x = ins["x"]

        @block.sync
        def _(sp):
            for i in range(parts):
                for c in range(CHANNELS):
                    sp.dma_start(image[:, i, c, :], x[c, i * P:(i + 1) * P, :]).then_inc(s.image[i].sem, 16)
            sp.dma_start(m.attention_w[1][:, :, 0:4 * D], ins["rwkv"]).then_inc(s.attention_w.sem, 16)
            load_attention(sp, m, s, ins, 0)
            sp.wait_ge(s.patch.sem, s.patch.at(parts))
            for c in range(CHANNELS):
                sp.dma_start(
                    m.patch_dram[c:c + 1, :].rearrange("c (i r g) -> r (c i) g", i=parts, g=GRID),
                    patch_sum[:, :, c * GRID:(c + 1) * GRID],
                ).then_inc(s.patch_store.sem, 16)
            sp.wait_ge(s.patch_store.sem, s.patch_store.at(16 * CHANNELS))
            sp.dma_start(patchT[:, :], m.patch_dram[:, :]).then_inc(s.patch_load.sem, 16)

        @block.vector
        def _(vec):
            n = 0
            for i in range(parts):
                vec.wait_ge(s.image[i].sem, s.image[i].at(16 * CHANNELS))
                acc = column_sum[:, i, :].rearrange("p (c w) -> p c w", c=CHANNELS)
                for r in range(PATCH):
                    line = image[:, i, :, r * SIDE:(r + 1) * SIDE]
                    if r == 0:
                        last = vec.tensor_scalar(acc, line, m.W1[:, 0:1], m.b1[:, 0:1], ALU.mult, ALU.add)
                    else:
                        last = vec.scalar_tensor_tensor(acc, line, m.W1[:, r:r + 1], acc, ALU.mult, ALU.add)
                    n += 1
                    link(vec, s.vec, last, n)
                each = column_sum[:, i, :].rearrange("p (g q) -> p g q", q=PATCH)
                n += 1
                link(vec, s.vec, vec.tensor_tensor(
                    each, each, m.W2[:, :].unsqueeze(1).to_broadcast([P, CHANNELS * GRID, PATCH]), ALU.mult), n)
                n += 1
                link(vec, s.vec, vec.tensor_reduce(patch_sum[:, i, :], each, AX, ALU.add), n)
                vec.tensor_scalar(patch_sum[:, i, :], patch_sum[:, i, :], m.b2[:, 0:1], None,
                                  ALU.add).then_inc(s.patch.sem, 1)
            with vec.Fori(0, TILES - 1, 2) as t:
                for p in range(2):
                    vec.wait_ge(s.mm.sem, s.mm.at(t + p + 1))
                    vec.tensor_tensor(tile(m.h, t + p), m.ps[p][:, 0:D], m.b3[:, :], ALU.add).then_inc(s.out.sem, 1)
                for p in range(2):
                    vec.wait_ge(s.out.sem, s.out.at(t + p + 1))
                    vec.bn_stats(tile(m.stats, t + p, 6), tile(m.h, t + p)).then_inc(s.stats.sem, 1)
            vec.wait_ge(s.stats.sem, s.stats.at(TILES))
            m.vec_links = n

        @block.scalar
        def _(act):
            act.wait_ge(s.patch_load.sem, s.patch_load.at(16))
            with act.Fori(0, TILES - 5, 6) as t:
                for p in range(6):
                    act.wait_ge(s.mm.sem, s.mm.at(t + p - 1))
                    act.activation(patch_tile[:, p % 2, :], patchT[:, ds((t + p) * P, P)], ACT.Copy).then_inc(s.stage.sem, 1)

        @block.tensor
        def _(pe):
            with pe.Fori(0, TILES - 1, 2) as t:
                for p in range(2):
                    pe.wait_ge(s.stage.sem, s.stage.at(t + p + 1))
                    pe.wait_ge(s.out.sem, s.out.at(t + p - 1))
                    pe.matmul(m.ps[p][:, 0:D], patch_tile[:, p, :], m.W3[:, :], start=True, stop=True).then_inc(s.mm.sem, 1)
    s.vec.close(m.vec_links)
    for signal, n in ((s.mm, TILES), (s.stage, TILES), (s.out, TILES), (s.stats, TILES)):
        signal.close(n)


def feature_phase(nc, m, s, src, norm=True, keep=None, scale=None, shift=None, router=None, keep_turned=True,
                  measured=False):
    experts = router[2] if router else 0
    with nc.Block(no_gpsimd_drain=True) as block:

        @block.vector
        def _(vec):
            if norm:
                if not measured:
                    with vec.Fori(0, TILES) as t:
                        vec.bn_stats(tile(m.stats, t, 6), tile(src, t)).then_inc(s.stats.sem, 1)
                    vec.wait_ge(s.stats.sem, s.stats.at(TILES))
                half = m.stats[:, :].rearrange("p (t k) -> p t k", k=6)
                mean, other, rstd = m.mean[:, :], m.other[:, :], m.rstd[:, :]
                link(vec, s.vec, vec.tensor_tensor(mean, half[:, :, 1], half[:, :, 4], ALU.add), 1)
                link(vec, s.vec, vec.tensor_tensor(other, half[:, :, 1], half[:, :, 4], ALU.subtract), 2)
                link(vec, s.vec, vec.tensor_scalar(mean, mean, 0.5, None, ALU.mult), 3)
                link(vec, s.vec, vec.scalar_tensor_tensor(other, other, 0.25, other, ALU.mult, ALU.mult), 4)
                link(vec, s.vec, vec.tensor_tensor(rstd, half[:, :, 2], half[:, :, 5], ALU.add), 5)
                link(vec, s.vec, vec.scalar_tensor_tensor(rstd, rstd, 1.0 / D, other, ALU.mult, ALU.add), 6)
                vec.tensor_scalar(rstd, rstd, EPS, None, ALU.add).then_inc(s.var.sem, 1)
                vec.wait_ge(s.std.sem, s.std.at(1))
                link(vec, s.vec, vec.reciprocal(rstd, rstd), 7)

            def logits(t, p):
                vec.wait_ge(s.route.sem, s.route.at(t + 1))
                out = m.logits[:, ds(t * experts, experts)]
                if router[1] is None:
                    vec.tensor_copy(out, m.ps[2 + p][:, 0:experts]).then_inc(s.logit.sem, 1)
                else:
                    vec.tensor_tensor(out, m.ps[2 + p][:, 0:experts], router[1], ALU.add).then_inc(s.logit.sem, 1)

            def rows(t, p):
                vec.wait_ge(s.turned.sem, s.turned.at(t - 1))
                x = m.x_tile[:, p, :]
                if norm:
                    vec.tensor_scalar(x, tile(src, t), m.mean[:, ds(t, 1)], m.rstd[:, ds(t, 1)],
                                      ALU.subtract, ALU.mult).then_inc(s.x.sem, 1)
                else:
                    vec.tensor_copy(x, tile(src, t)).then_inc(s.x.sem, 1)
                if keep is not None:
                    vec.wait_ge(s.x.sem, s.x.at(t + 1))
                    vec.tensor_copy(tile(keep, t), x).then_inc(s.kept.sem, 1)

            for p in range(2):
                rows(p, p)
            with vec.Fori(2, TILES - 1, 2) as t:
                for p in range(2):
                    rows(t + p, p)
                if router:
                    for p in range(2):
                        logits(t + (p - 2), p)
            if router:
                for p in range(2):
                    logits(TILES - 2 + p, p)

        @block.scalar
        def _(act):
            if norm:
                act.wait_ge(s.var.sem, s.var.at(1))
                act.activation(m.rstd[:, :], m.rstd[:, :], ACT.Sqrt).then_inc(s.std.sem, 1)
            with act.Fori(0, TILES - 5, 6) as t:
                for p in range(6):
                    act.wait_ge(s.turned.sem, s.turned.at(t + p + 1))
                    if router:
                        act.wait_ge(s.route.sem, s.route.at(t + p - 1))
                    bank = m.ps[p % 2][0:FP, 0:FC * P].rearrange("f (c k) -> f c k", c=FC)
                    for c in range(FC):
                        outs = [m.xs[:, p % 2, c, :]] if router else []
                        if keep_turned:
                            outs.append(m.xT[:, c, ds((t + p) * P, P)])
                        for out in outs:
                            if scale is None:
                                last = act.activation(out, bank[:, c, :], ACT.Copy)
                            else:
                                last = act.activation(out, bank[:, c, :], ACT.Identity,
                                                      bias=shift[:, c:c + 1], scale=scale[:, c:c + 1])
                    last.then_inc(s.xT.sem, 1)

        @block.tensor
        def _(pe):
            def route(t, p):
                pe.wait_ge(s.xT.sem, s.xT.at(t + 1))
                pe.wait_ge(s.logit.sem, s.logit.at(t - 1))
                for c in range(FC):
                    last = pe.matmul(m.ps[2 + p][:, 0:experts], m.xs[:, p, c, :], router[0][:, c, :],
                                     start=(c == 0), stop=(c == FC - 1))
                last.then_inc(s.route.sem, 1)

            def turn_rows(t, p):
                pe.wait_ge(s.x.sem, s.x.at(t + 1))
                pe.wait_ge(s.xT.sem, s.xT.at(t - 1))
                for c in range(FC):
                    last = pe.matmul(m.ps[p][0:FP, c * P:(c + 1) * P], m.x_tile[:, p, c * FP:(c + 1) * FP],
                                     m.ident[:, :], start=True, stop=True, is_transpose=True)
                last.then_inc(s.turned.sem, 1)

            turn_rows(0, 0)
            if router:
                with pe.Fori(1, TILES - 2, 2) as t:
                    for p in range(2):
                        turn_rows(t + p, 1 - p)
                        route(t + (p - 1), p)
                turn_rows(TILES - 1, 1)
                route(TILES - 2, 0)
                route(TILES - 1, 1)
            else:
                with pe.Fori(1, TILES - 2, 2) as t:
                    for p in range(2):
                        turn_rows(t + p, 1 - p)
                turn_rows(TILES - 1, 1)
    closing = [(s.x, TILES), (s.turned, TILES), (s.xT, TILES)]
    if norm:
        closing += [(s.vec, 7), (s.var, 1), (s.std, 1)]
        if not measured:
            closing += [(s.stats, TILES)]
    if keep is not None:
        closing += [(s.kept, TILES)]
    if router:
        closing += [(s.route, TILES), (s.logit, TILES)]
    for signal, n in closing:
        signal.close(n)


def project_phase(nc, m, s, weights, dst, bias=None, measure=True):
    with nc.Block(no_gpsimd_drain=True) as block:

        @block.scalar
        def _(act):
            with act.Fori(0, TILES - 5, 6) as t:
                for p in range(6):
                    act.wait_ge(s.mm.sem, s.mm.at(t + p - 1))
                    act.activation(m.xs[:, p % 2, :, :], m.xT[:, :, ds((t + p) * P, P)], ACT.Copy).then_inc(s.stage.sem, 1)

        @block.tensor
        def _(pe):
            with pe.Fori(0, TILES - 1, 2) as t:
                for p in range(2):
                    pe.wait_ge(s.stage.sem, s.stage.at(t + p + 1))
                    pe.wait_ge(s.out.sem, s.out.at(t + p - 1))
                    for c in range(FC):
                        last = pe.matmul(m.ps[p][:, 0:D], m.xs[:, p, c, :], weights[:, c, :],
                                         start=(c == 0), stop=(c == FC - 1))
                    last.then_inc(s.mm.sem, 1)

        @block.vector
        def _(vec):
            if bias is not None:
                all_tiles = dst[:, :].rearrange("p (t d) -> p t d", d=D)
                link(vec, s.vec, vec.tensor_tensor(all_tiles, all_tiles,
                                                   bias.unsqueeze(1).to_broadcast([P, TILES, D]), ALU.add), 1)
            with vec.Fori(0, TILES - 1, 2) as t:
                for p in range(2):
                    vec.wait_ge(s.mm.sem, s.mm.at(t + p + 1))
                    vec.tensor_tensor(tile(dst, t + p), m.ps[p][:, 0:D], tile(dst, t + p),
                                      ALU.add).then_inc(s.out.sem, 1)
                if measure:
                    for p in range(2):
                        vec.wait_ge(s.out.sem, s.out.at(t + p + 1))
                        vec.bn_stats(tile(m.stats, t + p, 6), tile(dst, t + p)).then_inc(s.stats.sem, 1)
            if measure:
                vec.wait_ge(s.stats.sem, s.stats.at(TILES))
    if bias is not None:
        s.vec.close(1)
    if measure:
        s.stats.close(TILES)
    for signal, n in ((s.mm, TILES), (s.stage, TILES), (s.out, TILES)):
        signal.close(n)


def store_phase(nc, s, src, out):
    with nc.Block(no_gpsimd_drain=True) as block:

        @block.sync
        def _(sp):
            sp.dma_start(out.rearrange("(t p) d -> p t d", p=P),
                         src[:, :].rearrange("p (t d) -> p t d", d=D)).then_inc(s.store.sem, 16)
            sp.wait_ge(s.store.sem, 16)


def add_phase(nc, m, s, dst, src):
    with nc.Block(no_gpsimd_drain=True) as block:

        @block.vector
        def _(vec):
            vec.tensor_tensor(dst[:, :], dst[:, :], src[:, :], ALU.add).then_inc(s.out.sem, 1)
            vec.wait_ge(s.out.sem, s.out.at(1))
            with vec.Fori(0, TILES) as t:
                vec.bn_stats(tile(m.stats, t, 6), tile(dst, t)).then_inc(s.stats.sem, 1)
            vec.wait_ge(s.stats.sem, s.stats.at(TILES))
    s.out.close(1)
    s.stats.close(TILES)


def load_attention(sp, m, s, ins, layer):
    n = ins[f"attention{layer}"].shape[2]
    sp.dma_start(m.attention_w[layer % 2][:, :, 0:n], ins[f"attention{layer}"]).then_inc(s.attention_w.sem, 16)


def attention_phase(nc, m, s, layer, kind, bias=None, prefetch=None):
    w = m.attention_w[layer % 2]
    Wq, Wk, Wv = (w[:, :, j * D:(j + 1) * D] for j in range(3))
    Wq_turned, Wk_turned = (w[:, :, j * D:(j + 1) * D] for j in (4, 5))
    rotary = kind == "erf"
    qbias, kbias, vbias = bias or (m.zero_bias,) * 3
    psQ, psK, psV, psS, psT, psC, psX, psR = m.ps
    spread = [FP, HPC, PAIR]
    read = s.scored if kind == "causal" else s.shifted
    lanes = HPC * SEQ

    def both(bank):
        return bank[0:FP, 0:FC * PAIR].rearrange("f (c k) -> f c k", c=FC)

    with (
        nc.sbuf_tensor(f"x_pair_{layer}", [FP, 2, FC, PAIR], F32) as x_pair,
        nc.sbuf_tensor(f"x_tripled_{layer}", [FP, 2, FC, 2, GROUP * SEQ], F32) as x_tripled,
        nc.sbuf_tensor(f"qT_{layer}", [FP, 2, FC, SECOND + SEQ], F32) as qT,
        nc.sbuf_tensor(f"k_rot_{layer}", [FP, 2, FC, PAIR], F32) as k_rot,
        nc.sbuf_tensor(f"rot_tmp_{layer}", [FP, 4, FC, PAIR], F32) as rot_tmp,
        nc.sbuf_tensor(f"k_spread_{layer}", [FP, 2, FC, HPC, PAIR], F32) as k_spread,
        nc.sbuf_tensor(f"v_spread_{layer}", [GROUP * SEQ, 2, 2, D], F32) as v_spread,
        nc.sbuf_tensor(f"weight_{layer}", [P, 2, HEADS * SEQ], F32) as weight,
        nc.sbuf_tensor(f"erf_tmp_{layer}", [P, 2, HEADS * SEQ], F32) as erf_tmp,
        nc.sbuf_tensor(f"inverse_{layer}", [P, 2, HEADS * SEQ if kind == "erf" else 1], F32) as inverse,
        nc.sbuf_tensor(f"weightT_{layer}", [GROUP * SEQ, 2, GROUPS, P], F32) as weightT,
        nc.sbuf_tensor(f"row_max_{layer}", [P, 2, HEADS], F32) as row_max,
        nc.sbuf_tensor(f"row_sum_{layer}", [P, 2, HEADS], F32) as row_sum,
        nc.sbuf_tensor(f"context_{layer}", [P, 2, D], F32) as context,
        nc.Block(no_gpsimd_drain=True) as block,
    ):
        FIRST, LAST = 4, 30

        def turns(eng, turn):
            for i in range(FIRST):
                turn(i, i % 2)
            with eng.Fori(FIRST, LAST - 1, 2) as i:
                for p in range(2):
                    turn(i + p, p)
            for i in range(LAST, PAIRS + 3):
                turn(i, i % 2)

        def has(i):
            return not isinstance(i, int) or 0 <= i < PAIRS

        @block.tensor
        def _(pe):
            def scores(i, p):
                pe.wait_ge(s.q.sem, s.q.at(i + 1))
                pe.wait_ge(s.k.sem, s.k.at(i + 1))
                pe.wait_ge(read.sem, read.at(i))
                for c in range(FC):
                    for b in range(2):
                        last = pe.matmul(psS[b * SECOND:b * SECOND + SECOND, c * lanes:(c + 1) * lanes],
                                         qT[:, p, c, b * SEQ:b * SEQ + SECOND],
                                         k_spread[:, p, c, :, b * SEQ:(b + 1) * SEQ], start=True, stop=True)
                last.then_inc(s.scores.sem, 1)

            def turn_weights(i, p):
                pe.wait_ge(s.weight.sem, s.weight.at(i + 1))
                pe.wait_ge(s.weightT.sem, s.weightT.at(i))
                for g in range(GROUPS):
                    n = GROUP * SEQ
                    last = pe.matmul(psT[0:n, g * P:(g + 1) * P], weight[:, p, g * n:(g + 1) * n], m.ident[:, :],
                                     start=True, stop=True, is_transpose=True)
                last.then_inc(s.turned.sem, 1)

            def projections(i, p):
                pe.wait_ge(s.stage.sem, s.stage.at(i + 1))
                pe.wait_ge(s.q.sem, s.q.at(i))
                pe.wait_ge(s.k.sem, s.k.at(i))
                pairs = [(psQ, Wq), (psK, Wk)] + [(psX, Wq_turned), (psR, Wk_turned)] * rotary
                for bank, weights in pairs:
                    if bank is psX:
                        pe.wait_ge(s.context_out.sem, s.context_out.at(i - 3))
                    for out in range(FC):
                        for c in range(FC):
                            last = pe.matmul(both(bank)[:, out, :], weights[:, c, out * FP:(out + 1) * FP],
                                             x_pair[:, p, c, :], start=(c == 0), stop=(c == FC - 1))
                last.then_inc(s.projected.sem, 1)

            def values(i, p):
                pe.wait_ge(s.v.sem, s.v.at(i))
                pe.wait_ge(s.tripled.sem, s.tripled.at(i + 1))
                for b in range(2):
                    for c in range(FC):
                        last = pe.matmul(psV[0:GROUP * SEQ, b * D:(b + 1) * D], x_tripled[:, p, c, b, :], Wv[:, c, :],
                                         start=(c == 0), stop=(c == FC - 1))
                last.then_inc(s.valued.sem, 1)

            def weigh(i, p):
                pe.wait_ge(s.weightT.sem, s.weightT.at(i + 1))
                pe.wait_ge(s.v.sem, s.v.at(i + 1))
                pe.wait_ge(s.context.sem, s.context.at(i))
                for g in range(GROUPS):
                    for b in range(2):
                        cols = slice(g * GROUP * HEAD, (g + 1) * GROUP * HEAD)
                        last = pe.matmul(psC[b * SECOND:b * SECOND + SECOND, cols],
                                         weightT[:, p, g, b * SECOND:b * SECOND + SECOND],
                                         v_spread[:, p, b, cols], start=True, stop=True)
                last.then_inc(s.weighed.sem, 1)

            def turn_context(i, p):
                pe.wait_ge(s.context.sem, s.context.at(i + 1))
                pe.wait_ge(s.context_out.sem, s.context_out.at(i))
                if rotary:
                    pe.wait_ge(s.q.sem, s.q.at(min(i + 4, PAIRS) if isinstance(i, int) else i + 4))
                for c in range(FC):
                    last = pe.matmul(psX[0:FP, c * P:(c + 1) * P], context[:, p, c * FP:(c + 1) * FP], m.ident[:, :],
                                     start=True, stop=True, is_transpose=True)
                last.then_inc(s.context_turned.sem, 1)

            def turn(i, p):
                if has(i - 1):
                    scores(i - 1, 1 - p)
                if not rotary and has(i - 2):
                    turn_weights(i - 2, p)
                if has(i):
                    projections(i, p)
                if rotary and has(i - 2):
                    turn_weights(i - 2, p)
                if has(i):
                    values(i, p)
                if has(i - 2):
                    weigh(i - 2, p)
                if has(i - 3):
                    turn_context(i - 3, 1 - p)

            pe.wait_ge(s.attention_w.sem, s.attention_w.at(16 * (layer + 2)))
            turns(pe, turn)

        @block.gpsimd
        def _(pool):
            def triple(i, p):
                pool.wait_ge(s.valued.sem, s.valued.at(i - 1))
                for c in range(FC):
                    for b in range(2):
                        last = pool.tensor_copy(
                            x_tripled[:, p, c, b, :].rearrange("f (r k) -> f r k", r=GROUP),
                            m.xT[:, c, ds(i * PAIR + b * SEQ, SEQ)].unsqueeze(1).to_broadcast([FP, GROUP, SEQ]))
                last.then_inc(s.tripled.sem, 1)

            def weights(i, p):
                x = weight[:, p, :].rearrange("q (h k) -> q h k", h=HEADS)
                pool.wait_ge(s.gelu.sem, s.gelu.at(i + 1))
                pool.wait_ge(s.inverted.sem, s.inverted.at(i + 1))
                link(pool, s.soft, pool.tensor_tensor(weight[:, p, :], erf_tmp[:, p, :], inverse[:, p, :], ALU.mult), i + 1)
                pool.tensor_tensor(x, x, m.causal_two[:, :].unsqueeze(1).to_broadcast([P, HEADS, SEQ]),
                                   ALU.mult).then_inc(s.weight.sem, 1)

            def turn(i, p):
                if has(i):
                    triple(i, p)
                if rotary and has(i - 1):
                    weights(i - 1, 1 - p)

            turns(pool, turn)

        @block.scalar
        def _(act):
            def stage(i, p):
                act.wait_ge(s.projected.sem, s.projected.at(i - 1))
                act.activation(x_pair[:, p, :, :], m.xT[:, :, ds(i * PAIR, PAIR)], ACT.Copy).then_inc(s.stage.sem, 1)

            def queries(i, p):
                act.wait_ge(s.projected.sem, s.projected.at(i + 1))
                act.wait_ge(s.scores.sem, s.scores.at(i - 1))
                for c in range(FC):
                    last = act.activation(qT[:, p, c, 0:PAIR], both(psQ)[:, c, :], ACT.Identity,
                                          bias=qbias[:, c:c + 1])
                last.then_inc(s.q.sem, 1)

            def exponentials(i, p):
                act.wait_ge(s.shifted.sem, s.shifted.at(i + 1))
                if kind == "erf":
                    act.activation(erf_tmp[:, p, :], weight[:, p, :], ACT.Gelu).then_inc(s.gelu.sem, 1)
                else:
                    act.activation(weight[:, p, :], weight[:, p, :], ACT.Exp, scale=0.25).then_inc(s.weight.sem, 1)

            def weights_out(i, p):
                act.wait_ge(s.turned.sem, s.turned.at(i + 1))
                act.wait_ge(s.weighed.sem, s.weighed.at(i - 1))
                act.activation(weightT[:, p, :, :], psT[0:GROUP * SEQ, 0:GROUPS * P].rearrange("k (g q) -> k g q", g=GROUPS),
                               ACT.Copy).then_inc(s.weightT.sem, 1)

            def context_out(i, p):
                act.wait_ge(s.context_turned.sem, s.context_turned.at(i + 1))
                for c in range(FC):
                    rows = psX[0:FP, c * P:(c + 1) * P].rearrange("f (b k) -> f b k", b=2)[:, :, 0:SEQ]
                    last = act.activation(m.xT[:, c, ds(i * PAIR, PAIR)].rearrange("f (b k) -> f b k", b=2), rows,
                                          ACT.Identity, bias=vbias[:, c:c + 1])
                last.then_inc(s.context_out.sem, 1)

            def turn(i, p):
                if has(i - 2):
                    weights_out(i - 2, p)
                if has(i - 1):
                    exponentials(i - 1, 1 - p)
                if has(i + 1):
                    stage(i + 1, 1 - p)
                if has(i) and not rotary:
                    queries(i, p)
                if has(i - 3):
                    context_out(i - 3, 1 - p)

            stage(0, 0)
            turns(act, turn)

        @block.vector
        def _(vec):
            vec.memset(qT[:, :, :, PAIR:SECOND + SEQ], 0.0).then_inc(s.vec.sem, 1)
            count = 0 if kind == "plain" else {"causal": 1, "erf": 4}[kind]

            def spread_keys(i, p):
                vec.wait_ge(s.projected.sem, s.projected.at(i + 1))
                vec.wait_ge(s.scores.sem, s.scores.at(i - 1))
                for c in range(FC):
                    key = both(psK)[:, c, :] if not rotary else k_rot[:, p, c, :]
                    last = vec.scalar_tensor_tensor(
                        k_spread[:, p, c, :, :], key.unsqueeze(1).to_broadcast(spread), kbias[:, c:c + 1],
                        m.head_mask[:, :].unsqueeze(2).to_broadcast(spread), ALU.add, ALU.mult)
                last.then_inc(s.k.sem, 1)

            def rotate(i, p):
                vec.wait_ge(s.projected.sem, s.projected.at(i + 1))
                vec.wait_ge(s.scores.sem, s.scores.at(i - 1))
                shape = [FP, FC * 2, SEQ]
                cos = m.cos[:, :].unsqueeze(1).to_broadcast(shape)
                sin = m.sin[:, :].unsqueeze(1).to_broadcast(shape)

                def flat(a):
                    return a.rearrange("f (x k) -> f x k", k=SEQ)
                t = [rot_tmp[:, j, :, :].rearrange("f c (b k) -> f (c b) k", b=2) for j in range(4)]
                vec.tensor_tensor(t[0], flat(psQ[0:FP, 0:FC * PAIR]), cos, ALU.mult)
                vec.tensor_tensor(t[1], flat(psX[0:FP, 0:FC * PAIR]), sin, ALU.mult)
                vec.tensor_tensor(t[2], flat(psK[0:FP, 0:FC * PAIR]), cos, ALU.mult)
                vec.tensor_tensor(t[3], flat(psR[0:FP, 0:FC * PAIR]), sin, ALU.mult).then_inc(s.rot.sem, 1)
                vec.wait_ge(s.rot.sem, s.rot.at(2 * i + 1))
                vec.tensor_tensor(qT[:, p, :, 0:PAIR], rot_tmp[:, 0, :, :], rot_tmp[:, 1, :, :], ALU.add).then_inc(s.q.sem, 1)
                vec.tensor_tensor(k_rot[:, p, :, :], rot_tmp[:, 2, :, :], rot_tmp[:, 3, :, :], ALU.add).then_inc(s.rot.sem, 1)
                vec.wait_ge(s.rot.sem, s.rot.at(2 * i + 2))

            def spread_values(i, p):
                vec.wait_ge(s.valued.sem, s.valued.at(i + 1))
                vec.wait_ge(s.weighed.sem, s.weighed.at(i - 1))
                shape = [GROUP * SEQ, 2 * GROUPS, GROUP * HEAD]
                vec.tensor_tensor(v_spread[:, p, :, :].rearrange("k b (g n) -> k (b g) n", g=GROUPS),
                                  psV[0:GROUP * SEQ, 0:2 * D].rearrange("k (x n) -> k x n", n=GROUP * HEAD),
                                  m.value_mask[:, :].unsqueeze(1).to_broadcast(shape), ALU.mult).then_inc(s.v.sem, 1)

            by_head = [P, HEADS, SEQ]

            def shift(i, p):
                vec.wait_ge(s.scores.sem, s.scores.at(i + 1))
                vec.wait_ge(s.turned.sem, s.turned.at(i - 1))
                x = weight[:, p, :].rearrange("q (h k) -> q h k", h=HEADS)
                ps = psS[:, 0:HEADS * SEQ].rearrange("q (h k) -> q h k", h=HEADS)
                mask = m.causal[:, :].unsqueeze(1).to_broadcast(by_head)
                if kind == "erf":
                    link(vec, s.scored, vec.tensor_scalar(erf_tmp[:, p, :], psS[:, 0:HEADS * SEQ], 0.0, 1e-20,
                                                          ALU.is_equal, ALU.mult), i + 1)
                    vec.scalar_tensor_tensor(weight[:, p, :], psS[:, 0:HEADS * SEQ], 0.25 * 2.0 ** 0.5,
                                             erf_tmp[:, p, :], ALU.mult, ALU.add).then_inc(s.shifted.sem, 1)
                    return
                src = ps
                if kind == "causal":
                    vec.tensor_tensor(x, ps, mask, ALU.add).then_inc(s.scored.sem, 1)
                    vec.wait_ge(s.scored.sem, s.scored.at(i + 1))
                    src = x
                link(vec, s.soft, vec.tensor_reduce(row_max[:, p, :], src, AX, ALU.max), 2 * i + 1)
                last = vec.tensor_tensor(x, src, row_max[:, p, :].unsqueeze(2).to_broadcast(by_head), ALU.subtract)
                last.then_inc(s.shifted.sem, 1)

            def invert(i, p):
                vec.wait_ge(s.shifted.sem, s.shifted.at(i + 1))
                vec.wait_ge(s.weight.sem, s.weight.at(i - 1))
                vec.reciprocal(inverse[:, p, :], weight[:, p, :]).then_inc(s.inverted.sem, 1)

            def total(i, p):
                x = weight[:, p, :].rearrange("q (h k) -> q h k", h=HEADS)
                vec.wait_ge(s.weight.sem, s.weight.at(i + 1))
                if kind == "erf":
                    link(vec, s.sums, vec.tensor_reduce(row_sum[:, p, :], x, AX, ALU.add), 2 * i + 1)
                    link(vec, s.sums, vec.tensor_scalar(row_sum[:, p, :], row_sum[:, p, :], 1e-6, None, ALU.max),
                         2 * i + 2)
                else:
                    link(vec, s.soft, vec.tensor_reduce(row_sum[:, p, :], x, AX, ALU.add), 2 * i + 2)
                vec.reciprocal(row_sum[:, p, :], row_sum[:, p, :]).then_inc(s.inverse.sem, 1)

            def normalise(i, p):
                vec.wait_ge(s.inverse.sem, s.inverse.at(i + 1))
                vec.wait_ge(s.weighed.sem, s.weighed.at(i + 1))
                vec.wait_ge(s.context_turned.sem, s.context_turned.at(i - 1))
                shape = [P, HEADS, HEAD]
                vec.tensor_tensor(context[:, p, :].rearrange("q (h d) -> q h d", h=HEADS),
                                  psC[:, 0:D].rearrange("q (h d) -> q h d", h=HEADS),
                                  row_sum[:, p, :].unsqueeze(2).to_broadcast(shape), ALU.mult).then_inc(s.context.sem, 1)

            def turn(i, p):
                if has(i - 1):
                    shift(i - 1, 1 - p)
                if rotary and has(i - 1):
                    invert(i - 1, 1 - p)
                if has(i):
                    if rotary:
                        rotate(i, p)
                    spread_keys(i, p)
                    spread_values(i, p)
                if rotary and has(i - 2):
                    total(i - 2, p)
                if not rotary and has(i - 1):
                    total(i - 1, 1 - p)
                if has(i - 2):
                    normalise(i - 2, p)

            vec.wait_ge(s.vec.sem, s.vec.at(1))
            turns(vec, turn)

        @block.sync
        def _(sp):
            if prefetch:
                prefetch(sp)
    n = PAIRS
    for signal in (s.q, s.k, s.v, s.tripled, s.scores, s.weight, s.weightT, s.turned, s.stage, s.projected, s.valued,
                   s.context, s.context_turned, s.context_out, s.weighed, s.shifted, s.inverse):
        signal.close(n)
    if kind != "plain":
        s.scored.close(n)
    s.vec.close(1)
    s.soft.close((1 if kind == "erf" else 2) * n)
    if kind == "erf":
        s.gelu.close(n)
        s.inverted.close(n)
        s.sums.close(2 * n)
        s.rot.close(2 * n)


class Steps:

    def __init__(self, vec, done, n=0):
        self.vec, self.done, self.n = vec, done, n

    def __call__(self, ins):
        self.n += 1
        link(self.vec, self.done, ins, self.n)


def rwkv_phase(nc, m, s):
    at_once = 16
    turns = IMAGES // at_once
    n_tok = at_once * SEQ
    width = SEQ + 1
    half = at_once // 2
    w = m.attention_w[1]
    STEPS = 14
    with ExitStack() as ctx:
        def buf(name, shape):
            return ctx.enter_context(nc.sbuf_tensor("rwkv_" + name, shape, F32))

        xpad = buf("xpad", [FP, FC, IMAGES, width])
        mixed = buf("mixed", [FP, 3, FC, at_once, SEQ])
        decay, kp, vp, mx, ea, eb, num, den = (
            buf(x, [FP, FC, at_once, width]) for x in ("decay", "kp", "vp", "mx", "ea", "eb", "num", "den"))
        zeros = buf("zeros", [P, FILL * D])
        er, t1, t2, t3 = (buf(x, [FP, FC, at_once, SEQ]) for x in ("er", "t1", "t2", "t3"))
        block = ctx.enter_context(nc.Block(no_gpsimd_drain=True))

        def rows(b):
            return b[:, :, :, :].rearrange("f c b k -> f (c b) k")

        def now(b):
            return rows(b)[:, :, 1:width]

        def before(b):
            return rows(b)[:, :, 0:SEQ]

        def line(b):
            return b[:, :, :, :].rearrange("f c b k -> f (c b k)")

        @block.sync
        def _(sp):
            sp.wait_ge(s.cleared.sem, s.cleared.at(1))
            with sp.Fori(0, MOST_PLACES // FILL) as i:
                sp.dma_start(m.rows[ds(i * (FILL * P), FILL * P), :].rearrange("(k p) d -> p k d", p=P),
                             zeros[:, :].rearrange("p (k d) -> p k d", d=D)).then_inc(s.filled.sem, 16)
            sp.wait_ge(s.filled.sem, 16 * (MOST_PLACES // FILL))

        @block.vector
        def _(vec):
            vec.memset(zeros[:, :], 0.0).then_inc(s.cleared.sem, 1)
            vec.memset(xpad[:, :, :, 0:1], 0.0)
            for b, value in ((kp, -1e38), (vp, 0.0), (ea, 0.0), (eb, 0.0), (decay, -2e38)):
                vec.memset(b[:, :, :, 0:1], value)
            vec.wait_ge(s.exps.sem, s.exps.at(1))
            for c in range(FC):
                vec.tensor_scalar(decay[:, c, :, 1:width], m.decay[:, c:c + 1].unsqueeze(2).to_broadcast([FP, at_once, SEQ]),
                                  -1.0, None, ALU.mult)
                vec.tensor_copy(xpad[:, c, :, 1:width],
                                m.xT[:, c, :].rearrange("f (b k) -> f b k", k=SEQ)).then_inc(s.x.sem, 1)
            link(vec, s.vec, vec.tensor_scalar(m.unmix[:, :], m.mix[:, :], -1.0, 1.0, ALU.mult, ALU.add), 1)
            def mix(g):
                vec.wait_ge(s.mixed.sem, s.mixed.at(g + 1))
                for j in range(3):
                    for c in range(FC):
                        last = vec.scalar_tensor_tensor(
                            mixed[:, j, c, :, :], xpad[:, c, ds(g * at_once, at_once), 0:SEQ],
                            m.unmix[:, j * FC + c:j * FC + c + 1], mixed[:, j, c, :, :], ALU.mult, ALU.add)
                last.then_inc(s.stage.sem, 1)

            def turn(g, more):
                step = Steps(vec, s.vec, g * STEPS + 1)
                vec.wait_ge(s.k.sem, s.k.at(g + 1))
                step(vec.tensor_tensor_scan(line(mx), line(decay), line(kp), 0.0, ALU.add, ALU.max))
                step(vec.tensor_tensor(now(ea), before(mx), now(decay), ALU.add))
                vec.tensor_tensor(now(ea), now(ea), now(mx), ALU.subtract)
                vec.tensor_tensor(now(eb), now(kp), now(mx), ALU.subtract).then_inc(s.shifted.sem, 1)
                for c in range(FC):
                    last = vec.tensor_scalar(t1[:, c, :, :], kp[:, c, :, 1:width], m.first[:, c:c + 1], None, ALU.add)
                step(last)
                step(vec.tensor_tensor(rows(t2), before(mx), rows(t1), ALU.max))
                vec.tensor_tensor(rows(t1), rows(t1), rows(t2), ALU.subtract)
                vec.tensor_tensor(rows(t2), before(mx), rows(t2), ALU.subtract).then_inc(s.scored.sem, 1)
                if more:
                    mix(g + 1)
                vec.wait_ge(s.exps.sem, s.exps.at(2 * g + 2))
                step(vec.tensor_tensor_scan(line(den), line(ea), line(eb), 0.0, ALU.mult, ALU.add))
                step(vec.tensor_tensor(now(eb), now(eb), now(vp), ALU.mult))
                step(vec.tensor_tensor_scan(line(num), line(ea), line(eb), 0.0, ALU.mult, ALU.add))
                vec.wait_ge(s.exps.sem, s.exps.at(2 * g + 3))
                step(vec.tensor_tensor(rows(t3), rows(t2), before(num), ALU.mult))
                step(vec.tensor_tensor(rows(t2), rows(t2), before(den), ALU.mult))
                step(vec.tensor_tensor(rows(t2), rows(t2), rows(t1), ALU.add))
                step(vec.tensor_tensor(rows(t1), rows(t1), now(vp), ALU.mult))
                step(vec.tensor_tensor(rows(t3), rows(t3), rows(t1), ALU.add))
                step(vec.scalar_tensor_tensor(rows(t2), rows(er), 1.0, rows(t2), ALU.add, ALU.mult))
                step(vec.reciprocal(rows(t2), rows(t2)))
                for c in range(FC):
                    last = vec.tensor_tensor(m.xT[:, c, ds(g * n_tok, n_tok)].rearrange("f (b k) -> f b k", k=SEQ),
                                             t3[:, c, :, :], t2[:, c, :, :], ALU.mult)
                last.then_inc(s.out.sem, 1)

            mix(0)
            with vec.Fori(0, turns - 1) as g:
                turn(g, True)
            turn(turns - 1, False)

        @block.tensor
        def _(pe):
            pe.wait_ge(s.attention_w.sem, s.attention_w.at(32))
            with pe.Fori(0, turns) as g:
                pe.wait_ge(s.stage.sem, s.stage.at(g + 1))
                for j in range(3):
                    if j == 0:
                        pe.wait_ge(s.r.sem, s.r.at(g))
                    elif j == 1:
                        pe.wait_ge(s.k.sem, s.k.at(g))
                    else:
                        pe.wait_ge(s.key_out.sem, s.key_out.at(g + 1))
                    for out in range(FC):
                        for b in range(2):
                            for c in range(FC):
                                last = pe.matmul(
                                    m.ps[4 * (j % 2) + 2 * out + b][0:FP, 0:half * SEQ],
                                    w[:, c, j * D + out * FP:j * D + (out + 1) * FP],
                                    mixed[:, j, c, b * half:(b + 1) * half, :].rearrange("f b k -> f (b k)"),
                                    start=(c == 0), stop=(c == FC - 1))
                    last.then_inc(s.mm.sem, 1)

        @block.scalar
        def _(act):
            act.activation(m.decay[:, :], m.decay[:, :], ACT.Exp).then_inc(s.exps.sem, 1)
            def mix(g):
                for j in range(3):
                    for c in range(FC):
                        last = act.activation(mixed[:, j, c, :, :], xpad[:, c, ds(g * at_once, at_once), 1:width],
                                              ACT.Copy, scale=m.mix[:, j * FC + c:j * FC + c + 1])
                last.then_inc(s.mixed.sem, 1)

            act.wait_ge(s.x.sem, s.x.at(FC))
            mix(0)

            def turn(g, more):
                def images(j, out, b):
                    return m.ps[4 * (j % 2) + 2 * out + b][0:FP, 0:half * SEQ].rearrange("f (b k) -> f b k", k=SEQ)

                for j, (dst, first) in enumerate(((kp, 1), (vp, 1), (er, 0))):
                    act.wait_ge(s.mm.sem, s.mm.at(3 * g + j + 1))
                    if j == 0:
                        act.wait_ge(s.out.sem, s.out.at(g))
                    for out in range(FC):
                        for b in range(2):
                            to = dst[:, out, b * half:(b + 1) * half, first:first + SEQ]
                            if j < 2:
                                last = act.activation(to, images(j, out, b), ACT.Copy)
                            else:
                                last = act.activation(to, images(j, out, b), ACT.Exp, scale=-1.0)
                    last.then_inc((s.key_out, s.k, s.r)[j].sem, 1)
                if more:
                    mix(g + 1)
                act.wait_ge(s.shifted.sem, s.shifted.at(g + 1))
                act.activation(now(ea), now(ea), ACT.Exp)
                act.activation(now(eb), now(eb), ACT.Exp).then_inc(s.exps.sem, 1)
                act.wait_ge(s.scored.sem, s.scored.at(g + 1))
                act.activation(rows(t1), rows(t1), ACT.Exp)
                act.activation(rows(t2), rows(t2), ACT.Exp).then_inc(s.exps.sem, 1)

            with act.Fori(0, turns - 1) as g:
                turn(g, True)
            turn(turns - 1, False)
    s.x.close(FC)
    s.mixed.close(turns)
    s.vec.close(1 + turns * STEPS)
    for signal in (s.stage, s.k, s.shifted, s.scored, s.out, s.r, s.key_out):
        signal.close(turns)
    s.mm.close(3 * turns)
    s.exps.close(2 * turns + 1)
    s.cleared.close(1)


def load_resident(sp, m, s, ins, ffn):
    loads = 0
    if ffn.joined:
        w = ins[ffn.name + "_w"]
        for e in range(ffn.experts):
            for rows in (slice(0, FP), slice(FP, FP + 1)):
                sp.dma_start(m.w1_all[rows, e * ffn.stride:(e + 1) * ffn.stride], w[e, rows, :]).then_inc(ffn.loaded.sem, 16)
                loads += 1
        ffn.loaded.close(16 * loads)
        return
    w1, w2 = ins[ffn.name + "_w1"], ins[ffn.name + "_w2"]
    for e in range(ffn.experts):
        sp.dma_start(m.expert_w1(ffn, e)[0:FP, :, :], w1[e, 0:FP, :, :]).then_inc(ffn.loaded.sem, 16)
        if w1.shape[1] > FP:
            sp.dma_start(m.expert_w1(ffn, e)[FP:FP + 1, :, :], w1[e, FP:FP + 1, :, :]).then_inc(ffn.loaded.sem, 16)
            loads += 1
        sp.dma_start(m.expert_w2(ffn, e)[0:ffn.block, :, :], w2[e, 0:ffn.block, :, :]).then_inc(ffn.loaded.sem, 16)
        loads += 2
    if ffn.out_bias is not None:
        n = ffn.out_bias.shape[1]
        sp.dma_start(ffn.out_bias[:, :], ins[ffn.name + "_b2"].to_broadcast([P, n])).then_inc(ffn.loaded.sem, 16)
        loads += 1
    if ffn.hidden_bias is not None:
        sp.dma_start(ffn.hidden_bias[:, :], ins[ffn.name + "_b1"]).then_inc(ffn.loaded.sem, 16)
        loads += 1
    ffn.loaded.close(16 * loads)


def expert_phase(nc, m, s, ffn, dst, first, experts, prefetch=None):
    gated = ffn.kind == "gate"
    func = {"gelu": ACT.Gelu, "silu": ACT.Silu, "gate": ACT.Silu}[ffn.kind]
    blocks = ffn.width // ffn.block
    rows = ffn.block
    w1 = [m.expert_w1(ffn, first + e) for e in range(experts)]
    w2 = [m.expert_w2(ffn, first + e) for e in range(experts)]
    tiles = CHUNK // P
    per = blocks * (2 if gated else 1)
    hidden_done = s.up_read if gated else s.act
    turn_blocks = CHUNKS * blocks
    BANKS = 2
    with (
        nc.sbuf_tensor(f"hT_{ffn.name}", [P, 2, blocks, CHUNK], F32) as hT,
        nc.sbuf_tensor(f"gate_{ffn.name}", [P, 2, CHUNK], F32) as gate,
        nc.sbuf_tensor(f"biased_{ffn.name}", [P, tiles, D], F32) as biased,
        nc.Block(no_gpsimd_drain=True) as block,
    ):

        def over_experts(eng, run):
            for e in range(experts):
                run(e)

        def over_chunks(eng, run):
            with eng.Fori(0, CHUNKS - 1, 2) as c:
                for p in range(2):
                    run(c + p, p)

        def turn_of(cp, j):
            return (cp * blocks + j) % BANKS

        def bank(kind, cp, j):
            return m.ps[(0 if kind == "hidden" else BANKS) + turn_of(cp, j)]

        @block.tensor
        def _(pe):
            pe.wait_ge(ffn.loaded.sem, ffn.loaded.base)

            def expert(e):

                def hidden(c, cp):
                    n = e * turn_blocks + c * blocks
                    for j in range(blocks):
                        x = [m.xT[:, k, ds(c * CHUNK, CHUNK)] for k in range(FC)]
                        pe.wait_ge(s.act.sem, s.act.at(n + (j - 1)))
                        if gated:
                            pe.wait_ge(s.up_read.sem, s.up_read.at(n + (j - 1)))
                        first = ffn.gate_at + j * rows if gated else j * rows
                        for k in range(FC):
                            last = pe.matmul(bank("hidden", cp, j)[0:rows, 0:CHUNK], w1[e][0:FP, k, first:first + rows], x[k],
                                             start=(k == 0), stop=(k == FC - 1))
                        if gated:
                            up = ffn.up_at + j * rows
                            for k in range(FC):
                                last = pe.matmul(bank("up", cp, j)[0:rows, 0:CHUNK], w1[e][0:FP, k, up:up + rows], x[k],
                                                 start=(k == 0), stop=(k == FC - 1))
                        last.then_inc(s.hidden.sem, 1)

                def output(c, cp):
                    n = e * CHUNKS + c
                    pe.wait_ge(hidden_done.sem, hidden_done.at(n * blocks + blocks))
                    for i in range(tiles):
                        pe.wait_ge(s.out.sem, s.out.at(n * tiles + (i - tiles + 1)))
                        for j in range(blocks):
                            last = pe.matmul(m.ps[2 * BANKS + i][:, 0:D], hT[0:rows, cp, j, i * P:(i + 1) * P],
                                             w2[e][0:rows, j, :], start=(j == 0), stop=(j == blocks - 1))
                        last.then_inc(s.mm.sem, 1)

                with pe.Fori(0, CHUNKS - 1, 2) as c:
                    hidden(c, 0)
                    hidden(c + 1, 1)
                    output(c, 0)
                    output(c + 1, 1)

            over_experts(pe, expert)

        @block.scalar
        def _(act):
            def expert(e):
                def chunk(c, cp):
                    n = e * turn_blocks + c * blocks
                    act.wait_ge(s.mm.sem, s.mm.at((e * CHUNKS + c) * tiles - tiles))
                    for j in range(blocks):
                        act.wait_ge(s.hidden.sem, s.hidden.at(n + (j + 1)))
                        b1 = ffn.hidden_bias[0:rows, e * per + j:e * per + j + 1]
                        to = hT[0:rows, cp, j, :]
                        if gated:
                            act.wait_ge(s.up_read.sem, s.up_read.at(n + (j - 1)))
                            to = gate[0:rows, turn_of(cp, j), :]
                        act.activation(to, bank("hidden", cp, j)[0:rows, 0:CHUNK], func, bias=b1).then_inc(s.act.sem, 1)

                over_chunks(act, chunk)

            over_experts(act, expert)

        @block.vector
        def _(vec):
            vec.wait_ge(ffn.loaded.sem, ffn.loaded.base)

            def expert(e):
                def gates(c, cp):
                    n = e * turn_blocks + c * blocks
                    vec.wait_ge(s.mm.sem, s.mm.at((e * CHUNKS + c) * tiles - tiles))
                    for j in range(blocks):
                        vec.wait_ge(s.hidden.sem, s.hidden.at(n + (j + 1)))
                        vec.wait_ge(s.act.sem, s.act.at(n + (j + 1)))
                        to, g = hT[0:rows, cp, j, :], gate[0:rows, turn_of(cp, j), :]
                        up = bank("up", cp, j)[0:rows, 0:CHUNK]
                        up_bias = ffn.hidden_bias[0:rows, e * per + blocks + j:e * per + blocks + j + 1]
                        vec.scalar_tensor_tensor(to, up, up_bias, g, ALU.add, ALU.mult).then_inc(s.up_read.sem, 1)

                def outputs(c, cp):
                    n = (e * CHUNKS + c) * tiles
                    for i in range(tiles):
                        vec.wait_ge(s.mm.sem, s.mm.at(n + (i + 1)))
                        to = tile(dst, c * tiles + i)
                        got = m.ps[2 * BANKS + i][:, 0:D]
                        vec.tensor_tensor(biased[:, i, :], got, ffn.out_bias[:, e * D:(e + 1) * D],
                                          ALU.add).then_inc(s.out.sem, 1)
                        vec.wait_ge(s.out.sem, s.out.at(n + (i + 1)))
                        vec.tensor_tensor(to, biased[:, i, :], to, ALU.add).then_inc(s.summed.sem, 1)

                with vec.Fori(0, CHUNKS - 1, 2) as c:
                    if gated:
                        gates(c, 0)
                        gates(c + 1, 1)
                    outputs(c, 0)
                    outputs(c + 1, 1)

            over_experts(vec, expert)

        @block.sync
        def _(sp):
            if prefetch:
                prefetch(sp)
    for signal, n in ((s.hidden, experts * turn_blocks), (s.act, experts * turn_blocks),
                      (s.mm, experts * CHUNKS * tiles), (s.out, experts * CHUNKS * tiles)):
        signal.close(n)
    if gated:
        s.up_read.close(experts * turn_blocks)
    s.summed.close(experts * CHUNKS * tiles)


def rows_phase(nc, m, s, ffn, src):
    k = ffn.top
    with (
        nc.sbuf_tensor(f"row_{ffn.name}", [P, RING, D], F32) as row,
        nc.sbuf_tensor(f"place_{ffn.name}", [P, RING, k], U32) as place,
        nc.sbuf_tensor(f"seen_{ffn.name}", [P, TILES * k], U32) as seen,
        nc.Block(no_gpsimd_drain=True) as block,
    ):
        @block.vector
        def _(vec):
            def stage(t, p):
                vec.tensor_copy(place[:, p, :], m.put[:, ds(t * k, k)])
                vec.tensor_scalar(row[:, p, :], tile(src, t), m.mean[:, ds(t, 1)], m.rstd[:, ds(t, 1)],
                                  ALU.subtract, ALU.mult).then_inc(s.x.sem, 1)

            for p in range(RING):
                stage(p, p)
            with vec.Fori(1, TILES // RING) as r:
                for p in range(RING):
                    vec.wait_ge(s.moved[p].sem, s.moved[p].at(r * (16 * k)))
                    stage(r * RING + p, p)

        @block.gpsimd
        def _(pool):
            with pool.Fori(0, TILES // RING) as r:
                for p in range(RING):
                    pool.wait_ge(s.x.sem, s.x.at(r * RING + (p + 1)))
                    t = r * RING + p
                    pool.tensor_copy(seen[:, ds(t * k, k)], m.put[:, ds(t * k, k)]).then_inc(s.seen.sem, 1)
                    for j in range(k):
                        pool.indirect_dma_start(m.rows, bass.IndirectOffsetOnAxis(ap=place[:, p, j:j + 1], axis=0),
                                                row[:, p, :], None).then_inc(s.moved[p].sem, 16)
            pool.wait_ge(s.seen.sem, s.seen.at(TILES))
            for p in range(RING):
                pool.wait_ge(s.moved[p].sem, s.moved[p].at(16 * k * (TILES // RING)))
    s.x.close(TILES)
    s.seen.close(TILES)
    for p in range(RING):
        s.moved[p].close(16 * k * (TILES // RING))


def mixture_phase(nc, m, s, ffn, scale=None, shift=None, prefetch=None):
    n = ffn.places
    gated = ffn.kind == "gate"
    func = {"gelu": ACT.Gelu, "silu": ACT.Silu, "gate": ACT.Silu}[ffn.kind]
    rows = FP + 1 if ffn.biased else FP
    block_rows = ffn.block + (1 if ffn.joined else 0)
    blocks = ffn.width // ffn.block
    wide = 2 * ffn.width if gated else ffn.width
    per_bank = 512 // P
    ahead = 4 if n % 4 == 0 else 2
    hidden_done = s.up_read if gated else s.act
    ones = (1 if ffn.biased else 0) + (1 if ffn.joined else 0)
    PEEL = 4 if ahead == 2 else 8
    copies = 4 if ffn.joined else 2
    W1 = m.w1_all[0:rows, :]
    W2 = m.w2_all[0:block_rows, :]
    with (
        nc.sbuf_tensor(f"slots_{ffn.name}", [P, ahead, D], F32) as slots,
        nc.sbuf_tensor(f"slotsT_{ffn.name}", [FP + 1, 2, FC, P], F32) as slotsT,
        nc.sbuf_tensor(f"w1_{ffn.name}", [FP + 1, copies, ffn.stride], F32) as w1,
        nc.sbuf_tensor(f"hiddenT_{ffn.name}", [P, 2, blocks, P], F32) as hT,
        nc.sbuf_tensor(f"gates_{ffn.name}", [P, 2, blocks if gated else 1, P], F32) as gate,
        nc.sbuf_tensor(f"result_{ffn.name}", [P, ahead, D], F32) as result,
        nc.Block(no_gpsimd_drain=True) as block,
    ):
        def turns(eng, turn):
            for i in range(PEEL):
                turn(i, i % ahead)
            with eng.Fori(PEEL, n - ahead + 1, ahead) as i:
                for p in range(ahead):
                    turn(i + p, p)
            for i in range(n, n + 2):
                turn(i, i % ahead)

        def has(i):
            return i not in (-2, -1, n, n + 1) if isinstance(i, int) else True

        def expert_of(eng, i):
            return eng.value_load(m.ids[0:1, ds(i, 1)], min_val=0, max_val=ffn.experts - 1)

        def hidden_bank(p, j):
            return m.ps[2 + 2 * p + j // per_bank][0:ffn.block, (j % per_bank) * P:(j % per_bank + 1) * P]

        @block.sync
        def _(sp):
            for i in range(ahead):
                sp.dma_start(slots[:, i, :], m.rows[i * P:(i + 1) * P, :]).then_inc(s.fetched[i].sem, 16)
            with sp.Fori(ahead, n - ahead + 1, ahead) as i:
                for p in range(ahead):
                    sp.wait_ge(s.turned.sem, s.turned.at(i + (p - ahead + 1)))
                    sp.dma_start(slots[:, p, :], m.rows[ds((i + p) * P, P), :]).then_inc(s.fetched[p].sem, 16)
            if prefetch:
                prefetch(sp)

        @block.tensor
        def _(pe):
            pe.wait_ge(ffn.loaded.sem, ffn.loaded.base)
            if ones:
                pe.wait_ge(s.cleared.sem, s.cleared.at(ones))

            def turn_slots(i, slot):
                p = slot % 2
                pe.wait_ge(s.fetched[slot].sem, s.fetched[slot].at((i - slot) * (16 // ahead) + 16))
                pe.wait_ge(s.xT.sem, s.xT.at(i - 1))
                for c in range(FC):
                    last = pe.matmul(m.ps[p][0:FP, c * P:(c + 1) * P], slots[:, slot, c * FP:(c + 1) * FP],
                                     m.ident[:, :], start=True, stop=True, is_transpose=True)
                last.then_inc(s.turned.sem, 1)

            def hidden(i, slot):
                p = slot % 2
                pe.wait_ge(s.xT.sem, s.xT.at(i + 1))
                pe.wait_ge(s.copied.sem, s.copied.at(i + 1))
                pe.wait_ge(hidden_done.sem, hidden_done.at(i - 1))
                for half in range(2 if gated else 1):
                    for j in range(blocks):
                        to = hidden_bank(p, j + half * per_bank)
                        first = (half * ffn.up_at + (1 - half) * ffn.gate_at) if gated else 0
                        for c in range(FC):
                            high = rows if c == 0 else FP
                            at = c * wide + first + j * ffn.block
                            last = pe.matmul(to, w1[0:high, slot % copies, at:at + ffn.block], slotsT[0:high, p, c, :],
                                             start=(c == 0), stop=(c == FC - 1))
                last.then_inc(s.hidden.sem, 1)

            def output(i, slot):
                p = slot % 2
                if not ffn.joined:
                    e = expert_of(pe, i)
                pe.wait_ge(hidden_done.sem, hidden_done.at(i + 1))
                pe.wait_ge(s.out.sem, s.out.at(i - 1))
                for j in range(blocks):
                    w2 = w1[0:block_rows, slot, FC * wide:] if ffn.joined else W2[:, ds(e * (blocks * D) + j * D, D)]
                    last = pe.matmul(m.ps[6 + p][:, 0:D], hT[0:block_rows, p, j, :], w2,
                                     start=(j == 0), stop=(j == blocks - 1))
                last.then_inc(s.mm.sem, 1)

            def turn(i, slot):
                if has(i):
                    turn_slots(i, slot)
                if has(i - 1):
                    hidden(i - 1, (slot - 1) % ahead)
                if has(i - 2):
                    output(i - 2, (slot - 2) % ahead)

            turns(pe, turn)

        @block.scalar
        def _(act):
            act.wait_ge(ffn.loaded.sem, ffn.loaded.base)

            def features(i, p):
                act.wait_ge(s.hidden.sem, s.hidden.at(i - 1))
                act.wait_ge(s.turned.sem, s.turned.at(i + 1))
                if scale is None:
                    act.activation(slotsT[0:FP, p, :, :], m.ps[p][0:FP, 0:FC * P].rearrange("f (c k) -> f c k", c=FC),
                                   ACT.Copy).then_inc(s.xT.sem, 1)
                else:
                    for c in range(FC):
                        last = act.activation(slotsT[0:FP, p, c, :], m.ps[p][0:FP, c * P:(c + 1) * P], ACT.Identity,
                                              bias=shift[:, c:c + 1], scale=scale[:, c:c + 1])
                    last.then_inc(s.xT.sem, 1)

            def copy(i, slot):
                e = expert_of(act, i)
                act.activation(w1[0:rows, slot, :], W1[:, ds(e * ffn.stride, ffn.stride)], ACT.Copy).then_inc(s.copied.sem, 1)

            def activate(i, p):
                act.wait_ge(s.hidden.sem, s.hidden.at(i + 1))
                act.wait_ge(s.mm.sem, s.mm.at(i - 1))
                to = gate if gated else hT
                for b in range(0, blocks, per_bank):
                    k = min(per_bank, blocks - b)
                    last = act.activation(to[0:ffn.block, p, b:b + k, :].rearrange("f j k -> f (j k)"),
                                          m.ps[2 + 2 * p + b // per_bank][0:ffn.block, 0:k * P], func)
                last.then_inc(s.act.sem, 1)

            def turn(i, slot):
                p = slot % 2
                if has(i) and ffn.joined:
                    act.wait_ge(s.mm.sem, s.mm.at(i - 3))
                if has(i):
                    features(i, p)
                if has(i) and ffn.joined:
                    copy(i, slot)
                if has(i - 1):
                    activate(i - 1, 1 - p)

            turns(act, turn)

        @block.vector
        def _(vec):
            vec.wait_ge(ffn.loaded.sem, ffn.loaded.base)
            if ffn.biased:
                vec.memset(slotsT[FP:FP + 1, :, 0, :], 1.0).then_inc(s.cleared.sem, 1)
            if ffn.joined:
                vec.memset(hT[ffn.block:ffn.block + 1, :, :, :], 1.0).then_inc(s.cleared.sem, 1)

            def copy(i, p):
                e = expert_of(vec, i)
                vec.wait_ge(s.hidden.sem, s.hidden.at(i - 1))
                vec.tensor_copy(w1[0:rows, p, :], W1[:, ds(e * ffn.stride, ffn.stride)]).then_inc(s.copied.sem, 1)

            def gates(i, p):
                vec.wait_ge(s.act.sem, s.act.at(i + 1))
                vec.tensor_tensor(hT[0:ffn.block, p, :, :].rearrange("f j k -> f (j k)"),
                                  m.ps[3 + 2 * p][0:ffn.block, 0:blocks * P],
                                  gate[0:ffn.block, p, :, :].rearrange("f j k -> f (j k)"), ALU.mult).then_inc(s.up_read.sem, 1)

            def output(i, slot):
                p = slot % 2
                if ffn.biased and not ffn.joined:
                    e = expert_of(vec, i)
                vec.wait_ge(s.mm.sem, s.mm.at(i + 1))
                if not (isinstance(i, int) and i < ahead):
                    vec.wait_ge(s.stored[slot].sem, s.stored[slot].at((i - slot) * (16 // ahead)))
                if ffn.biased and not ffn.joined:
                    vec.tensor_tensor(result[:, slot, :], m.ps[6 + p][:, 0:D], ffn.out_bias[:, ds(e * D, D)],
                                      ALU.add).then_inc(s.out.sem, 1)
                else:
                    vec.tensor_copy(result[:, slot, :], m.ps[6 + p][:, 0:D]).then_inc(s.out.sem, 1)

            def turn(i, slot):
                p = slot % 2
                if has(i) and not ffn.joined:
                    copy(i, p)
                if has(i - 1) and gated:
                    gates(i - 1, 1 - p)
                if has(i - 2):
                    output(i - 2, (slot - 2) % ahead)

            turns(vec, turn)

        @block.gpsimd
        def _(pool):
            with pool.Fori(0, n - ahead + 1, ahead) as i:
                for p in range(ahead):
                    pool.wait_ge(s.out.sem, s.out.at(i + (p + 1)))
                    pool.dma_start(m.results[ds((i + p) * P, P), :], result[:, p, :]).then_inc(s.stored[p].sem, 16)
            for p in range(ahead):
                pool.wait_ge(s.stored[p].sem, s.stored[p].at(16 // ahead * n))
    for signal in (s.turned, s.xT, s.hidden, s.act, s.copied, s.mm, s.out):
        signal.close(n)
    s.cleared.close(ones)
    if gated:
        s.up_read.close(n)
    for p in range(ahead):
        s.fetched[p].close(16 // ahead * n)
        s.stored[p].close(16 // ahead * n)


def combine_phase(nc, m, s, ffn, dst, measure=False):
    k = ffn.top
    turns = TILES // RING
    with (
        nc.sbuf_tensor(f"gathered_{ffn.name}", [P, RING, k, D], F32) as gathered,
        nc.sbuf_tensor(f"from_{ffn.name}", [P, RING, k], U32) as place,
        nc.sbuf_tensor(f"seen_back_{ffn.name}", [P, TILES * k], U32) as seen,
        nc.Block(no_gpsimd_drain=True) as block,
    ):
        @block.vector
        def _(vec):
            def stage(r, p):
                vec.tensor_copy(place[:, p, :], m.get[:, ds((r * RING + p) * k, k)]).then_inc(s.stage.sem, 1)

            def add(r, p):
                vec.wait_ge(s.moved[p].sem, s.moved[p].at((r + 1) * (16 * k)))
                for j in range(k):
                    t = r * RING + p
                    if j > 0:
                        vec.wait_ge(s.summed.sem, s.summed.at(t * k + j))
                    vec.scalar_tensor_tensor(tile(dst, t), gathered[:, p, j, :], m.gates[:, ds(t * k + j, 1)],
                                             tile(dst, t), ALU.mult, ALU.add).then_inc(s.summed.sem, 1)
                if measure:
                    vec.wait_ge(s.summed.sem, s.summed.at((t + 1) * k))
                    vec.bn_stats(tile(m.stats, t, 6), tile(dst, t)).then_inc(s.stats.sem, 1)

            for p in range(RING):
                vec.tensor_copy(place[:, p, :], m.get[:, p * k:(p + 1) * k]).then_inc(s.stage.sem, 1)
            with vec.Fori(0, turns - 1) as r:
                for p in range(RING):
                    add(r, p)
                    vec.wait_ge(s.summed.sem, s.summed.at((r * RING + (p + 1)) * k))
                    stage(r + 1, p)
            for p in range(RING):
                add(turns - 1, p)
            if measure:
                vec.wait_ge(s.stats.sem, s.stats.at(TILES))

        @block.gpsimd
        def _(pool):
            with pool.Fori(0, turns) as r:
                for p in range(RING):
                    pool.wait_ge(s.stage.sem, s.stage.at(r * RING + (p + 1)))
                    t = r * RING + p
                    pool.tensor_copy(seen[:, ds(t * k, k)], m.get[:, ds(t * k, k)]).then_inc(s.seen.sem, 1)
                    for j in range(k):
                        pool.indirect_dma_start(gathered[:, p, j, :], None, m.results[0:ffn.places * P, :],
                                                bass.IndirectOffsetOnAxis(ap=place[:, p, j:j + 1], axis=0),
                                                ).then_inc(s.moved[p].sem, 16)
            pool.wait_ge(s.seen.sem, s.seen.at(TILES))
    s.stage.close(TILES)
    s.summed.close(TILES * k)
    if measure:
        s.stats.close(TILES)
    s.seen.close(TILES)
    for p in range(RING):
        s.moved[p].close(16 * k * turns)


def pick_largest(vec, step, m, most, x, onehot, experts):
    shape = [P, TILES, experts]
    step(vec.tensor_reduce(most, x, AX, ALU.max))
    step(vec.tensor_tensor(onehot, x, most.unsqueeze(2).to_broadcast(shape), ALU.is_equal))
    step(vec.tensor_tensor(onehot, onehot, m.rank[:, 0:experts].unsqueeze(1).to_broadcast(shape), ALU.mult))
    step(vec.tensor_reduce(most, onehot, AX, ALU.max))
    step(vec.tensor_tensor(onehot, onehot, most.unsqueeze(2).to_broadcast(shape), ALU.is_equal))


class Scratch:

    def __init__(self, nc, ctx, ffn):
        def sb(name, *shape, dtype=F32):
            return ctx.enter_context(nc.sbuf_tensor(f"{name}_{ffn.name}", list(shape), dtype))

        cols = TILES * ffn.experts
        self.pick = [sb(f"pick{i}", P, cols) for i in range(max(2, ffn.top))]
        self.other, self.union, self.place = sb("other", P, cols), sb("union", P, cols), sb("place_of", P, cols)
        self.most, self.token = sb("most", P, TILES), sb("token", P, 3, TILES)
        self.group = sb("group", P, 3, TILES * 4)
        self.prefix, self.running = sb("prefix", P, cols), sb("running", P, cols)
        self.over, self.full = sb("over", P, ffn.experts, TILES), sb("full", P, ffn.experts)
        self.end, self.start = sb("end", P, ffn.experts), sb("start", P, ffn.experts)
        self.past, self.id = sb("past", 1, ffn.places, ffn.experts), sb("id", 1, ffn.places)
        self.flat, self.put = sb("flat", P, TILES), sb("put_f", P, TILES * ffn.top)


def view(buf, k):
    return buf[:, 0:TILES * k].rearrange("p (t e) -> p t e", e=k)


def before_tile(vec, step, m, w, counts, experts):
    cols = TILES * experts
    step(vec.tensor_copy(w.prefix[:, :].rearrange("p (e t) -> p t e", t=TILES), counts.rearrange("p (t e) -> p t e", e=experts)))
    step(vec.tensor_tensor_scan(w.running[:, :], m.restart[:, 0:cols], w.prefix[:, :], 0.0, ALU.mult, ALU.add))
    step(vec.tensor_tensor(w.prefix[:, :], w.running[:, :], w.prefix[:, :], ALU.subtract))


def count_union(pe, m, s, w, cols):
    pe.wait_ge(s.union.sem, s.union.at(1))
    pe.matmul(m.ps[4][:, 0:cols], m.triangle[:, :], w.union[:, :], start=True, stop=True)
    pe.matmul(m.ps[5][:, 0:cols], m.ones[:, :], w.union[:, :], start=True, stop=True).then_inc(s.counted.sem, 1)


def give_places(vec, step, m, s, w, ffn):
    experts, k, cols = ffn.experts, ffn.top, TILES * ffn.experts
    wide = [P, TILES, experts]
    if k == 1:
        vec.tensor_copy(w.union[:, :], w.pick[0][:, :]).then_inc(s.union.sem, 1)
    else:
        have = w.pick[0]
        for j in range(1, k):
            last = vec.tensor_tensor(w.union[:, :], have[:, :], w.pick[j][:, :], ALU.add)
            if j == k - 1:
                last.then_inc(s.union.sem, 1)
            else:
                step(last)
            have = w.union
    vec.wait_ge(s.counted.sem, s.counted.at(1))
    before_tile(vec, step, m, w, m.ps[5][:, 0:cols], experts)
    step(vec.tensor_tensor(view(w.place, experts), m.ps[4][:, 0:cols].rearrange("p (t e) -> p t e", e=experts),
                           w.prefix[:, :].rearrange("p (e t) -> p t e", t=TILES), ALU.add))
    count = w.running[:, :].rearrange("p (e t) -> p e t", t=TILES)[:, :, TILES - 1]
    step(vec.tensor_scalar(w.full[:, :], count, 1.0 / P, None, ALU.mult))
    many = [P, experts, TILES]
    step(vec.tensor_tensor(w.over[:, :, :], w.full[:, :].unsqueeze(2).to_broadcast(many),
                           m.index[:, 0:TILES].unsqueeze(1).to_broadcast(many), ALU.is_gt))
    step(vec.tensor_reduce(w.full[:, :], w.over[:, :, :], AX, ALU.add))
    step(vec.tensor_tensor_scan(w.end[:, :], m.ones[:, 0:experts], w.full[:, :], 0.0, ALU.mult, ALU.add))
    step(vec.tensor_tensor(w.start[:, :], w.end[:, :], w.full[:, :], ALU.subtract))
    step(vec.tensor_scalar(w.start[:, :], w.start[:, :], float(P), -1.0, ALU.mult, ALU.add))
    step(vec.tensor_tensor(view(w.place, experts), view(w.place, experts), w.start[:, :].unsqueeze(1).to_broadcast(wide), ALU.add))
    get = w.put[:, :].rearrange("p (t k) -> p t k", k=k)
    for j in range(k):
        step(vec.tensor_tensor(w.other[:, :], w.place[:, :], w.pick[j][:, :], ALU.mult))
        step(vec.tensor_reduce(get[:, :, j], view(w.other, experts), AX, ALU.add))
    step(vec.tensor_copy(m.get[:, 0:TILES * k], w.put[:, :]))
    if ffn.capacity:
        for j in range(k):
            step(vec.tensor_reduce(w.flat[:, :], view(w.pick[j], experts), AX, ALU.add))
            step(vec.tensor_scalar(w.flat[:, :], w.flat[:, :], -1.0, 1.0, ALU.mult, ALU.add))
            step(vec.tensor_scalar(w.most[:, :], m.token_id[:, :], float(ffn.places * P + j * TOKENS), None, ALU.add))
            step(vec.tensor_tensor(w.flat[:, :], w.flat[:, :], w.most[:, :], ALU.mult))
            step(vec.tensor_tensor(get[:, :, j], get[:, :, j], w.flat[:, :], ALU.add))
    step(vec.tensor_copy(m.put[:, 0:TILES * k], w.put[:, :]))
    three = [1, ffn.places, experts]
    step(vec.tensor_tensor(w.past[:, :, :], m.index[0:1, 0:ffn.places].unsqueeze(2).to_broadcast(three),
                           w.end[0:1, :].unsqueeze(1).to_broadcast(three), ALU.is_ge))
    step(vec.tensor_reduce(w.id[:, :], w.past[:, :, :], AX, ALU.add))
    step(vec.tensor_scalar(w.id[:, :], w.id[:, :], float(experts - 1), None, ALU.min))
    step(vec.tensor_copy(m.ids[:, 0:ffn.places], w.id[:, :]))


def route_top2_phase(nc, m, s, ffn):
    experts, cols = ffn.experts, TILES * ffn.experts
    x = view(m.logits, experts)
    with ExitStack() as ctx:
        w = Scratch(nc, ctx, ffn)
        first, second, other = (view(b, experts) for b in (w.pick[0], w.pick[1], w.other))
        v1, v2, inv = w.token[:, 0, :], w.token[:, 1, :], w.token[:, 2, :]
        gates = m.gates[:, 0:TILES * 2].rearrange("p (t k) -> p t k", k=2)
        block = ctx.enter_context(nc.Block(no_gpsimd_drain=True))

        @block.vector
        def _(vec):
            step = Steps(vec, s.vec)
            pick_largest(vec, step, m, w.most[:, :], x, first, experts)
            step(vec.tensor_tensor(other, x, first, ALU.mult))
            step(vec.tensor_reduce(v1, other, AX, ALU.add))
            step(vec.scalar_tensor_tensor(other, first, NEG, x, ALU.mult, ALU.add))
            pick_largest(vec, step, m, w.most[:, :], other, second, experts)
            step(vec.tensor_tensor(other, x, second, ALU.mult))
            step(vec.tensor_reduce(v2, other, AX, ALU.add))
            vec.tensor_tensor(v2, v2, v1, ALU.subtract).then_inc(s.x.sem, 1)
            if ffn.capacity:
                for j in range(2):
                    vec.wait_ge(s.mm.sem, s.mm.at(j + 1))
                    before_tile(vec, step, m, w, m.ps[2 + j][:, 0:cols], experts)
                    step(vec.tensor_tensor(other, m.ps[j][:, 0:cols].rearrange("p (t e) -> p t e", e=experts),
                                           w.prefix[:, :].rearrange("p (e t) -> p t e", t=TILES), ALU.add))
                    step(vec.tensor_scalar(other, other, float(ffn.capacity), None, ALU.is_le))
                    step(vec.tensor_tensor(w.pick[j][:, :], w.pick[j][:, :], w.other[:, :], ALU.mult))
            vec.wait_ge(s.exps.sem, s.exps.at(1))
            step(vec.tensor_scalar(inv, v2, 1.0, None, ALU.add))
            step(vec.reciprocal(inv, inv))
            step(vec.tensor_tensor(v2, v2, inv, ALU.mult))
            for j, gate in enumerate((inv, v2)):
                if ffn.capacity:
                    step(vec.tensor_reduce(w.flat[:, :], view(w.pick[j], experts), AX, ALU.add))
                    step(vec.tensor_tensor(gates[:, :, j], gate, w.flat[:, :], ALU.mult))
                else:
                    step(vec.tensor_copy(gates[:, :, j], gate))
            give_places(vec, step, m, s, w, ffn)
            m.vec_links = step.n

        @block.scalar
        def _(act):
            act.wait_ge(s.x.sem, s.x.at(1))
            act.activation(v2, v2, ACT.Exp).then_inc(s.exps.sem, 1)

        @block.tensor
        def _(pe):
            if ffn.capacity:
                pe.wait_ge(s.x.sem, s.x.at(1))
                for j in range(2):
                    pick = w.pick[j][:, :]
                    pe.matmul(m.ps[j][:, 0:cols], m.triangle[:, :], pick, start=True, stop=True)
                    pe.matmul(m.ps[2 + j][:, 0:cols], m.ones[:, :], pick, start=True, stop=True).then_inc(s.mm.sem, 1)
            count_union(pe, m, s, w, cols)
    s.vec.close(m.vec_links)
    for signal in (s.x, s.exps, s.union, s.counted):
        signal.close(1)
    if ffn.capacity:
        s.mm.close(2)


def route_top1_phase(nc, m, s, ffn):
    experts, cols = ffn.experts, TILES * ffn.experts
    x = view(m.logits, experts)
    with ExitStack() as ctx:
        w = Scratch(nc, ctx, ffn)
        first, most = view(w.pick[0], experts), w.token[:, 0, :]
        block = ctx.enter_context(nc.Block(no_gpsimd_drain=True))

        @block.vector
        def _(vec):
            step = Steps(vec, s.vec)
            step(vec.tensor_reduce(most, x, AX, ALU.max))
            vec.tensor_tensor(x, x, most.unsqueeze(2).to_broadcast([P, TILES, experts]), ALU.subtract).then_inc(s.x.sem, 1)
            vec.wait_ge(s.exps.sem, s.exps.at(1))
            step(vec.tensor_reduce(most, x, AX, ALU.add))
            step(vec.reciprocal(most, most))
            step(vec.tensor_tensor(x, x, most.unsqueeze(2).to_broadcast([P, TILES, experts]), ALU.mult))
            step(vec.tensor_reduce(m.gates[:, 0:TILES], x, AX, ALU.max))
            pick_largest(vec, step, m, w.most[:, :], x, first, experts)
            give_places(vec, step, m, s, w, ffn)
            m.vec_links = step.n

        @block.scalar
        def _(act):
            act.wait_ge(s.x.sem, s.x.at(1))
            act.activation(x, x, ACT.Exp).then_inc(s.exps.sem, 1)

        @block.tensor
        def _(pe):
            count_union(pe, m, s, w, cols)
    s.vec.close(m.vec_links)
    for signal in (s.x, s.exps, s.union, s.counted):
        signal.close(1)


def route_groups_phase(nc, m, s, ffn, groups, top_groups, scaling):
    experts, top, cols = ffn.experts, ffn.top, TILES * ffn.experts
    per = experts // groups
    rows = TILES * groups
    with ExitStack() as ctx:
        w = Scratch(nc, ctx, ffn)
        score, sfc, one, left = m.logits, w.other, w.union, w.place
        total = w.token[:, 0, :]
        gates = m.gates[:, 0:TILES * top].rearrange("p (t k) -> p t k", k=top)
        block = ctx.enter_context(nc.Block(no_gpsimd_drain=True))

        def grouped(buf):
            return buf[:, 0:cols].rearrange("p (t k) -> p t k", k=per)

        def by_group(j):
            return w.group[:, j, :].rearrange("p (t g) -> p t g", g=groups)

        @block.vector
        def _(vec):
            step = Steps(vec, s.vec)
            vec.wait_ge(s.exps.sem, s.exps.at(1))
            step(vec.tensor_tensor(view(sfc, experts), view(score, experts),
                                   m.correction[:, :].unsqueeze(1).to_broadcast([P, TILES, experts]), ALU.add))
            best, second = w.group[:, 0, :], w.group[:, 1, :]
            wide = [P, rows, per]
            step(vec.tensor_reduce(best, grouped(sfc), AX, ALU.max))
            step(vec.tensor_tensor(grouped(one), grouped(sfc), best.unsqueeze(2).to_broadcast(wide), ALU.is_equal))
            step(vec.tensor_tensor(grouped(one), grouped(one), m.rank[:, 0:per].unsqueeze(1).to_broadcast(wide), ALU.mult))
            step(vec.tensor_reduce(second, grouped(one), AX, ALU.max))
            step(vec.tensor_tensor(grouped(one), grouped(one), second.unsqueeze(2).to_broadcast(wide), ALU.is_equal))
            step(vec.scalar_tensor_tensor(left[:, :], one[:, :], NEG, sfc[:, :], ALU.mult, ALU.add))
            step(vec.tensor_reduce(second, grouped(left), AX, ALU.max))
            step(vec.tensor_tensor(best, best, second, ALU.add))
            chosen = w.group[:, 2, :]
            for n in range(top_groups):
                pick_largest(vec, step, m, w.most[:, :], by_group(0), by_group(1), groups)
                if n == 0:
                    step(vec.tensor_copy(chosen, second))
                else:
                    step(vec.tensor_tensor(chosen, chosen, second, ALU.add))
                if n < top_groups - 1:
                    step(vec.scalar_tensor_tensor(best, second, NEG, best, ALU.mult, ALU.add))
            step(vec.tensor_tensor(grouped(sfc), grouped(sfc), chosen.unsqueeze(2).to_broadcast(wide), ALU.mult))
            for n in range(top):
                pick_largest(vec, step, m, w.most[:, :], view(sfc, experts), view(w.pick[n], experts), experts)
                if n < top - 1:
                    step(vec.scalar_tensor_tensor(sfc[:, :], w.pick[n][:, :], NEG, sfc[:, :], ALU.mult, ALU.add))
                step(vec.tensor_tensor(left[:, :], w.pick[n][:, :], score[:, 0:cols], ALU.mult))
                step(vec.tensor_reduce(gates[:, :, n], view(left, experts), AX, ALU.add))
            step(vec.tensor_reduce(total, gates, AX, ALU.add))
            step(vec.tensor_scalar(total, total, 1e-20, None, ALU.add))
            step(vec.reciprocal(total, total))
            step(vec.tensor_tensor(gates, gates, total.unsqueeze(2).to_broadcast([P, TILES, top]), ALU.mult))
            step(vec.tensor_scalar(gates, gates, scaling, None, ALU.mult))
            give_places(vec, step, m, s, w, ffn)
            m.vec_links = step.n

        @block.scalar
        def _(act):
            act.activation(m.logits[:, 0:cols], m.logits[:, 0:cols], ACT.Sigmoid).then_inc(s.exps.sem, 1)

        @block.tensor
        def _(pe):
            count_union(pe, m, s, w, cols)
    s.vec.close(m.vec_links)
    for signal in (s.exps, s.union, s.counted):
        signal.close(1)


class Signals:

    def __init__(self, make):
        def signal(name):
            return Signal(make(name))

        def arrival(name):
            return Signal(make(name), 0)

        self.vec = signal("vec")
        self.soft = signal("soft")
        self.rot = signal("rot")
        self.stats = signal("stats")
        self.var = signal("var")
        self.std = signal("std")
        self.x = signal("x")
        self.kept = signal("kept")
        self.turned = signal("turned")
        self.xT = signal("xT")
        self.route = signal("route")
        self.logit = signal("logit")
        self.stage = signal("stage")
        self.mm = signal("mm")
        self.out = signal("out")
        self.q = signal("q")
        self.k = signal("k")
        self.v = signal("v")
        self.r = signal("r")
        self.key_out = signal("key_out")
        self.projected = signal("projected")
        self.valued = signal("valued")
        self.tripled = signal("tripled")
        self.scores = signal("scores")
        self.scored = signal("scored")
        self.shifted = signal("shifted")
        self.gelu = signal("gelu")
        self.exps = signal("exps")
        self.weight = signal("weight")
        self.weightT = signal("weightT")
        self.inverse = signal("inverse")
        self.weighed = signal("weighed")
        self.context = signal("context")
        self.context_turned = signal("context_turned")
        self.context_out = signal("context_out")
        self.hidden = signal("hidden")
        self.act = signal("act")
        self.up_read = signal("up_read")
        self.summed = signal("summed")
        self.patch = signal("patch")
        self.inverted = signal("inverted")
        self.sums = signal("sums")
        self.mixed = signal("mixed")
        self.seen = signal("seen")
        self.union = signal("union")
        self.counted = signal("counted")
        self.copied = signal("copied")
        self.cleared = signal("cleared")
        self.lead = [self.vec, self.soft, self.rot, self.stats, self.var, self.std, self.x, self.kept, self.turned,
                     self.xT, self.route, self.logit, self.stage, self.mm, self.out, self.q, self.k, self.v, self.r,
                     self.key_out, self.projected, self.tripled, self.scores, self.scored, self.shifted, self.gelu,
                     self.exps, self.weight, self.weightT, self.inverse, self.weighed, self.context,
                     self.context_turned, self.context_out, self.hidden, self.act, self.up_read, self.summed,
                     self.patch, self.mixed, self.valued, self.inverted, self.sums, self.seen, self.union, self.counted, self.copied, self.cleared]
        self.consts = arrival("consts")
        self.image = [arrival(f"image{i}") for i in range(IMAGES * GRID // P)]
        self.patch_store = arrival("patch_store")
        self.patch_load = arrival("patch_load")
        self.attention_w = arrival("attention_w")
        self.expert_w = [arrival(f"expert_w{i}") for i in range(2)]
        self.filled = arrival("filled")
        self.moved = [arrival(f"moved{i}") for i in range(RING)]
        self.fetched = [arrival(f"fetched{i}") for i in range(4)]
        self.stored = [arrival(f"stored{i}") for i in range(4)]
        self.store = arrival("store")


class Memory:

    def __init__(self, nc, ctx):
        def sb(name, *shape):
            return ctx.enter_context(nc.sbuf_tensor(name, list(shape), F32))

        self.loads = []

        def const(name, *shape):
            buf = sb(name, *shape)
            self.loads.append((name, buf))
            return buf

        self.ident, self.triangle, self.ones = const("ident", P, P), const("triangle", P, P), const("ones", P, P)
        self.rank, self.restart = const("rank", P, 16), const("restart", P, 16 * TILES)
        self.index, self.token_id = const("index", P, MOST_PLACES), const("token_id", P, TILES)
        self.head_mask = const("head_mask", FP, HPC)
        self.value_mask = const("value_mask", GROUP * SEQ, GROUP * HEAD)
        self.causal, self.causal_two = const("causal", P, SEQ), const("causal_two", P, SEQ)
        self.cos, self.sin, self.zero_bias = const("cos", FP, SEQ), const("sin", FP, SEQ), const("zero_bias", FP, FC)
        self.W1, self.b1, self.W2, self.b2 = const("W1", P, PATCH), const("b1", P, 1), const("W2", P, PATCH), const("b2", P, 1)
        self.W3, self.b3 = const("W3", CHANNELS, D), const("b3", P, D)
        self.mix, self.decay, self.first = const("mix", FP, 3 * FC), const("decay", FP, FC), const("first", FP, FC)
        self.ln = const("ln", FP, 4 * FC)
        self.qkv0, self.qkv1 = const("qkv0", FP, 3 * FC), const("qkv1", FP, 3 * FC)
        self.out0, self.out1 = const("out0", P, D), const("out1", P, D)
        self.router0, self.router_b0 = const("router0", FP, FC, 4), const("router_b0", P, 4)
        self.router1, self.router2 = const("router1", FP, FC, 8), const("router2", FP, FC, 8)
        self.router3, self.router_b3 = const("router3", FP, FC, 16), const("router_b3", P, 16)
        self.correction = const("correction", P, 16)
        self.h, self.xT = sb("h", P, TILES * D), sb("xT", FP, FC, TOKENS)
        self.xs, self.x_tile = sb("xs", FP, 2, FC, P), sb("x_tile", P, 2, D)
        self.stats, self.mean = sb("stats", P, TILES * 6), sb("mean", P, TILES)
        self.other, self.rstd, self.unmix = sb("other", P, TILES), sb("rstd", P, TILES), sb("unmix", FP, 3 * FC)
        self.logits, self.gates = sb("logits", P, TILES * 16), sb("gates", P, TILES * 4)
        self.put = ctx.enter_context(nc.sbuf_tensor("put", [P, TILES * 4], U32))
        self.get = ctx.enter_context(nc.sbuf_tensor("get", [P, TILES * 4], U32))
        self.ids = ctx.enter_context(nc.sbuf_tensor("ids", [1, MOST_PLACES], I32))
        self.attention_w = [sb(f"attention_w{i}", FP, FC, 6 * D) for i in range(2)]
        self.ps = [ctx.enter_context(nc.psum_tensor(f"bank{i}", [P, 512], F32)) for i in range(8)]


    def grow(self, nc, ctx):
        self.w1_all = ctx.enter_context(nc.sbuf_tensor("expert_w1", [P, 8 * FC * 1024], F32))
        self.w2_all = ctx.enter_context(nc.sbuf_tensor("expert_w2", [P, 8 * 6 * D], F32))
        self.out_bias = ctx.enter_context(nc.sbuf_tensor("out_bias", [P, 8 * D], F32))
        self.hidden_bias = ctx.enter_context(nc.sbuf_tensor("hidden_bias", [P, 6], F32))
        whole = 8 * FC * 1024
        self.z = self.w1_all[:, whole - TILES * D:whole]

    def expert_w1(self, ffn, e):
        n = FC * ffn.columns
        at = ffn.first + e * n
        return self.w1_all[0:P, at:at + n].rearrange("f (c k) -> f c k", c=FC)

    def expert_w2(self, ffn, e):
        n = ffn.width // ffn.block * D
        at = ffn.second + e * n
        return self.w2_all[0:P, at:at + n].rearrange("f (j k) -> f j k", k=D)


class FeedForward:

    def __init__(self, loaded, name, experts, kind, width, top=0, biased=True, block=P, gate_at=0, up_at=0, capacity=None,
                 first=0, second=0, joined=False, out_bias=None, hidden_bias=None):
        self.loaded = loaded
        self.name, self.experts, self.kind, self.width, self.top = name, experts, kind, width, top
        self.biased, self.block, self.gate_at, self.up_at = biased, block, gate_at, up_at
        self.columns = 2 * width if kind == "gate" else width
        self.capacity, self.first, self.second, self.joined = capacity, first, second, joined
        self.stride = FC * self.columns + (D if joined else 0)
        self.out_bias, self.hidden_bias = out_bias, hidden_bias
        self.places = most_places(experts, top)


def start_phase(nc, m, s, ins):
    with nc.Block(no_gpsimd_drain=True) as block:

        @block.vector
        def _(vec):
            for signal in s.lead:
                vec.sem_inc(signal.sem, signal.base)

        @block.sync
        def _(sp):
            for name, buf in m.loads:
                shape = list(buf.shape)
                src = ins[name] if ins[name].shape[0] == shape[0] else ins[name].to_broadcast(shape)
                sp.dma_start(buf[:, :] if len(shape) == 2 else buf[:, :, :], src).then_inc(s.consts.sem, 16)
            sp.wait_ge(s.consts.sem, 16 * len(m.loads))


def tower(nc, ins, out, patch_dram, rows, results):
    with ExitStack() as ctx:
        m = Memory(nc, ctx)
        s = Signals(lambda name: ctx.enter_context(nc.semaphore(name)))
        m.patch_dram, m.rows, m.results = patch_dram, rows, results

        def three(buf, first=0):
            return [buf[:, (first + j) * FC:(first + j + 1) * FC] for j in range(3)]

        def output_w(layer):
            return m.attention_w[layer % 2][:, :, 3 * D:4 * D]

        g1, b1, g2, b2 = (m.ln[:, j * FC:(j + 1) * FC] for j in range(4))

        start_phase(nc, m, s, ins)
        token_phase(nc, m, s, ins)

        feature_phase(nc, m, s, m.h, measured=True)
        rwkv_phase(nc, m, s)
        m.grow(nc, ctx)
        ffn0 = FeedForward(s.expert_w[1], "ffn0", 4, "gelu", 768, top=2, out_bias=m.out_bias[:, 0:4 * D])
        mlp = FeedForward(s.expert_w[0], "mlp", 1, "gelu", 768, first=4 * FC * 768, second=4 * 6 * D,
                          out_bias=m.out_bias[:, 4 * D:5 * D], hidden_bias=m.hidden_bias[:, :])
        ffn1 = FeedForward(s.expert_w[0], "ffn1", 8, "silu", 768, top=1, out_bias=m.out_bias[:, :])
        ffn2 = FeedForward(s.expert_w[1], "ffn2", 8, "gate", 512, top=2, biased=False, gate_at=512, capacity=int(1.2 * TOKENS / 8))
        ffn3 = FeedForward(s.expert_w[0], "ffn3", 16, "gate", 96, top=4, block=96, up_at=96, joined=True)
        shared = FeedForward(s.expert_w[0], "shared", 2, "gate", 96, block=96, up_at=96, first=ffn3.experts * ffn3.stride,
                             out_bias=m.out_bias[:, 0:2 * D], hidden_bias=m.hidden_bias[0:FP, 0:4])

        project_phase(nc, m, s, output_w(1), m.h)
        feature_phase(nc, m, s, m.h, keep=m.z, measured=True)
        feature_phase(nc, m, s, m.z, scale=g1, shift=b1)
        attention_phase(nc, m, s, 0, "plain", three(m.qkv0), lambda sp: load_resident(sp, m, s, ins, mlp))
        project_phase(nc, m, s, output_w(0), m.z, m.out0[:, :], measure=False)
        feature_phase(nc, m, s, m.z, norm=False)

        def load_next(sp):
            load_attention(sp, m, s, ins, 1)
            load_resident(sp, m, s, ins, ffn0)

        expert_phase(nc, m, s, mlp, m.z, 0, 1, load_next)
        feature_phase(nc, m, s, m.z, scale=g2, shift=b2, router=(m.router0, m.router_b0[:, :], 4),
                      keep_turned=False)
        route_top2_phase(nc, m, s, ffn0)
        rows_phase(nc, m, s, ffn0, m.z)
        mixture_phase(nc, m, s, ffn0, scale=g2, shift=b2)
        combine_phase(nc, m, s, ffn0, m.z)
        add_phase(nc, m, s, m.h, m.z)

        feature_phase(nc, m, s, m.h, measured=True)
        attention_phase(nc, m, s, 1, "causal", three(m.qkv1), lambda sp: load_resident(sp, m, s, ins, ffn1))
        project_phase(nc, m, s, output_w(1), m.h, m.out1[:, :])
        feature_phase(nc, m, s, m.h, router=(m.router1, None, 8), keep_turned=False, measured=True)
        route_top1_phase(nc, m, s, ffn1)
        rows_phase(nc, m, s, ffn1, m.h)
        mixture_phase(nc, m, s, ffn1, prefetch=lambda sp: load_attention(sp, m, s, ins, 2))
        combine_phase(nc, m, s, ffn1, m.h, measure=True)

        feature_phase(nc, m, s, m.h, measured=True)
        attention_phase(nc, m, s, 2, "erf", prefetch=lambda sp: load_resident(sp, m, s, ins, ffn2))
        project_phase(nc, m, s, output_w(2), m.h)
        feature_phase(nc, m, s, m.h, router=(m.router2, None, 8), keep_turned=False, measured=True)
        route_top2_phase(nc, m, s, ffn2)
        rows_phase(nc, m, s, ffn2, m.h)
        mixture_phase(nc, m, s, ffn2, prefetch=lambda sp: load_attention(sp, m, s, ins, 3))
        combine_phase(nc, m, s, ffn2, m.h, measure=True)

        def load_last(sp):
            load_resident(sp, m, s, ins, ffn3)
            load_resident(sp, m, s, ins, shared)

        feature_phase(nc, m, s, m.h, measured=True)
        attention_phase(nc, m, s, 3, "causal", prefetch=load_last)
        project_phase(nc, m, s, output_w(3), m.h)
        feature_phase(nc, m, s, m.h, router=(m.router3, m.router_b3[:, :], 16), measured=True)
        route_groups_phase(nc, m, s, ffn3, groups=4, top_groups=2, scaling=2.5)
        rows_phase(nc, m, s, ffn3, m.h)
        mixture_phase(nc, m, s, ffn3)
        expert_phase(nc, m, s, shared, m.h, 0, 2)
        combine_phase(nc, m, s, ffn3, m.h)

        store_phase(nc, s, m.h, out)


def constants():
    f = np.float32
    p = np.arange(P)
    query = np.where(p < SEQ, p, np.where((p >= SECOND) & (p < SECOND + SEQ), p - SECOND, SEQ))
    seen = np.arange(SEQ)[None, :] <= query[:, None]
    half = HEAD // 2
    freq = (f(1.0) / f(10000.0) ** (np.arange(half, dtype=f) / f(half))).astype(f)
    angle = freq[:, None] * np.arange(SEQ, dtype=f)[None, :]
    pair = (np.arange(FP) % HEAD) // 2
    sign = np.where(np.arange(FP) % 2 == 0, f(-1), f(1))
    return {
        "ident": np.eye(P, dtype=f),
        "triangle": (p[:, None] <= p[None, :]).astype(f),
        "ones": np.ones((P, P), f),
        "rank": np.tile(np.arange(16, 0, -1).astype(f), (P, 1)),
        "restart": np.tile((np.arange(16 * TILES) % TILES != 0).astype(f), (P, 1)),
        "index": np.tile(np.arange(MOST_PLACES, dtype=f), (P, 1)),
        "token_id": (np.arange(TILES)[None, :] * P + p[:, None]).astype(f),
        "head_mask": (np.arange(FP)[:, None] // HEAD == np.arange(HPC)[None, :]).astype(f),
        "value_mask": (np.arange(GROUP * SEQ)[:, None] // SEQ == np.arange(GROUP * HEAD)[None, :] // HEAD).astype(f),
        "causal": np.where(seen, f(0), f(NEG)).astype(f),
        "causal_two": np.where(seen, f(2), f(0)).astype(f),
        "cos": np.cos(angle)[pair].astype(f),
        "sin": (np.sin(angle)[pair] * sign[:, None]).astype(f),
        "zero_bias": np.zeros((FP, FC), f),
    }


def layout(a):
    def feature(w):
        return w.reshape(FC, FP, -1).transpose(1, 0, 2)

    def column(*v):
        return np.concatenate([x.reshape(FC, FP).T for x in v], axis=1)

    def hidden(v, rows):
        return v.reshape(-1, rows).T

    def first(w, bias=None):
        w = w.reshape(w.shape[0], FC, FP, -1).transpose(0, 2, 1, 3)
        if bias is None:
            return w
        return np.concatenate([w, np.stack([bias, np.zeros_like(bias)], axis=1)[:, None]], axis=1)

    def second(w, rows):
        return w.reshape(w.shape[0], -1, rows, D).transpose(0, 2, 1, 3)

    def side(*w):
        return feature(np.concatenate(w, axis=1))

    turned = np.arange(D) ^ 1
    wide = D // 2
    t = constants()
    x = a["x"].reshape(IMAGES, CHANNELS, GRID, PATCH * SIDE).transpose(1, 0, 2, 3)
    t.update({
        "x": x.reshape(CHANNELS, IMAGES * GRID, PATCH * SIDE),
        "W1": a["L0_tok_W1"], "b1": a["L0_tok_b1"].reshape(1, 1), "W2": a["L0_tok_W2"],
        "b2": a["L0_tok_b2"].reshape(1, 1), "W3": a["L0_tok_W3"].T, "b3": a["L0_tok_b3"].reshape(1, D),
        "mix": column(a["L0_attn_mix_k"], a["L0_attn_mix_v"], a["L0_attn_mix_r"]),
        "decay": column(a["L0_attn_time_decay"]), "first": column(a["L0_attn_time_first"]),
        "rwkv": side(*(a[f"L0_attn_W{k}"].T for k in "kvro")),
        "ln": column(a["L0_ffn_ln1_g"], a["L0_ffn_ln1_b"], a["L0_ffn_ln2_g"], a["L0_ffn_ln2_b"]),
        "attention0": side(a["L0_ffn_in_w"].T, a["L0_ffn_out_w"].T),
        "attention1": side(a["L1_attn_W_attn"], a["L1_attn_W_proj"]),
        "attention2": side(*(a[f"L2_attn_W{k}"].T for k in ("q", "k", "v", "proj")),
                           a["L2_attn_Wq"].T[:, turned], a["L2_attn_Wk"].T[:, turned]),
        "attention3": side(*(a[f"L3_attn_w{k}"].T for k in "qkvo")),
        "qkv0": column(*a["L0_ffn_in_b"].reshape(3, D)), "qkv1": column(*a["L1_attn_b_attn"].reshape(3, D)),
        "out0": a["L0_ffn_out_b"].reshape(1, D), "out1": a["L1_attn_b_proj"].reshape(1, D),
        "router0": feature(a["L0_ffn_gate_w"].T), "router_b0": a["L0_ffn_gate_b"].reshape(1, -1),
        "router1": feature(a["L1_ffn_Wg"]), "router2": feature(a["L2_ffn_Wg"]),
        "router3": feature(a["L3_ffn_router_w"].T), "router_b3": a["L3_ffn_router_b"].reshape(1, -1),
        "correction": a["L3_ffn_corr_bias"].reshape(1, -1),
        "mlp_w1": first(a["L0_ffn_mlp_w1"][None]), "mlp_w2": second(a["L0_ffn_mlp_w2"][None], P),
        "mlp_b1": hidden(a["L0_ffn_mlp_b1"][None], P), "mlp_b2": a["L0_ffn_mlp_b2"].reshape(1, D),
        "ffn0_w1": first(a["L0_ffn_exp_w1"], a["L0_ffn_exp_b1"]), "ffn0_w2": second(a["L0_ffn_exp_w2"], P),
        "ffn0_b2": a["L0_ffn_exp_b2"].reshape(1, -1),
        "ffn1_w1": first(a["L1_ffn_W1"], a["L1_ffn_b1"]), "ffn1_w2": second(a["L1_ffn_W2"], P),
        "ffn1_b2": a["L1_ffn_b2"].reshape(1, -1),
        "ffn2_w1": first(a["L2_ffn_W1"]), "ffn2_w2": second(a["L2_ffn_W2"], P),
        "ffn3_w": np.concatenate([
            first(np.concatenate([a["L3_ffn_gWg"], a["L3_ffn_gWu"]], axis=2),
                  np.concatenate([a["L3_ffn_gbg"], a["L3_ffn_gbu"]], axis=1)).reshape(16, FP + 1, -1),
            np.concatenate([a["L3_ffn_gWd"], a["L3_ffn_gbd"][:, None, :]], axis=1)], axis=2),
        "shared_w1": first(np.stack([np.concatenate([a["L3_ffn_sWg"][:, h], a["L3_ffn_sWu"][:, h]], axis=1)
                                     for h in (slice(0, wide), slice(wide, D))])),
        "shared_w2": second(a["L3_ffn_sWd"].reshape(2, wide, D), wide),
        "shared_b1": np.stack([a["L3_ffn_sbg"][:wide], a["L3_ffn_sbu"][:wide],
                               a["L3_ffn_sbg"][wide:], a["L3_ffn_sbu"][wide:]], axis=1),
        "shared_b2": np.concatenate([a["L3_ffn_sbd"], np.zeros(D, np.float32)]).reshape(1, -1),
    })
    return {k: np.ascontiguousarray(v) for k, v in t.items()}


def kernel(**inputs):
    import concourse.bacc as bacc
    from concourse.bass_utils import run_bass_kernel_spmd

    arrays = layout({k: np.asarray(v) for k, v in inputs.items()})
    nc = bacc.Bacc("TRN2", target_bir_lowering=False, num_devices=1)
    ins = {k: nc.dram_tensor(f"in_{k}", v.shape, F32, kind="ExternalInput").ap() for k, v in arrays.items()}
    out = nc.dram_tensor("tokens", (TOKENS, D), F32, kind="ExternalOutput").ap()
    patch_dram = nc.dram_tensor("patch_sums", (CHANNELS, TOKENS), F32, kind="Internal").ap()
    rows = nc.dram_tensor("placed_rows", (MOST_PLACES * P, D), F32, kind="Internal").ap()
    results = nc.dram_tensor("results", (MOST_PLACES * P, D), F32, kind="Internal").ap()
    tower(nc, ins, out, patch_dram, rows, results)
    result = run_bass_kernel_spmd(nc, [{f"in_{k}": v for k, v in arrays.items()}], core_ids=[0])
    return result.results[0]["tokens"].reshape(IMAGES, SEQ, D)
```
